# Optimizing a Trainium2 kernel written in Bass

```python
import numpy as np
import jax
import jax.numpy as jnp

def _softmax(x, axis=-1):
    return jax.nn.softmax(x, axis=axis)

def _gelu(x):
    return jax.nn.gelu(x, approximate=True)

def _silu(x):
    return jax.nn.silu(x)

def _sigmoid(x):
    return jax.nn.sigmoid(x)

def _layernorm(x, axis=-1, eps=1e-05):
    m = jnp.mean(x, axis=axis, keepdims=True)
    v = jnp.var(x, axis=axis, keepdims=True)
    return (x - m) / jnp.sqrt(v + eps)

def _scatter_add(tgt, idx, src, axis=0):
    return tgt.at[idx].add(src)

def _segment_sum(src, seg, n):
    return jax.ops.segment_sum(src, seg, n)
kernel_name = 'mk_decoder_postln_d2_seqx_r4_ae1ded'

def setup_inputs(seed: int=0):
    np.random.seed(seed)
    _w = jnp.asarray

    def _rec_inputs():
        import jax
        import jax.numpy as jnp
        _rk = jax.random.key(seed)
        x = -0.0002928 + 1 * jax.random.normal(jax.random.fold_in(_rk, 1), (16, 112, 256), jnp.float32)
        _lenS = 112 - jax.random.randint(jax.random.fold_in(_rk, 7), (16,), 0, max(1, 112 // 4) + 1, jnp.int32)
        _lenS2 = 375 - jax.random.randint(jax.random.fold_in(_rk, 8), (16,), 0, max(1, 375 // 4) + 1, jnp.int32)
        _ctx_1024P = jax.random.normal(jax.random.fold_in(_rk, 11), (16, 16, 256), jnp.float32)
        _ctx_1024c = jax.random.dirichlet(jax.random.fold_in(_rk, 511), 0.3 * jnp.ones((16,), jnp.float32), (16, 375))
        _ctx_1024t = jnp.einsum('bsk,bkd->bsd', _ctx_1024c, _ctx_1024P)
        _ctx_1024t = _ctx_1024t * jax.lax.rsqrt(jnp.mean(jnp.square(_ctx_1024t)) + 1e-12) * 0.953939
        ctx_1024 = -1.39393e-06 + 0.999914 * (_ctx_1024t + 0.3 * jax.random.normal(jax.random.fold_in(_rk, 611), (16, 375, 256), jnp.float32))
        _validS = jnp.arange(112)[None, :] < _lenS[:, None]
        _validS2 = jnp.arange(375)[None, :] < _lenS2[:, None]
        _causal = jnp.tril(jnp.ones((112, 112), dtype=bool))
        mask_1x1xSxS2_if1 = jnp.where(jnp.ones((1, 1, 112, 375), dtype=bool), 1, 0).astype(jnp.int32)
        mask_BxS2_bf1 = jnp.ones((16, 375), dtype=bool)
        return (x, ctx_1024, mask_1x1xSxS2_if1, mask_BxS2_bf1)
    x, ctx_1024, mask_1x1xSxS2_if1, mask_BxS2_bf1 = _rec_inputs()

    def _L0_attn_setup():
        import jax, jax.numpy as jnp
        import numpy as np
        import math
        D = 256
        W = 128

        def _decay_mask(L, gamma, dtype):
            i = jnp.arange(L)
            diff = i[:, None] - i[None, :]
            same_block = i[:, None] // W == i[None, :] // W
            safe_exp = jnp.maximum(diff, 0).astype(dtype)
            in_block = jnp.where(diff >= 0, gamma ** safe_exp, jnp.zeros((), dtype))
            return jnp.where(same_block, in_block, jnp.ones((), dtype))
        key = jax.random.key(seed)
        ks = jax.random.split(key, 5)
        B, L = (2, 1024)
        x = jax.random.normal(ks[0], (B, L, D), dtype=jnp.float32)
        Wqkv = jax.random.normal(ks[1], (D, 3 * D), dtype=jnp.float32) * 0.02
        bqkv = jnp.zeros((3 * D,), dtype=jnp.float32)
        Wproj = jax.random.normal(ks[2], (D, D), dtype=jnp.float32) * 0.02
        bproj = jnp.zeros((D,), dtype=jnp.float32)
        gamma = jnp.float32(0.9)
        return {'x': x, 'Wqkv': Wqkv, 'bqkv': bqkv, 'Wproj': Wproj, 'bproj': bproj, 'gamma': gamma}
    _L0_attn_all = _L0_attn_setup()
    _L0_attn_in = {k: v for k, v in _L0_attn_all.items() if k in ('Wqkv', 'bqkv', 'Wproj', 'bproj', 'gamma')}
    del _L0_attn_all

    def _L0_xattn_setup():
        import jax, jax.numpy as jnp
        import numpy as np
        D_MODEL = 256
        HEADS = 16
        D_K = D_MODEL // HEADS
        B, S = (2, 512)
        NEG = -1000000000.0
        key = jax.random.key(seed)
        ks = jax.random.split(key, 7)
        Query = jax.random.normal(ks[0], (B, S, D_MODEL), dtype=jnp.float32)
        Key = jax.random.normal(ks[1], (B, S, D_MODEL), dtype=jnp.float32)
        Value = jax.random.normal(ks[2], (B, S, D_MODEL), dtype=jnp.float32)
        mask = jnp.ones((1, 1, S, S), dtype=jnp.int32)
        sc = 1.0 / np.sqrt(D_MODEL)
        W_q = jax.random.normal(ks[3], (D_MODEL, D_MODEL), dtype=jnp.float32) * sc
        W_k = jax.random.normal(ks[4], (D_MODEL, D_MODEL), dtype=jnp.float32) * sc
        W_v = jax.random.normal(ks[5], (D_MODEL, D_MODEL), dtype=jnp.float32) * sc
        W_o = jax.random.normal(ks[6], (D_MODEL, D_MODEL), dtype=jnp.float32) * sc
        return {'Query': Query, 'Key': Key, 'Value': Value, 'mask': mask, 'W_q': W_q, 'W_k': W_k, 'W_v': W_v, 'W_o': W_o}
    _L0_xattn_all = _L0_xattn_setup()
    _L0_xattn_in = {k: v for k, v in _L0_xattn_all.items() if k in ('W_q', 'W_k', 'W_v', 'W_o')}
    del _L0_xattn_all

    def _L0_ffn_setup():
        import jax, jax.numpy as jnp
        import numpy as np
        B, S, DIM = (4, 512, 256)
        E, K, HID = (8, 2, 1024)
        key = jax.random.key(seed)
        ks = jax.random.split(key, 8)
        init = lambda k, sh: jax.random.normal(k, sh, jnp.float32) * 0.02
        return {'x': jax.random.normal(ks[0], (B, S, DIM), jnp.float32), 'gate_w': init(ks[1], (DIM, E)), 'gate_b': jnp.zeros((E,), jnp.float32), 'w1': init(ks[2], (E, DIM, HID)), 'b1': jnp.zeros((E, HID), jnp.float32), 'w2': init(ks[3], (E, HID, DIM)), 'b2': jnp.zeros((E, DIM), jnp.float32), 'ws1': init(ks[4], (DIM, HID)), 'bs1': jnp.zeros((HID,), jnp.float32), 'ws2': init(ks[5], (HID, DIM)), 'bs2': jnp.zeros((DIM,), jnp.float32)}
    _L0_ffn_all = _L0_ffn_setup()
    _L0_ffn_in = {k: v for k, v in _L0_ffn_all.items() if k in ('gate_w', 'gate_b', 'w1', 'b1', 'w2', 'b2', 'ws1', 'bs1', 'ws2', 'bs2')}
    del _L0_ffn_all

    def _L1_attn_setup():
        import jax, jax.numpy as jnp
        import numpy as np
        B, S, E = (2, 512, 256)
        H = 16
        D = E // H
        key = jax.random.key(seed)
        ks = jax.random.split(key, 11)
        s = 1.0 / np.sqrt(E)
        return {'x': jax.random.normal(ks[0], (B, S, E), dtype=jnp.float32), 'Wq': jax.random.uniform(ks[1], (E, E), jnp.float32, -s, s), 'bq': jnp.zeros((E,), jnp.float32), 'Wk': jax.random.uniform(ks[2], (E, E), jnp.float32, -s, s), 'bk': jnp.zeros((E,), jnp.float32), 'Wv': jax.random.uniform(ks[3], (E, E), jnp.float32, -s, s), 'bv': jnp.zeros((E,), jnp.float32), 'Wo': jax.random.uniform(ks[4], (E, E), jnp.float32, -s, s), 'bo': jnp.zeros((E,), jnp.float32), 'J_attn': jax.random.normal(ks[5], (H, D, D), jnp.float32) * 0.02, 'lambda_attn': jnp.float32(0.5)}
    _L1_attn_all = _L1_attn_setup()
    _L1_attn_in = {k: v for k, v in _L1_attn_all.items() if k in ('Wq', 'bq', 'Wk', 'bk', 'Wv', 'bv', 'Wo', 'bo', 'J_attn', 'lambda_attn')}
    del _L1_attn_all

    def _L1_xattn_setup():
        import jax, jax.numpy as jnp
        import numpy as np
        B, TQ, TK, D, H = (4, 256, 512, 256, 16)
        HD = D // H

        def _to_heads(t):
            Bx, T, _ = t.shape
            return t.reshape(Bx, T, H, HD).transpose(0, 2, 1, 3)
        key = jax.random.key(seed)
        ks = jax.random.split(key, 8)

        def xavier(k, shape):
            fan_in, fan_out = (shape[0], shape[1])
            limit = float(np.sqrt(6.0 / (fan_in + fan_out)))
            return jax.random.uniform(k, shape, jnp.float32, -limit, limit)
        return {'x': jax.random.normal(ks[0], (B, TQ, D), jnp.float32), 'memory': jax.random.normal(ks[1], (B, TK, D), jnp.float32), 'memory_padding_mask': jnp.ones((B, TK), dtype=bool), 'W_q': xavier(ks[2], (D, D)), 'b_q': jnp.zeros((D,), jnp.float32), 'W_kv': xavier(ks[3], (D, 2 * D)), 'b_kv': jnp.zeros((2 * D,), jnp.float32), 'W_o': xavier(ks[4], (D, D)), 'b_o': jnp.zeros((D,), jnp.float32)}
    _L1_xattn_all = _L1_xattn_setup()
    _L1_xattn_in = {k: v for k, v in _L1_xattn_all.items() if k in ('W_q', 'b_q', 'W_kv', 'b_kv', 'W_o', 'b_o')}
    del _L1_xattn_all

    def _L1_ffn_setup():
        import jax, jax.numpy as jnp
        import numpy as np
        B, S, D = (2, 512, 256)
        H, E, P, K = (8, 8, 128, 2)
        SCALE = 1.0 / np.sqrt(P)

        def _get_sel_gate(x, w, route_scale):
            logits = jnp.einsum('bsd,ed->bse', x, w).astype(jnp.float32)
            raw = logits.reshape(x.shape[0], x.shape[1], H, E)
            probs = jax.nn.sigmoid(raw)
            vals, idx = jax.lax.top_k(probs, K)
            vals = vals / jnp.clip(vals.sum(-1, keepdims=True), 1e-09)
            vals = vals * route_scale
            gate = (jax.nn.one_hot(idx, E, dtype=vals.dtype) * vals[..., None]).sum(-2)
            return gate
        key = jax.random.key(seed)
        ks = jax.random.split(key, 8)
        std = 1.0 / np.sqrt(D)
        return {'x': jax.random.normal(ks[0], (B, S, D), jnp.float32), 'q_w': jax.random.normal(ks[1], (H * P, D), jnp.float32) * std, 'k_w': jax.random.normal(ks[2], (H * P, D), jnp.float32) * std, 'v_w': jax.random.normal(ks[3], (H * E, D, P), jnp.float32) * std, 'o_w': jax.random.normal(ks[4], (H * E, P, D), jnp.float32) * (1.0 / np.sqrt(H * P)), 'sel_v_w': jax.random.normal(ks[5], (H * E, D), jnp.float32) * std, 'sel_o_w': jax.random.normal(ks[6], (H * E, D), jnp.float32) * std, 'route_scale': jnp.ones((1,), jnp.float32)}
    _L1_ffn_all = _L1_ffn_setup()
    _L1_ffn_in = {k: v for k, v in _L1_ffn_all.items() if k in ('q_w', 'k_w', 'v_w', 'o_w', 'sel_v_w', 'sel_o_w', 'route_scale')}
    del _L1_ffn_all
    return {'x': x, 'ctx_1024': ctx_1024, 'mask_1x1xSxS2_if1': mask_1x1xSxS2_if1, 'mask_BxS2_bf1': mask_BxS2_bf1, 'L0_attn_Wqkv': _L0_attn_in['Wqkv'], 'L0_attn_bqkv': _L0_attn_in['bqkv'], 'L0_attn_Wproj': _L0_attn_in['Wproj'], 'L0_attn_bproj': _L0_attn_in['bproj'], 'L0_attn_gamma': _L0_attn_in['gamma'], 'L0_xattn_W_q': _L0_xattn_in['W_q'], 'L0_xattn_W_k': _L0_xattn_in['W_k'], 'L0_xattn_W_v': _L0_xattn_in['W_v'], 'L0_xattn_W_o': _L0_xattn_in['W_o'], 'L0_ffn_gate_w': _L0_ffn_in['gate_w'], 'L0_ffn_gate_b': _L0_ffn_in['gate_b'], 'L0_ffn_w1': _L0_ffn_in['w1'], 'L0_ffn_b1': _L0_ffn_in['b1'], 'L0_ffn_w2': _L0_ffn_in['w2'], 'L0_ffn_b2': _L0_ffn_in['b2'], 'L0_ffn_ws1': _L0_ffn_in['ws1'], 'L0_ffn_bs1': _L0_ffn_in['bs1'], 'L0_ffn_ws2': _L0_ffn_in['ws2'], 'L0_ffn_bs2': _L0_ffn_in['bs2'], 'L1_attn_Wq': _L1_attn_in['Wq'], 'L1_attn_bq': _L1_attn_in['bq'], 'L1_attn_Wk': _L1_attn_in['Wk'], 'L1_attn_bk': _L1_attn_in['bk'], 'L1_attn_Wv': _L1_attn_in['Wv'], 'L1_attn_bv': _L1_attn_in['bv'], 'L1_attn_Wo': _L1_attn_in['Wo'], 'L1_attn_bo': _L1_attn_in['bo'], 'L1_attn_J_attn': _L1_attn_in['J_attn'], 'L1_attn_lambda_attn': _L1_attn_in['lambda_attn'], 'L1_xattn_W_q': _L1_xattn_in['W_q'], 'L1_xattn_b_q': _L1_xattn_in['b_q'], 'L1_xattn_W_kv': _L1_xattn_in['W_kv'], 'L1_xattn_b_kv': _L1_xattn_in['b_kv'], 'L1_xattn_W_o': _L1_xattn_in['W_o'], 'L1_xattn_b_o': _L1_xattn_in['b_o'], 'L1_ffn_q_w': _L1_ffn_in['q_w'], 'L1_ffn_k_w': _L1_ffn_in['k_w'], 'L1_ffn_v_w': _L1_ffn_in['v_w'], 'L1_ffn_o_w': _L1_ffn_in['o_w'], 'L1_ffn_sel_v_w': _L1_ffn_in['sel_v_w'], 'L1_ffn_sel_o_w': _L1_ffn_in['sel_o_w'], 'L1_ffn_route_scale': _L1_ffn_in['route_scale']}

def reference(x, ctx_1024, mask_1x1xSxS2_if1, mask_BxS2_bf1, L0_attn_Wqkv, L0_attn_bqkv, L0_attn_Wproj, L0_attn_bproj, L0_attn_gamma, L0_xattn_W_q, L0_xattn_W_k, L0_xattn_W_v, L0_xattn_W_o, L0_ffn_gate_w, L0_ffn_gate_b, L0_ffn_w1, L0_ffn_b1, L0_ffn_w2, L0_ffn_b2, L0_ffn_ws1, L0_ffn_bs1, L0_ffn_ws2, L0_ffn_bs2, L1_attn_Wq, L1_attn_bq, L1_attn_Wk, L1_attn_bk, L1_attn_Wv, L1_attn_bv, L1_attn_Wo, L1_attn_bo, L1_attn_J_attn, L1_attn_lambda_attn, L1_xattn_W_q, L1_xattn_b_q, L1_xattn_W_kv, L1_xattn_b_kv, L1_xattn_W_o, L1_xattn_b_o, L1_ffn_q_w, L1_ffn_k_w, L1_ffn_v_w, L1_ffn_o_w, L1_ffn_sel_v_w, L1_ffn_sel_o_w, L1_ffn_route_scale):
    import jax
    import jax.numpy as jnp

    def _L0_attn_ref(x, Wqkv, bqkv, Wproj, bproj, gamma):
        import jax, jax.numpy as jnp
        import numpy as np
        import math
        D = 256
        W = 128

        def _decay_mask(L, gamma, dtype):
            i = jnp.arange(L)
            diff = i[:, None] - i[None, :]
            same_block = i[:, None] // W == i[None, :] // W
            safe_exp = jnp.maximum(diff, 0).astype(dtype)
            in_block = jnp.where(diff >= 0, gamma ** safe_exp, jnp.zeros((), dtype))
            return jnp.where(same_block, in_block, jnp.ones((), dtype))
        B, L, d = x.shape
        qkv = x @ Wqkv + bqkv
        q, k, v = jnp.split(qkv, 3, axis=-1)
        attn = jnp.einsum('bqd,bkd->bqk', q, k) / math.sqrt(d)
        mask = _decay_mask(L, gamma, x.dtype)
        attn = attn * mask[None, :, :]
        attn = jax.nn.softmax(attn, axis=-1)
        out = jnp.einsum('bqk,bkd->bqd', attn, v)
        return out @ Wproj + bproj

    def _L0_xattn_ref(Query, Key, Value, mask, W_q, W_k, W_v, W_o):
        import jax, jax.numpy as jnp
        import numpy as np
        D_MODEL = 256
        HEADS = 16
        D_K = D_MODEL // HEADS
        B, S = (2, 512)
        NEG = -1000000000.0

        def split_heads(x):
            b, s, _ = x.shape
            return x.reshape(b, s, HEADS, D_K).transpose(0, 2, 1, 3)
        Q = split_heads(Query @ W_q.T)
        K = split_heads(Key @ W_k.T)
        V = split_heads(Value @ W_v.T)
        scores = jnp.einsum('bhqd,bhkd->bhqk', Q, K) / jnp.sqrt(jnp.asarray(D_K, dtype=Q.dtype))
        scores = jnp.where(mask == 0, jnp.asarray(NEG, dtype=scores.dtype), scores)
        attn = jax.nn.softmax(scores, axis=-1)
        X = jnp.einsum('bhqk,bhkd->bhqd', attn, V)
        X = X.transpose(0, 2, 1, 3).reshape(X.shape[0], -1, HEADS * D_K)
        return X @ W_o.T

    def _L0_ffn_ref(x, gate_w, gate_b, w1, b1, w2, b2, ws1, bs1, ws2, bs2):
        import jax, jax.numpy as jnp
        import numpy as np
        B, S, DIM = (4, 512, 256)
        E, K, HID = (8, 2, 1024)
        orig_shape = x.shape
        xf = x.reshape(-1, DIM)
        logits = xf @ gate_w + gate_b
        top_w, top_i = jax.lax.top_k(logits, K)
        gw = jax.nn.softmax(top_w, axis=-1).astype(xf.dtype)
        combine = (gw[:, :, None] * jax.nn.one_hot(top_i, E, dtype=xf.dtype)).sum(axis=1)
        out = jnp.zeros_like(xf)
        for e in range(E):
            h = jax.nn.gelu(xf @ w1[e] + b1[e], approximate=False)
            out = out + combine[:, e:e + 1] * (h @ w2[e] + b2[e])
        shared = jax.nn.gelu(xf @ ws1 + bs1, approximate=False) @ ws2 + bs2
        return (out + shared).reshape(orig_shape)

    def _L1_attn_ref(x, Wq, bq, Wk, bk, Wv, bv, Wo, bo, J_attn, lambda_attn):
        import jax, jax.numpy as jnp
        import numpy as np
        B, S, E = (2, 512, 256)
        H = 16
        D = E // H
        b, s, _ = x.shape
        scale = jnp.sqrt(jnp.float32(D))

        def split_heads(y):
            return y.reshape(b, s, H, D).transpose(0, 2, 1, 3)
        Q = split_heads(x @ Wq.T + bq)
        K = split_heads(x @ Wk.T + bk)
        V = split_heads(x @ Wv.T + bv)
        attn_scores = jnp.einsum('bhid,bhjd->bhij', Q, K) / scale
        Qn = jnp.tanh(Q)
        Kn = jnp.tanh(K)
        QJ = jnp.einsum('bhid,hde->bhie', Qn, J_attn)
        delta = jnp.einsum('bhie,bhje->bhij', QJ, Kn)
        attn_scores = attn_scores + lambda_attn * delta
        attn_probs = jax.nn.softmax(attn_scores, axis=-1)
        out = jnp.einsum('bhij,bhjd->bhid', attn_probs, V)
        out = out.transpose(0, 2, 1, 3).reshape(b, s, E)
        return out @ Wo.T + bo

    def _L1_xattn_ref(x, memory, memory_padding_mask, W_q, b_q, W_kv, b_kv, W_o, b_o):
        import jax, jax.numpy as jnp
        import numpy as np
        B, TQ, TK, D, H = (4, 256, 512, 256, 16)
        HD = D // H

        def _to_heads(t):
            Bx, T, _ = t.shape
            return t.reshape(Bx, T, H, HD).transpose(0, 2, 1, 3)
        q = x @ W_q + b_q
        kv = memory @ W_kv + b_kv
        k, v = (kv[..., :D], kv[..., D:])
        q = _to_heads(q)
        k = _to_heads(k)
        v = _to_heads(v)
        scores = jnp.einsum('bhqd,bhkd->bhqk', q, k) * (1.0 / np.sqrt(HD))
        pad = ~memory_padding_mask
        scores = jnp.where(pad[:, None, None, :], -jnp.inf, scores)
        A = jax.nn.softmax(scores, axis=-1)
        ctx = jnp.einsum('bhqk,bhkd->bhqd', A, v)
        y = ctx.transpose(0, 2, 1, 3).reshape(x.shape[0], x.shape[1], D)
        return y @ W_o + b_o

    def _L1_ffn_ref(x, q_w, k_w, v_w, o_w, sel_v_w, sel_o_w, route_scale):
        import jax, jax.numpy as jnp
        import numpy as np
        B, S, D = (2, 512, 256)
        H, E, P, K = (8, 8, 128, 2)
        SCALE = 1.0 / np.sqrt(P)

        def _get_sel_gate(x, w, route_scale):
            logits = jnp.einsum('bsd,ed->bse', x, w).astype(jnp.float32)
            raw = logits.reshape(x.shape[0], x.shape[1], H, E)
            probs = jax.nn.sigmoid(raw)
            vals, idx = jax.lax.top_k(probs, K)
            vals = vals / jnp.clip(vals.sum(-1, keepdims=True), 1e-09)
            vals = vals * route_scale
            gate = (jax.nn.one_hot(idx, E, dtype=vals.dtype) * vals[..., None]).sum(-2)
            return gate
        rs = route_scale[0]
        gate_v = _get_sel_gate(x, sel_v_w, rs)
        gate_o = _get_sel_gate(x, sel_o_w, rs)
        q = jnp.einsum('bsd,hpd->bhsp', x, q_w.reshape(H, P, D))
        k = jnp.einsum('bsd,hpd->bhsp', x, k_w.reshape(H, P, D))
        xv = jnp.einsum('bsd,hedp->bshep', x, v_w.reshape(H, E, D, P))
        v = jnp.einsum('bshep,bshe->bhsp', xv, gate_v)
        att = jax.nn.softmax(jnp.einsum('bhqp,bhkp->bhqk', q, k) * SCALE, axis=-1)
        ctx = jnp.einsum('bhqk,bhkp->bqhp', att, v)
        weighted = ctx[:, :, :, None, :] * gate_o[..., None]
        out = jnp.einsum('bshep,hepd->bsd', weighted, o_w.reshape(H, E, P, D))
        return out
    x = _layernorm(x + _L0_attn_ref(x, L0_attn_Wqkv, L0_attn_bqkv, L0_attn_Wproj, L0_attn_bproj, L0_attn_gamma), axis=-1)
    x = _layernorm(x + _L0_xattn_ref(x, ctx_1024, ctx_1024, mask_1x1xSxS2_if1, L0_xattn_W_q, L0_xattn_W_k, L0_xattn_W_v, L0_xattn_W_o), axis=-1)
    x = _layernorm(x + _L0_ffn_ref(x, L0_ffn_gate_w, L0_ffn_gate_b, L0_ffn_w1, L0_ffn_b1, L0_ffn_w2, L0_ffn_b2, L0_ffn_ws1, L0_ffn_bs1, L0_ffn_ws2, L0_ffn_bs2), axis=-1)
    x = _layernorm(x + _L1_attn_ref(x, L1_attn_Wq, L1_attn_bq, L1_attn_Wk, L1_attn_bk, L1_attn_Wv, L1_attn_bv, L1_attn_Wo, L1_attn_bo, L1_attn_J_attn, L1_attn_lambda_attn), axis=-1)
    x = _layernorm(x + _L1_xattn_ref(x, ctx_1024, mask_BxS2_bf1, L1_xattn_W_q, L1_xattn_b_q, L1_xattn_W_kv, L1_xattn_b_kv, L1_xattn_W_o, L1_xattn_b_o), axis=-1)
    x = _layernorm(x + _L1_ffn_ref(x, L1_ffn_q_w, L1_ffn_k_w, L1_ffn_v_w, L1_ffn_o_w, L1_ffn_sel_v_w, L1_ffn_sel_o_w, L1_ffn_route_scale), axis=-1)
    return x

_drawn_inputs = setup_inputs


def setup_inputs(seed=0):
    import zlib

    import numpy as np

    out = dict(_drawn_inputs(seed))
    spreads = {'L0_attn_bqkv': (0.0, 0.1),
     'L0_attn_bproj': (0.0, 0.1),
     'L0_ffn_gate_b': (0.0, 0.1),
     'L0_ffn_b1': (0.0, 0.1),
     'L0_ffn_b2': (0.0, 0.1),
     'L0_ffn_bs1': (0.0, 0.1),
     'L0_ffn_bs2': (0.0, 0.1),
     'L1_attn_bq': (0.0, 0.8),
     'L1_attn_bk': (0.0, 0.8),
     'L1_attn_bv': (0.0, 0.1),
     'L1_attn_bo': (0.0, 0.1),
     'L1_xattn_b_q': (0.0, 0.309),
     'L1_xattn_b_kv': (0.0, 0.1),
     'L1_xattn_b_o': (0.0, 0.1)}
    factors = {'L0_attn_Wqkv': 2.892, 'L1_attn_Wq': 2.848, 'L1_attn_Wk': 2.813, 'L1_attn_J_attn': 8.0}
    for name, (base, spread) in spreads.items():
        noise = np.random.default_rng([zlib.crc32(name.encode()), seed]).standard_normal(out[name].shape)
        drawn = base * np.exp(spread * noise) if base else spread * noise
        out[name] = jnp.asarray(drawn.astype(out[name].dtype))
    for name, factor in factors.items():
        out[name] = (out[name] * factor).astype(out[name].dtype)
    return out
```

```python
from contextlib import ExitStack

import concourse.bass as bass
from concourse import mybir

F32 = mybir.dt.float32
F32R = mybir.dt.float32r
U8 = mybir.dt.uint8
I32 = mybir.dt.int32
ALU = mybir.AluOpType
ACT = mybir.ActivationFunctionType
AX = mybir.AxisListType

B, T, D = 16, 112, 256
TOK = B * T
P = 128
DC = D // P
S2 = 375
KT, KP = 3, 125
CB = 4
NC = B // CB
CT = CB * T
H, HD = 16, 16
EPS = 1e-5
NEG = 4.0e9
ds = bass.ds


class Stage:

    def __init__(self, nc, name):
        self.nc, self.name, self.stack, self.sems = nc, name, ExitStack(), []

    def __enter__(self):
        self.stack.__enter__()
        return self

    def __exit__(self, *error):
        self.stack.__exit__(*error)
        if self.sems:
            self.nc.clear_and_free_semaphores(self.sems)
            self.nc.all_engine_barrier()

    def sb(self, name, shape, dt=F32):
        return self.stack.enter_context(self.nc.sbuf_tensor(f"{self.name}_{name}", shape, dt))

    def dram(self, name, shape, dt=F32):
        return self.nc.dram_tensor(f"{self.name}_{name}", shape, dt).ap()

    def banks(self, name, n):
        return self.stack.enter_context(self.nc.psum_tensor(f"{self.name}_{name}", [P, n, 512], F32))

    def sem(self, name):
        self.sems.append(self.nc.alloc_semaphore(f"{self.name}_{name}"))
        return self.sems[-1]

    def block(self):
        return self.stack.enter_context(self.nc.Block())


class Chain:

    def __init__(self, engine, sem, base=0):
        self.engine, self.sem, self.base, self.n = engine, sem, base, 0

    def link(self, instruction, passed=None):
        self.n += 1
        instruction.then_inc(self.sem, 1)
        if passed is None:
            self.engine.wait_ge(self.sem, self.base + self.n)
        else:
            wait_apart(self.engine, passed, (self.sem, self.base + self.n))


def wait(engine, sem, count):
    if not isinstance(count, int) or count > 0:
        engine.wait_ge(sem, count)


def wait_apart(engine, passed, *waits):
    for sem, count in waits:
        wait(engine, sem, count)
    if not all(isinstance(count, int) for sem, count in waits):
        engine.sem_inc(passed, 1)


def split_product(nc, out, w, x, first=True, last=True):
    nc.tensor.matmul(out, w[0], x[0], start=first, stop=False)
    nc.tensor.matmul(out, w[0], x[1], start=False, stop=False)
    return nc.tensor.matmul(out, w[1], x[0], start=False, stop=last)


def rows(ap, n):
    return ap.rearrange("(a n) -> a n", a=1).broadcast_to([n, ap.shape[0]])


def column(ap, m):
    return ap[m * P:(m + 1) * P].rearrange("(p a) -> p a", a=1)



def stage_load(nc, x_in, x, xt, ident):
    with Stage(nc, "load") as s:
        ps = s.banks("ps", 4)
        loaded, ident_zero, ident_ready = s.sem("loaded"), s.sem("ident_zero"), s.sem("ident_ready")
        transposed, xt_ready = s.sem("transposed"), s.sem("xt_ready")
        block = s.block()

        @block.sync
        def _(sp):
            sp.dma_start(x[:], x_in.rearrange("b t d -> t b d")).then_inc(loaded, 16)

        @block.gpsimd
        def _(pool):
            pool.memset(ident[:], 0.0).then_inc(ident_zero, 1)
            pool.wait_ge(ident_zero, 1)
            pool.affine_select(out=ident[:], in_=ident[:], compare_op=ALU.not_equal, fill=1.0, base=0,
                               pattern=[[-1, P]], channel_multiplier=1).then_inc(ident_ready, 1)

        @block.tensor
        def _(pe):
            pe.wait_ge(loaded, 16)
            pe.wait_ge(ident_ready, 1)
            for c in range(NC):
                for d in range(DC):
                    n = c * DC + d
                    if n >= 4:
                        pe.wait_ge(xt_ready, n - 3)
                    for j in range(CB):
                        last = nc.tensor.transpose(ps[:, n % 4, j * T:(j + 1) * T],
                                                   x[:, c * CB + j, d * P:(d + 1) * P], ident[0:T, 0:T])
                    last.then_inc(transposed, 1)

        @block.scalar
        def _(act):
            for n in range(NC * DC):
                c, d = n // DC, n % DC
                act.wait_ge(transposed, n + 1)
                nc.scalar.copy(xt[:, d, c * CT:(c + 1) * CT], ps[:, n % 4, 0:CT]).then_inc(xt_ready, 1)


def stage_decay_attention(nc, x, xt, ident, Wqkv, bqkv, Wproj, bproj, gamma):
    with Stage(nc, "decay") as s:
        w = s.sb("w", [P, DC, 3 * D])
        wp = s.sb("wp", [P, DC, D])
        qk_bias = s.sb("qk_bias", [P, 4])
        v_bias = s.sb("v_bias", [T, D])
        y_bias = s.sb("y_bias", [T, D])
        gam = s.sb("gam", [T, 1])
        power = s.sb("power", [T, T])
        mask = s.sb("mask", [T, T])
        half = s.sb("half", [T, CB])
        xs = s.sb("xs", [P, DC, CT])
        qk = s.sb("qk", [P, 4, CT])
        v = s.sb("v", [T, CB, D])
        sc = s.sb("sc", [T, CB, T])
        mx = s.sb("mx", [T, CB])
        e = s.sb("e", [T, CB, T])
        rs = s.sb("rs", [T, CB])
        ri = s.sb("ri", [T, CB])
        pr = s.sb("pr", [T, CB, T])
        pt = s.sb("pt", [T, CB, T])
        o = s.sb("o", [P, DC, CT])
        y = s.sb("y", [T, CB, D])
        st = s.sb("st", [T, CB, 6])
        mv = s.sb("mv", [T, CB, 2])
        var = s.sb("var", [T, CB])
        rstd = s.sb("rstd", [T, CB])
        xn = s.sb("xn", [T, CB, D])
        ps = s.banks("ps", 8)
        w_loaded, act_passed, dve_passed = s.sem("w_loaded"), s.sem("act_passed"), s.sem("dve_passed")
        gam_loaded, mask_ready, pool_chain = s.sem("gam_loaded"), s.sem("mask_ready"), s.sem("pool_chain")
        half_ready = s.sem("half_ready")
        xs_ready, qk_done, v_done, qk_ready = (s.sem(n) for n in ("xs_ready", "qk_done", "v_done", "qk_ready"))
        chain = s.sem("chain")
        s_done, shifted, exped, normed = s.sem("s_done"), s.sem("shifted"), s.sem("exped"), s.sem("normed")
        t_done, pt_ready, o_done, o_ready = (s.sem(n) for n in ("t_done", "pt_ready", "o_done", "o_ready"))
        y_done, var_ready, rstd_ready, xn_ready = (s.sem(n) for n in ("y_done", "var_ready", "rstd_ready", "xn_ready"))
        xt_done, xt_ready, x_stored = s.sem("xt_done"), s.sem("xt_ready"), s.sem("x_stored")
        block = s.block()
        CHAIN = 12

        @block.sync
        def _(sp):
            sp.dma_start(w[:], Wqkv.rearrange("(c p) n -> p c n", p=P)).then_inc(w_loaded, 16)
            sp.dma_start(wp[:], Wproj.rearrange("(c p) n -> p c n", p=P)).then_inc(w_loaded, 16)
            for m in range(4):
                sp.dma_start(qk_bias[:, m:m + 1], column(bqkv, m)).then_inc(w_loaded, 16)
            sp.dma_start(v_bias[:], rows(bqkv[2 * D:3 * D], T)).then_inc(w_loaded, 16)
            sp.dma_start(y_bias[:], rows(bproj, T)).then_inc(w_loaded, 16)
            sp.dma_start(gam[:], rows(gamma, T)).then_inc(gam_loaded, 16)

        @block.gpsimd
        def _(pool):
            c = Chain(pool, pool_chain)
            pool.memset(half[:], -0.5).then_inc(half_ready, 1)
            c.link(pool.iota(power[:], pattern=[[-1, T]], base=0, channel_multiplier=1,
                             allow_small_or_imprecise_dtypes=True))
            c.link(pool.tensor_scalar_max(power[:], power[:], 0.0))
            pool.wait_ge(gam_loaded, 16)
            c.link(pool.tensor_tensor(mask[:], gam[:].broadcast_to([T, T]), power[:], ALU.pow))
            pool.affine_select(out=mask[:], in_=mask[:], compare_op=ALU.is_ge, fill=0.0, base=0,
                               pattern=[[-1, T]], channel_multiplier=1).then_inc(mask_ready, 1)
            with pool.Fori(0, NC) as c:
                pool.wait_ge(var_ready, c + 1)
                pool.tensor_tensor(rstd[:], var[:], half[:], ALU.pow).then_inc(rstd_ready, 1)
                pool.wait_ge(xn_ready, c + 1)
                pool.tensor_copy(x[:, ds(c * CB, CB), :], xn[:]).then_inc(x_stored, 1)

        @block.tensor
        def _(pe):
            pe.wait_ge(w_loaded, 128)
            with pe.Fori(0, NC) as c:
                pe.wait_ge(xs_ready, c + 1)
                for m in range(4):
                    for k in range(DC):
                        last = nc.tensor.matmul(ps[:, m, 0:CT], w[:, k, m * P:(m + 1) * P], xs[:, k, :],
                                                start=k == 0, stop=k == DC - 1)
                    last.then_inc(qk_done, 1)
                for j in range(CB):
                    for k in range(DC):
                        last = nc.tensor.matmul(ps[0:T, 4 + j // 2, (j % 2) * D:(j % 2 + 1) * D],
                                                xs[:, k, j * T:(j + 1) * T], w[:, k, 2 * D:3 * D],
                                                start=k == 0, stop=k == DC - 1)
                last.then_inc(v_done, 1)
                pe.wait_ge(qk_ready, 4 * c + 4)
                for j in range(CB):
                    for k in range(DC):
                        last = nc.tensor.matmul(ps[0:T, 6, j * T:(j + 1) * T], qk[:, k, j * T:(j + 1) * T],
                                                qk[:, 2 + k, j * T:(j + 1) * T], start=k == 0, stop=k == DC - 1)
                last.then_inc(s_done, 1)
                pe.wait_ge(normed, c + 1)
                for j in range(CB):
                    last = nc.tensor.transpose(ps[0:T, 7, j * T:(j + 1) * T], pr[:, j, :], ident[0:T, 0:T])
                last.then_inc(t_done, 1)
                pe.wait_ge(pt_ready, c + 1)
                for d in range(DC):
                    for j in range(CB):
                        last = nc.tensor.matmul(ps[:, d, j * T:(j + 1) * T], v[:, j, d * P:(d + 1) * P],
                                                pt[:, j, :], start=True, stop=True)
                    last.then_inc(o_done, 1)
                pe.wait_ge(o_ready, DC * c + DC)
                for j in range(CB):
                    for k in range(DC):
                        last = nc.tensor.matmul(ps[0:T, 2 + j // 2, (j % 2) * D:(j % 2 + 1) * D],
                                                o[:, k, j * T:(j + 1) * T], wp[:, k, :],
                                                start=k == 0, stop=k == DC - 1)
                last.then_inc(y_done, 1)
                pe.wait_ge(xn_ready, c + 1)
                for d in range(DC):
                    for j in range(CB):
                        last = nc.tensor.transpose(ps[:, 4 + d, j * T:(j + 1) * T],
                                                   xn[:, j, d * P:(d + 1) * P], ident[0:T, 0:T])
                    last.then_inc(xt_done, 1)

        @block.scalar
        def _(act):
            act.wait_ge(w_loaded, 128)
            with act.Fori(0, NC) as c:
                nc.scalar.copy(xs[:], xt[:, :, ds(c * CT, CT)]).then_inc(xs_ready, 1)
                for m in range(4):
                    act.wait_ge(qk_done, 4 * c + m + 1)
                    nc.scalar.activation(qk[:, m, :], ps[:, m, 0:CT], ACT.Identity,
                                         bias=qk_bias[:, m:m + 1]).then_inc(qk_ready, 1)
                act.wait_ge(shifted, c + 1)
                nc.scalar.activation(e[:], sc[:], ACT.Exp, scale=1.0 / 16.0).then_inc(exped, 1)
                act.wait_ge(t_done, c + 1)
                nc.scalar.copy(pt[:].rearrange("p a b -> p (a b)"), ps[0:T, 7, 0:CT]).then_inc(pt_ready, 1)
                for d in range(DC):
                    act.wait_ge(o_done, DC * c + d + 1)
                    nc.scalar.copy(o[:, d, :], ps[:, d, 0:CT]).then_inc(o_ready, 1)
                for d in range(DC):
                    wait_apart(act, act_passed, (xt_done, DC * c + d + 1))
                    nc.scalar.copy(xt[:, d, ds(c * CT, CT)], ps[:, 4 + d, 0:CT]).then_inc(xt_ready, 1)

        @block.vector
        def _(dve):
            dve.wait_ge(w_loaded, 128)
            dve.wait_ge(mask_ready, 1)
            dve.wait_ge(half_ready, 1)
            with dve.Fori(0, NC) as c:
                ch = Chain(dve, chain, c * CHAIN)
                dve.wait_ge(v_done, c + 1)
                for j in range(CB):
                    ch.link(nc.vector.tensor_add(v[:, j, :], ps[0:T, 4 + j // 2, (j % 2) * D:(j % 2 + 1) * D], v_bias[:]))
                dve.wait_ge(s_done, c + 1)
                ch.link(nc.vector.tensor_tensor(sc[:], ps[0:T, 6, 0:CT].rearrange("p (a b) -> p a b", a=CB),
                                                mask[:].unsqueeze(1).broadcast_to([T, CB, T]), ALU.mult))
                ch.link(nc.vector.reduce_max(mx[:], sc[:], axis=AX.X))
                nc.vector.tensor_tensor(sc[:], sc[:], mx[:].unsqueeze(2).broadcast_to([T, CB, T]),
                                        ALU.subtract).then_inc(shifted, 1)
                dve.wait_ge(exped, c + 1)
                ch.link(nc.vector.reduce_sum(rs[:], e[:], axis=AX.X))
                ch.link(nc.vector.reciprocal(ri[:], rs[:]))
                nc.vector.tensor_tensor(pr[:], e[:], ri[:].unsqueeze(2).broadcast_to([T, CB, T]),
                                        ALU.mult).then_inc(normed, 1)
                ch.link(nc.vector.tensor_tensor(y[:], x[:, ds(c * CB, CB), :],
                                                y_bias[:].unsqueeze(1).broadcast_to([T, CB, D]), ALU.add))
                dve.wait_ge(y_done, c + 1)
                ch.link(nc.vector.tensor_add(y[:].rearrange("p (a b) d -> p a (b d)", a=2), ps[0:T, 2:4, :],
                                             y[:].rearrange("p (a b) d -> p a (b d)", a=2)))
                for j in range(CB):
                    last = nc.vector.bn_stats(st[:, j, :], y[:, j, :])
                ch.link(last, dve_passed)
                for j in range(CB):
                    last = nc.vector.bn_aggr(mv[:, j, :], st[:, j, :])
                ch.link(last)
                nc.vector.tensor_scalar_add(var[:], mv[:, :, 1], EPS).then_inc(var_ready, 1)
                dve.wait_ge(rstd_ready, c + 1)
                for j in range(CB):
                    last = nc.vector.tensor_scalar(xn[:, j, :], y[:, j, :], mv[:, j, 0:1], rstd[:, j:j + 1],
                                                   ALU.subtract, ALU.mult)
                last.then_inc(xn_ready, 1)
                dve.wait_ge(x_stored, c + 1)
                assert ch.n == CHAIN, ch.n


def stage_cross_attention(nc, name, x, xt, ident, ctx, weights, transposed, biases, mask, mask_by_batch):
    with Stage(nc, name) as s:
        QW, KW, VW, OW = range(4)
        wraw = s.sb("wraw", [P, 4, DC, D])
        wt = [s.sb(f"w{n}", [P, DC, D]) for n in range(4)]
        w = [wt[n] if transposed[n] else wraw[:, n] for n in range(4)]
        qk_bias = s.sb("qk_bias", [P, 2, DC])
        v_bias = s.sb("v_bias", [P, D])
        o_bias = s.sb("o_bias", [T, D])
        half = s.sb("half", [T, 1])
        cx_raw = [s.sb(f"cx_raw{i}", [KP, KT, D]) for i in range(2)]
        cx = s.sb("cx", [P, DC, S2])
        PAIR = 2 * HD
        KEYS = S2 + S2 % 2
        ks = s.sb("ks", [P, 2 * DC, S2], F32R)
        qs = s.sb("qs", [P, 2 * DC, T], F32R)
        k_dram = [s.dram(f"k_dram{b}", [2 * D, S2]) for b in range(2)]
        q_dram = [s.dram(f"q_dram{b}", [2 * D, T]) for b in range(2)]
        kk = [s.sb(f"k{b}", [3 * PAIR, H // 2, KEYS], F32R) for b in range(2)]
        q = [s.sb(f"q{b}", [3 * PAIR, H // 2, 2, T], F32R) for b in range(2)]
        vv = [s.sb(f"v{b}", [KP, KT, H, 32]) for b in range(2)]
        mask_raw = [s.sb(f"mask_raw{i}", [T, S2], U8 if mask_by_batch else I32) for i in range(2)]
        masked = [s.sb(f"masked{i}", [T, S2]) for i in range(2)]
        NB = 8
        sc = s.sb("sc", [T, NB, S2])
        mn = [s.sb(f"mn{b}", [T, H]) for b in range(2)]
        pr = s.sb("pr", [T, NB, S2])
        rs = [s.sb(f"rs{b}", [T, H]) for b in range(2)]
        pt = s.sb("pt", [KP, NB, KT * T])
        osb = s.sb("osb", [P, 4 * T])
        ri = s.sb("ri", [T, H])
        otok = s.sb("otok", [T, H, HD])
        o = s.sb("o", [P, DC, T])
        y = s.sb("y", [T, D])
        st = s.sb("st", [T, 6])
        mv = s.sb("mv", [T, 2])
        var = s.sb("var", [T, 1])
        rstd = s.sb("rstd", [T, 1])
        xn = s.sb("xn", [T, D])
        ps = s.banks("ps", 8)
        FRONT, SCORES, TURNED, OUT, TAIL = 0, 2, 4, 6, 7

        dve_passed, sp_passed, pool_passed = s.sem("dve_passed"), s.sem("sp_passed"), s.sem("pool_passed")
        const_loaded, w_turned, w_ready = (s.sem(n) for n in ("const_loaded", "w_turned", "w_ready"))
        pool_chain, const_ready, mask_ready, v_zero = (s.sem(n) for n in ("pool_chain", "const_ready", "mask_ready", "v_zero"))
        mask_loaded = [s.sem(f"mask_loaded{i}") for i in range(2)]
        ctx_loaded = [s.sem(f"ctx_loaded{i}") for i in range(2)]
        f_done, f_act, f_dve, stack_zero = (s.sem(n) for n in ("f_done", "f_act", "f_dve", "stack_zero"))
        q_stored, k_stored = s.sem("q_stored"), s.sem("k_stored")
        q_stacked, k_stacked = s.sem("q_stacked"), s.sem("k_stacked")
        x_stored = s.sem("x_stored")
        s_done, s_max, exped, t_done = (s.sem(n) for n in ("s_done", "s_max", "exped", "t_done"))
        pt_act, pt_dve, pv_done = (s.sem(n) for n in ("pt_act", "pt_dve", "pv_done"))
        o_read, t1_done, otok_ready, t2_done = (s.sem(n) for n in ("o_read", "t1_done", "otok_ready", "t2_done"))
        o_ready, y_done, var_ready, rstd_ready = (s.sem(n) for n in ("o_ready", "y_done", "var_ready", "rstd_ready"))
        xn_ready, xt_done, xt_ready, chain = (s.sem(n) for n in ("xn_ready", "xt_done", "xt_ready", "chain"))
        CHAIN = 5
        UNITS, ACT_UNITS, DVE_UNITS = 6, 5, 4
        TL, EL, VL = 3, 3, 5
        Q_PARTS, K_PARTS = 6, 3
        block = s.block()

        def over_batches(engine, batch):
            batch(0, 0, True, False)
            with engine.Fori(0, (B - 2) // 2) as i:
                batch(i * 2 + 1, 1, False, False)
                batch(i * 2 + 2, 0, False, False)
            batch(B - 1, 1, False, True)

        def wait_front_read(engine, b, u):
            if u < 0:
                b, u = b - 1, u + UNITS
            if isinstance(b, int) and b < 0:
                return
            if u < 2:
                engine.wait_ge(f_act, b * ACT_UNITS + u + 1)
            else:
                engine.wait_ge(f_dve, b * DVE_UNITS + u - 1)

        def wait_turned_read(engine, b, h):
            if h < 0:
                b, h = b - 1, h + H
            if isinstance(b, int) and b < 0:
                return
            if h % 4 == 3:
                engine.wait_ge(pt_act, b * 4 + h // 4 + 1)
            else:
                engine.wait_ge(pt_dve, b * 12 + h // 4 * 3 + h % 4 + 1)

        @block.sync
        def _(sp):
            for n in range(4):
                sp.dma_start(wraw[:, n], weights[n].rearrange("(c p) n -> p c n", p=P)).then_inc(const_loaded, 16)
            if biases:
                for n in range(2):
                    for m in range(DC):
                        sp.dma_start(qk_bias[:, n, m:m + 1], column(biases[n], m)).then_inc(const_loaded, 16)
                sp.dma_start(v_bias[:], rows(biases[2], P)).then_inc(const_loaded, 16)
                sp.dma_start(o_bias[:], rows(biases[3], T)).then_inc(const_loaded, 16)
            if not mask_by_batch:
                sp.dma_start(mask_raw[0][:], mask).then_inc(mask_loaded[0], 16)

            def load(b, parity):
                wait_apart(sp, sp_passed, (f_done, b * UNITS - 2 * UNITS + DC))
                sp.dma_start(cx_raw[parity][:], ctx[ds(b, 1)].rearrange("a (k p) d -> p (a k) d", p=KP))\
                  .then_inc(ctx_loaded[parity], 16)
                if mask_by_batch:
                    wait_apart(sp, sp_passed, (mask_ready, b - 1))
                    sp.dma_start(mask_raw[parity][:], mask[ds(b, 1)].broadcast_to([T, S2]))\
                      .then_inc(mask_loaded[parity], 16)

            def stack(b, parity):
                wait_apart(sp, sp_passed, (f_dve, b * DVE_UNITS + 1))
                wait_apart(sp, sp_passed, (q_stacked, (b - 1) * Q_PARTS * 16))
                sp.dma_start(q_dram[parity][:].rearrange("(c p) t -> p c t", p=P), qs[:].bitcast(F32))\
                    .then_inc(q_stored, 16)
                wait_apart(sp, sp_passed, (f_dve, b * DVE_UNITS + 3))
                wait_apart(sp, sp_passed, (k_stacked, (b - 1) * K_PARTS * 16))
                sp.dma_start(k_dram[parity][:].rearrange("(c p) s -> p c s", p=P), ks[:].bitcast(F32))\
                    .then_inc(k_stored, 16)
                wait_apart(sp, sp_passed, (q_stored, (b + 1) * 16))
                wait_apart(sp, sp_passed, (s_done, (b - 1) * H))
                if isinstance(b, int) and b < 2:
                    sp.wait_ge(stack_zero, 1)
                for part, source in enumerate((0, 0, D)):
                    for i in range(2):
                        r = part * PAIR + i * HD
                        sp.dma_start(q[parity][r:r + HD, :, i, :].bitcast(F32),
                                     q_dram[parity][source:source + D, :]
                                     .rearrange("(j i d) t -> i d j t", i=2, d=HD)[i]).then_inc(q_stacked, 16)
                wait_apart(sp, sp_passed, (k_stored, (b + 1) * 16))
                for part, source in enumerate((0, D, 0)):
                    sp.dma_start(kk[parity][part * PAIR:(part + 1) * PAIR, :, 0:S2].bitcast(F32),
                                 k_dram[parity][source:source + D, :].rearrange("(j r) s -> r j s", r=PAIR))\
                        .then_inc(k_stacked, 16)

            load(0, 0)
            load(1, 1)
            stack(0, 0)
            load(2, 0)
            with sp.Fori(0, (B - 4) // 2) as i:
                stack(i * 2 + 1, 1)
                load(i * 2 + 3, 1)
                stack(i * 2 + 2, 0)
                load(i * 2 + 4, 0)
            stack(B - 3, 1)
            load(B - 1, 1)
            stack(B - 2, 0)
            stack(B - 1, 1)

        @block.gpsimd
        def _(pool):
            for b in range(2):
                pool.memset(q[b][:].bitcast(F32), 0.0)
                last = pool.memset(kk[b][:, :, S2:].bitcast(F32), 0.0)
            last.then_inc(stack_zero, 1)
            for b in range(2):
                last = pool.memset(vv[b][:], 0.0)
            last.then_inc(v_zero, 1)
            if not biases:
                pool.memset(qk_bias[:], 0.0)
                pool.memset(v_bias[:], 0.0)
                pool.memset(o_bias[:], 0.0)
            pool.memset(half[:], -0.5).then_inc(const_ready, 1)

            def convert_mask(b, parity):
                wait_apart(pool, pool_passed, (mask_loaded[parity], (b - parity) * 8 + 16), (s_max, (b - 1) * H))
                pool.tensor_scalar(masked[parity][:], mask_raw[parity][:], -1.0, NEG * 1e20, ALU.add, ALU.mult)\
                    .then_inc(mask_ready, 1)

            if mask_by_batch:
                convert_mask(0, 0)

            def batch(b, parity, first, last):
                if mask_by_batch and not last:
                    convert_mask(b + 1, 1 - parity)
                if not first:
                    normalise(b - 1)

            def normalise(b):
                pool.wait_ge(var_ready, b + 1)
                pool.tensor_tensor(rstd[:], var[:], half[:], ALU.pow).then_inc(rstd_ready, 1)
                pool.wait_ge(xn_ready, b + 1)
                pool.tensor_copy(x[:, ds(b, 1), :], xn[:].unsqueeze(1)).then_inc(x_stored, 1)

            over_batches(pool, batch)
            normalise(B - 1)

        @block.tensor
        def _(pe):
            pe.wait_ge(const_loaded, 16 * (4 + (6 if biases else 0)))
            for n in range(4):
                if transposed[n]:
                    for k in range(DC):
                        for m in range(DC):
                            last = nc.tensor.transpose(ps[:, n, k * D + m * P:k * D + (m + 1) * P],
                                                       wraw[:, n, m, k * P:(k + 1) * P], ident[:])
                    last.then_inc(w_turned, 1)
            pe.wait_ge(w_ready, sum(transposed))

            def front(b, parity, u):
                bank = ps[:, FRONT + u % 2, :]
                wait_front_read(pe, b, u - 2)
                if u < 2:
                    if u == 0:
                        pe.wait_ge(ctx_loaded[parity], (b - parity) * 8 + 16)
                    for t in range(KT):
                        last = nc.tensor.transpose(bank[:, t * KP:(t + 1) * KP],
                                                   cx_raw[parity][:, t, u * P:(u + 1) * P], ident[0:KP, 0:KP])
                elif u in (2, 5):
                    if u == 2:
                        wait_front_read(pe, b, 1)
                    for t in (2,) if u == 2 else (0, 1):
                        for k in range(DC):
                            last = nc.tensor.matmul(bank[0:KP, t % 2 * D:(t % 2 + 1) * D],
                                                    cx[:, k, t * KP:(t + 1) * KP], w[VW][:, k, :],
                                                    start=k == 0, stop=k == DC - 1)
                    if u == 2:
                        for m in range(DC):
                            for k in range(DC):
                                last = nc.tensor.matmul(bank[:, D + m * T:D + (m + 1) * T],
                                                        w[QW][:, k, m * P:(m + 1) * P], xt[:, k, ds(b * T, T)],
                                                        start=k == 0, stop=k == DC - 1)
                else:
                    for k in range(DC):
                        last = nc.tensor.matmul(bank[:, 0:S2], w[KW][:, k, (u - 3) * P:(u - 2) * P], cx[:, k, :],
                                                start=k == 0, stop=k == DC - 1)
                last.then_inc(f_done, 1)

            def scores(b, parity, h):
                if h == 0:
                    wait_front_read(pe, b, UNITS - 1)
                    pe.wait_ge(q_stacked, (b + 1) * Q_PARTS * 16)
                    pe.wait_ge(k_stacked, (b + 1) * K_PARTS * 16)
                wait(pe, s_max, b * H + h - 1)
                nc.tensor.matmul(ps[0:T, SCORES + h % 2, 0:KEYS], q[parity][:, h // 2, h % 2, :],
                                 kk[parity][:, h // 2, :], start=True, stop=True).then_inc(s_done, 1)

            def turn(b, h):
                pe.wait_ge(exped, b * H + h + 1)
                wait_turned_read(pe, b, h - 2)
                for t in range(KT):
                    last = nc.tensor.transpose(ps[0:KP, TURNED + h % 2, t * T:(t + 1) * T],
                                               pr[:, h % NB, t * KP:(t + 1) * KP], ident[0:T, 0:T])
                last.then_inc(t_done, 1)

            def values(b, parity, h):
                wait_turned_read(pe, b, h)
                if h == 0:
                    wait(pe, o_read, b)
                r = h % 4 * 32
                for t in range(KT):
                    last = nc.tensor.matmul(ps[r:r + 32, OUT, h // 4 * T:(h // 4 + 1) * T], vv[parity][:, t, h, :],
                                            pt[:, h % NB, t * T:(t + 1) * T], start=t == 0, stop=t == KT - 1)
                last.then_inc(pv_done, 1)

            def tail(b, part):
                if part == 0:
                    pe.wait_ge(o_read, b + 1)
                    for g in range(4):
                        last = nc.tensor.transpose(ps[0:T, TAIL, g * P:(g + 1) * P], osb[:, g * T:(g + 1) * T], ident[:])
                    last.then_inc(t1_done, 1)
                elif part == 1:
                    pe.wait_ge(otok_ready, b + 1)
                    for k in range(DC):
                        last = nc.tensor.transpose(ps[:, TAIL, k * T:(k + 1) * T],
                                                   otok[:, k * 8:(k + 1) * 8, :].rearrange("p a b -> p (a b)"), ident[0:T, 0:T])
                    last.then_inc(t2_done, 1)
                elif part == 2:
                    pe.wait_ge(o_ready, b + 1)
                    for k in range(DC):
                        last = nc.tensor.matmul(ps[0:T, TAIL, 0:D], o[:, k, :], w[OW][:, k, :],
                                                start=k == 0, stop=k == DC - 1)
                    last.then_inc(y_done, 1)
                else:
                    pe.wait_ge(xn_ready, b + 1)
                    for k in range(DC):
                        last = nc.tensor.transpose(ps[:, TAIL, k * T:(k + 1) * T], xn[:, k * P:(k + 1) * P], ident[0:T, 0:T])
                    last.then_inc(xt_done, 1)

            TAIL_AT = {6: 0, 8: 1, 10: 2, 14: 3}
            FRONT_AT = {0: 0, 1: 1, 4: 2, 5: 3, 7: 4, 10: 5}

            def batch(b, parity, first, last):
                for i in range(H):
                    scores(b, parity, i)
                    if i >= TL:
                        turn(b, i - TL)
                    elif not first:
                        turn(b - 1, i - TL + H)
                    if not last and i in FRONT_AT:
                        front(b + 1, 1 - parity, FRONT_AT[i])
                    if not first and i in TAIL_AT:
                        tail(b - 1, TAIL_AT[i])
                    if i >= VL:
                        values(b, parity, i - VL)
                    elif not first:
                        values(b - 1, 1 - parity, i - VL + H)

            for u in range(UNITS):
                front(0, 0, u)
            over_batches(pe, batch)
            for h in range(H - TL, H):
                turn(B - 1, h)
            for h in range(H - VL, H):
                values(B - 1, 1, h)
            for part in range(4):
                tail(B - 1, part)

        @block.scalar
        def _(act):
            turned = [n for n in range(4) if transposed[n]]
            for i, n in enumerate(turned):
                act.wait_ge(w_turned, i + 1)
                nc.scalar.copy(w[n][:].rearrange("p a b -> p (a b)"), ps[:, n, :]).then_inc(w_ready, 1)
            if biases:
                act.wait_ge(const_loaded, 16 * 10)
            act.wait_ge(const_ready, 1)

            def front(b, parity, u):
                act.wait_ge(f_done, b * UNITS + u + 1)
                bank = ps[:, FRONT + u % 2, :]
                if u < 2:
                    nc.scalar.copy(cx[:, u, :], bank[:, 0:S2]).then_inc(f_act, 1)
                elif u == 2:
                    wait(act, q_stored, b * 16)
                    for m in range(DC):
                        last = nc.scalar.activation(qs[:, m, :], bank[:, D + m * T:D + (m + 1) * T], ACT.Identity,
                                                    bias=qk_bias[:, 0, m:m + 1])
                    last.then_inc(f_act, 1)
                else:
                    wait(act, k_stored, b * 16)
                    nc.scalar.activation(ks[:, u - 3, :], bank[:, 0:S2], ACT.Identity,
                                         bias=qk_bias[:, 1, u - 3:u - 2]).then_inc(f_act, 1)

            def exponent(b, parity, h):
                act.wait_ge(s_max, b * H + h + 1)
                wait(act, t_done, b * H + h - NB + 1)
                nc.scalar.activation(pr[:, h % NB, :], sc[:, h % NB, :], ACT.Exp, bias=mn[parity][:, h:h + 1],
                                     scale=-1.0, accum_out=rs[parity][:, h:h + 1]).then_inc(exped, 1)

            def evacuate(b, h):
                act.wait_ge(t_done, b * H + h + 1)
                wait(act, pv_done, b * H + h - NB + 1)
                nc.scalar.copy(pt[:, h % NB, :], ps[0:KP, TURNED + h % 2, 0:KT * T]).then_inc(pt_act, 1)

            def tail(b, part):
                if part == 0:
                    act.wait_ge(pv_done, b * H + H)
                    wait(act, t1_done, b)
                    nc.scalar.copy(osb[:], ps[:, OUT, 0:4 * T]).then_inc(o_read, 1)
                elif part == 1:
                    act.wait_ge(t2_done, b + 1)
                    nc.scalar.copy(o[:].rearrange("p a b -> p (a b)"), ps[:, TAIL, 0:DC * T]).then_inc(o_ready, 1)
                else:
                    act.wait_ge(xt_done, b + 1)
                    nc.scalar.copy(xt[:, :, ds(b * T, T)], ps[:, TAIL, 0:DC * T].rearrange("p (a b) -> p a b", a=DC))\
                        .then_inc(xt_ready, 1)

            TAIL_AT = {5: 0, 9: 1, 15: 2}
            FRONT_AT = {0: 0, 1: 1, 4: 2, 5: 3, 7: 4}

            def batch(b, parity, first, last):
                for i in range(H):
                    if not first and TAIL_AT.get(i) == 0:
                        tail(b - 1, 0)
                    if (i - EL) % 4 == 3:
                        if i >= EL:
                            evacuate(b, i - EL)
                        elif not first:
                            evacuate(b - 1, i - EL + H)
                    exponent(b, parity, i)
                    if not last and i in FRONT_AT:
                        front(b + 1, 1 - parity, FRONT_AT[i])
                    if not first and TAIL_AT.get(i, 0) > 0:
                        tail(b - 1, TAIL_AT[i])

            for u in range(ACT_UNITS):
                front(0, 0, u)
            over_batches(act, batch)
            evacuate(B - 1, H - 1)
            for part in range(3):
                tail(B - 1, part)

        @block.vector
        def _(dve):
            pre = Chain(dve, chain)
            dve.wait_ge(const_ready, 1)
            if biases:
                dve.wait_ge(const_loaded, 16 * 10)
            dve.wait_ge(v_zero, 1)
            if not mask_by_batch:
                dve.wait_ge(mask_loaded[0], 16)
                pre.link(nc.vector.tensor_scalar(masked[0][:], mask_raw[0][:], 0, NEG, ALU.not_equal, ALU.mult))
                pre.link(nc.vector.tensor_scalar_add(masked[0][:], masked[0][:], -NEG))
            before = pre.n

            def front(b, parity, u):
                if u == 5:
                    dve.wait_ge(f_done, b * UNITS + u + 1)
                else:
                    dve.wait_ge(f_act, b * ACT_UNITS + u + 1)
                bank = ps[:, FRONT + u % 2, :]
                if u == 2:
                    for m in range(DC):
                        nc.vector.scalar_tensor_tensor(out=qs[:, DC + m, :], in0=bank[:, D + m * T:D + (m + 1) * T],
                                                       scalar=qk_bias[:, 0, m:m + 1], in1=qs[:, m, :].bitcast(F32),
                                                       op0=ALU.add, op1=ALU.subtract)
                if u in (2, 5):
                    wait(dve, pv_done, (b - 1) * H)
                    for t in (2,) if u == 2 else (0, 1):
                        last = nc.vector.tensor_add(vv[parity][:, t, :, 0:HD],
                                                    bank[0:KP, t % 2 * D:(t % 2 + 1) * D]
                                                    .rearrange("p (h d) -> p h d", d=HD),
                                                    v_bias[0:KP].rearrange("p (h d) -> p h d", d=HD))
                else:
                    last = nc.vector.scalar_tensor_tensor(out=ks[:, DC + u - 3, :], in0=bank[:, 0:S2],
                                                          scalar=qk_bias[:, 1, u - 3:u - 2],
                                                          in1=ks[:, u - 3, :].bitcast(F32),
                                                          op0=ALU.add, op1=ALU.subtract)
                last.then_inc(f_dve, 1)

            def maximum(b, parity, h):
                wait_apart(dve, dve_passed, (s_done, b * H + h + 1), (exped, b * H + h - NB + 1))
                mask_of = masked[parity if mask_by_batch else 0]
                nc.vector.tensor_tensor_reduce(out=sc[:, h % NB, :], in0=ps[0:T, SCORES + h % 2, 0:S2], in1=mask_of[:],
                                               scale=-0.25, scalar=3e38, op0=ALU.add, op1=ALU.min,
                                               accum_out=mn[parity][:, h:h + 1]).then_inc(s_max, 1)

            def evacuate(b, h):
                dve.wait_ge(t_done, b * H + h + 1)
                wait(dve, pv_done, b * H + h - NB + 1)
                nc.vector.tensor_copy(pt[:, h % NB, :], ps[0:KP, TURNED + h % 2, 0:KT * T]).then_inc(pt_dve, 1)

            def tail(b, parity, part, ch):
                if part == 0:
                    dve.wait_ge(exped, b * H + H)
                    ch.link(nc.vector.reciprocal(ri[:], rs[parity][:]))
                    dve.wait_ge(t1_done, b + 1)
                    nc.vector.tensor_tensor(otok[:], ps[0:T, TAIL, :].rearrange("p (h e) -> p h e", e=32)[:, :, 0:HD],
                                            ri[:].unsqueeze(2).broadcast_to([T, H, HD]), ALU.mult).then_inc(otok_ready, 1)
                elif part == 1:
                    ch.link(nc.vector.tensor_add(y[:].unsqueeze(1), x[:, ds(b, 1), :], o_bias[:].unsqueeze(1)))
                    dve.wait_ge(y_done, b + 1)
                    ch.link(nc.vector.tensor_add(y[:], ps[0:T, TAIL, 0:D], y[:]))
                    ch.link(nc.vector.bn_stats(st[:], y[:]), dve_passed)
                    ch.link(nc.vector.bn_aggr(mv[:], st[:]))
                    nc.vector.tensor_scalar_add(var[:], mv[:, 1:2], EPS).then_inc(var_ready, 1)
                else:
                    dve.wait_ge(rstd_ready, b + 1)
                    wait(dve, x_stored, b)
                    nc.vector.tensor_scalar(xn[:], y[:], mv[:, 0:1], rstd[:], ALU.subtract, ALU.mult).then_inc(xn_ready, 1)

            TAIL_AT = {7: 0, 11: 1, 13: 2}
            FRONT_AT = {5: 2, 6: 3, 8: 4, 10: 5}

            def batch(b, parity, first, last):
                ch = Chain(dve, chain, before if first else before + (b - 1) * CHAIN)
                for i in range(H):
                    if mask_by_batch and i == 0:
                        dve.wait_ge(mask_ready, b + 1)
                    maximum(b, parity, i)
                    if not last and i in FRONT_AT:
                        front(b + 1, 1 - parity, FRONT_AT[i])
                    if not first and i in TAIL_AT:
                        tail(b - 1, 1 - parity, TAIL_AT[i], ch)
                    if (i - EL) % 4 != 3:
                        if i >= EL:
                            evacuate(b, i - EL)
                        elif not first:
                            evacuate(b - 1, i - EL + H)
                assert ch.n == (0 if first else CHAIN), ch.n

            for u in range(2, UNITS):
                front(0, 0, u)
            over_batches(dve, batch)
            for h in range(H - EL, H - 1):
                evacuate(B - 1, h)
            ch = Chain(dve, chain, before + (B - 1) * CHAIN)
            for part in range(3):
                tail(B - 1, 1, part, ch)


def stage_coupled_attention(nc, x, xt, ident, weights, biases, J, lam):
    with Stage(nc, "coupled") as s:
        QW, KW, VW, OW = range(4)
        GH = 4
        G = H // GH
        HP = P // HD
        wraw = s.sb("wraw", [P, 4, DC, D])
        w = [s.sb(f"w{n}", [P, DC, D]) for n in range(4)]
        qk_bias = s.sb("qk_bias", [P, 2, DC])
        v_bias = s.sb("v_bias", [T, D])
        o_bias = s.sb("o_bias", [T, D])
        Jd = s.sb("Jd", [P, DC, P])
        lam4 = s.sb("lam4", [P, 1])
        head_mask = s.sb("head_mask", [P, HP])
        half = s.sb("half", [T, 1])
        xs = s.sb("xs", [P, DC, T])
        k32 = s.sb("k32", [P, DC, T])
        qn = s.sb("qn", [P, DC, T])
        kn = s.sb("kn", [P, DC, T])
        q = [s.sb(f"q{b}", [P, DC, T]) for b in range(2)]
        qj = [s.sb(f"qj{b}", [P, DC, T]) for b in range(2)]
        km = [s.sb(f"km{b}", [P, DC, HP, T]) for b in range(2)]
        knm = [s.sb(f"knm{b}", [P, DC, HP, T]) for b in range(2)]
        vv = [s.sb(f"v{b}", [T, H, 32]) for b in range(2)]
        NB = 2
        sc = s.sb("sc", [T, NB, GH, T])
        mx = s.sb("mx", [T, NB, GH])
        pr = s.sb("pr", [T, NB, GH, T])
        rs = [s.sb(f"rs{b}", [T, H]) for b in range(2)]
        pt = s.sb("pt", [T, NB, GH, T])
        osb = s.sb("osb", [P, 4 * T])
        ri = s.sb("ri", [T, H])
        otok = s.sb("otok", [T, H, HD])
        o = s.sb("o", [P, DC, T])
        y = s.sb("y", [T, D])
        st = s.sb("st", [T, 6])
        mv = s.sb("mv", [T, 2])
        var = s.sb("var", [T, 1])
        rstd = s.sb("rstd", [T, 1])
        xn = s.sb("xn", [T, D])
        ps = s.banks("ps", 8)
        FRONT, SCORES, TURNED, OUT, TAIL = 0, 2, 4, 6, 7

        dve_passed = s.sem("dve_passed")
        const_loaded, w_turned, w_ready, J_zero = (s.sem(n) for n in ("const_loaded", "w_turned", "w_ready", "J_zero"))
        pool_chain, const_ready, v_zero, x_stored = (s.sem(n) for n in ("pool_chain", "const_ready", "v_zero", "x_stored"))
        xs_ready, qk_done, v_done, j_done = (s.sem(n) for n in ("xs_ready", "qk_done", "v_done", "j_done"))
        qk_ready, tanh_ready, v_ready, qj_ready, k_ready = (s.sem(n) for n in ("qk_ready", "tanh_ready", "v_ready", "qj_ready", "k_ready"))
        s_done, shifted, exped, summed, t_done, pt_ready, pv_done = (
            s.sem(n) for n in ("s_done", "shifted", "exped", "summed", "t_done", "pt_ready", "pv_done"))
        o_read, t1_done, otok_ready, t2_done = (s.sem(n) for n in ("o_read", "t1_done", "otok_ready", "t2_done"))
        o_ready, y_done, var_ready, rstd_ready = (s.sem(n) for n in ("o_ready", "y_done", "var_ready", "rstd_ready"))
        xn_ready, xt_done, xt_ready, chain = (s.sem(n) for n in ("xn_ready", "xt_done", "xt_ready", "chain"))
        CHAIN = G + 5
        LOADS = 11 + H
        block = s.block()

        def over_batches(engine, batch):
            batch(0, 0, True, False)
            with engine.Fori(0, (B - 2) // 2) as i:
                batch(i * 2 + 1, 1, False, False)
                batch(i * 2 + 2, 0, False, False)
            batch(B - 1, 1, False, True)

        @block.sync
        def _(sp):
            for n in range(4):
                sp.dma_start(wraw[:, n], weights[n].rearrange("(c p) n -> p c n", p=P)).then_inc(const_loaded, 16)
            for n in range(2):
                for m in range(DC):
                    sp.dma_start(qk_bias[:, n, m:m + 1], column(biases[n], m)).then_inc(const_loaded, 16)
            sp.dma_start(v_bias[:], rows(biases[2], T)).then_inc(const_loaded, 16)
            sp.dma_start(o_bias[:], rows(biases[3], T)).then_inc(const_loaded, 16)
            sp.dma_start(lam4[:], rows(lam, P)).then_inc(const_loaded, 16)
            sp.wait_ge(J_zero, 1)
            for h in range(H):
                r = h % HP * HD
                sp.dma_start(Jd[r:r + HD, h // HP, r:r + HD], J[h]).then_inc(const_loaded, 16)

        @block.gpsimd
        def _(pool):
            c = Chain(pool, pool_chain)
            pool.memset(Jd[:], 0.0).then_inc(J_zero, 1)
            pool.memset(half[:], -0.5)
            for b in range(2):
                last = pool.memset(vv[b][:], 0.0)
            last.then_inc(v_zero, 1)
            c.link(pool.memset(head_mask[:], 1.0))
            c.link(pool.affine_select(out=head_mask[:], in_=head_mask[:], compare_op=ALU.is_ge, fill=0.0, base=0,
                                      pattern=[[-HD, HP]], channel_multiplier=1))
            pool.affine_select(out=head_mask[:], in_=head_mask[:], compare_op=ALU.is_ge, fill=0.0, base=HD - 1,
                               pattern=[[HD, HP]], channel_multiplier=-1).then_inc(const_ready, 1)

            def normalise(b):
                pool.wait_ge(var_ready, b + 1)
                pool.tensor_tensor(rstd[:], var[:], half[:], ALU.pow).then_inc(rstd_ready, 1)
                pool.wait_ge(xn_ready, b + 1)
                pool.tensor_copy(x[:, ds(b, 1), :], xn[:].unsqueeze(1)).then_inc(x_stored, 1)

            def batch(b, parity, first, last):
                if not first:
                    normalise(b - 1)

            over_batches(pool, batch)
            normalise(B - 1)

        @block.tensor
        def _(pe):
            pe.wait_ge(const_loaded, 16 * LOADS)
            for n in range(4):
                for k in range(DC):
                    for m in range(DC):
                        last = nc.tensor.transpose(ps[:, n, k * D + m * P:k * D + (m + 1) * P],
                                                   wraw[:, n, m, k * P:(k + 1) * P], ident[:])
                last.then_inc(w_turned, 1)
            pe.wait_ge(w_ready, 4)

            def front(b, parity, u):
                bank = ps[:, FRONT + u % 2, :]
                if u == 0:
                    pe.wait_ge(xs_ready, b + 1)
                    wait(pe, qj_ready, b)
                    for n, wn in ((0, QW), (1, KW)):
                        for m in range(DC):
                            for k in range(DC):
                                last = nc.tensor.matmul(bank[:, (n * DC + m) * T:(n * DC + m + 1) * T],
                                                        w[wn][:, k, m * P:(m + 1) * P], xs[:, k, :],
                                                        start=k == 0, stop=k == DC - 1)
                    last.then_inc(qk_done, 1)
                elif u == 1:
                    wait(pe, v_ready, b)
                    for k in range(DC):
                        last = nc.tensor.matmul(bank[0:T, 0:D], xs[:, k, :], w[VW][:, k, :],
                                                start=k == 0, stop=k == DC - 1)
                    last.then_inc(v_done, 1)
                else:
                    pe.wait_ge(tanh_ready, 2 * b + 2)
                    for m in range(DC):
                        last = nc.tensor.matmul(bank[:, m * T:(m + 1) * T], Jd[:, m, :], qn[:, m, :], start=True, stop=True)
                    last.then_inc(j_done, 1)

            def scores(b, parity, g):
                if g == 0:
                    pe.wait_ge(k_ready, b + 1)
                    pe.wait_ge(qj_ready, b + 1)
                wait(pe, shifted, b * G + g - 1)
                c, h = g * GH // HP, g * GH % HP
                bank = ps[0:T, SCORES + g % 2, 0:GH * T]
                nc.tensor.matmul(bank, q[parity][:, c, :], km[parity][:, c, h:h + GH, :].rearrange("p a b -> p (a b)"),
                                 start=True, stop=False)
                nc.tensor.matmul(bank, qj[parity][:, c, :], knm[parity][:, c, h:h + GH, :].rearrange("p a b -> p (a b)"),
                                 start=False, stop=True).then_inc(s_done, 1)

            def turn(b, g):
                pe.wait_ge(exped, b * G + g + 1)
                wait(pe, pt_ready, b * G + g - 1)
                for j in range(GH):
                    last = nc.tensor.transpose(ps[0:T, TURNED + g % 2, j * T:(j + 1) * T], pr[:, g % NB, j, :], ident[0:T, 0:T])
                last.then_inc(t_done, 1)

            def values(b, parity, g):
                pe.wait_ge(pt_ready, b * G + g + 1)
                if g == 0:
                    wait(pe, o_read, b)
                    pe.wait_ge(v_ready, b + 1)
                for j in range(GH):
                    last = nc.tensor.matmul(ps[j * 32:j * 32 + 32, OUT, g * T:(g + 1) * T], vv[parity][:, g * GH + j, :],
                                            pt[:, g % NB, j, :], start=True, stop=True)
                last.then_inc(pv_done, 1)

            def tail(b, part):
                if part == 0:
                    pe.wait_ge(o_read, b + 1)
                    for g in range(4):
                        last = nc.tensor.transpose(ps[0:T, TAIL, g * P:(g + 1) * P], osb[:, g * T:(g + 1) * T], ident[:])
                    last.then_inc(t1_done, 1)
                elif part == 1:
                    pe.wait_ge(otok_ready, b + 1)
                    for k in range(DC):
                        last = nc.tensor.transpose(ps[:, TAIL, k * T:(k + 1) * T],
                                                   otok[:, k * 8:(k + 1) * 8, :].rearrange("p a b -> p (a b)"), ident[0:T, 0:T])
                    last.then_inc(t2_done, 1)
                elif part == 2:
                    pe.wait_ge(o_ready, b + 1)
                    for k in range(DC):
                        last = nc.tensor.matmul(ps[0:T, TAIL, 0:D], o[:, k, :], w[OW][:, k, :],
                                                start=k == 0, stop=k == DC - 1)
                    last.then_inc(y_done, 1)
                else:
                    pe.wait_ge(xn_ready, b + 1)
                    for k in range(DC):
                        last = nc.tensor.transpose(ps[:, TAIL, k * T:(k + 1) * T], xn[:, k * P:(k + 1) * P], ident[0:T, 0:T])
                    last.then_inc(xt_done, 1)

            for u in range(3):
                front(0, 0, u)

            def steps(b, parity, first, last):
                for g in range(G):
                    scores(b, parity, g)
                    if not first and g == 0:
                        turn(b - 1, G - 1)
                    if g >= 1:
                        turn(b, g - 1)
                    if not last and g < 3:
                        front(b + 1, 1 - parity, g)
                    if not first and g == 0:
                        values(b - 1, 1 - parity, G - 2)
                        values(b - 1, 1 - parity, G - 1)
                    if g >= 2:
                        values(b, parity, g - 2)
                    if not first and g in (1, 2, 3):
                        tail(b - 1, g - 1)
                    if not first and g == 3:
                        tail(b - 1, 3)

            over_batches(pe, steps)
            turn(B - 1, G - 1)
            values(B - 1, 1, G - 2)
            values(B - 1, 1, G - 1)
            for part in range(4):
                tail(B - 1, part)

        @block.scalar
        def _(act):
            for n in range(4):
                act.wait_ge(w_turned, n + 1)
                nc.scalar.copy(w[n][:].rearrange("p a b -> p (a b)"), ps[:, n, :]).then_inc(w_ready, 1)
            act.wait_ge(const_ready, 2)

            def front(b, parity, u):
                bank = ps[:, FRONT + u % 2, :]
                if u == 0:
                    wait(act, v_done, b)
                    nc.scalar.copy(xs[:], xt[:, :, ds(b * T, T)]).then_inc(xs_ready, 1)
                elif u == 1:
                    act.wait_ge(qk_done, b + 1)
                    wait(act, k_ready, b)
                    for m in range(DC):
                        nc.scalar.activation(q[parity][:, m, :], bank0[:, m * T:(m + 1) * T], ACT.Identity,
                                             bias=qk_bias[:, 0, m:m + 1])
                    for m in range(DC):
                        last = nc.scalar.activation(k32[:, m, :], bank0[:, (DC + m) * T:(DC + m + 1) * T], ACT.Identity,
                                                    bias=qk_bias[:, 1, m:m + 1])
                    last.then_inc(qk_ready, 1)
                    act.wait_ge(qk_ready, b + 1)
                    nc.scalar.activation(qn[:], q[parity][:], ACT.Tanh).then_inc(tanh_ready, 1)
                    nc.scalar.activation(kn[:], k32[:], ACT.Tanh).then_inc(tanh_ready, 1)
                else:
                    act.wait_ge(j_done, b + 1)
                    nc.scalar.activation(qj[parity][:].rearrange("p a b -> p (a b)"), bank0[:, 0:DC * T], ACT.Identity,
                                         scale=lam4[:]).then_inc(qj_ready, 1)

            bank0 = ps[:, FRONT, :]

            def exponent(b, g):
                act.wait_ge(shifted, b * G + g + 1)
                wait(act, t_done, b * G + g - NB + 1)
                wait(act, summed, b * G + g - NB + 1)
                nc.scalar.activation(pr[:, g % NB], sc[:, g % NB], ACT.Exp, scale=0.25).then_inc(exped, 1)

            def evacuate(b, g):
                act.wait_ge(t_done, b * G + g + 1)
                wait(act, pv_done, b * G + g - NB + 1)
                nc.scalar.copy(pt[:, g % NB].rearrange("p a b -> p (a b)"), ps[0:T, TURNED + g % 2, 0:GH * T])\
                    .then_inc(pt_ready, 1)

            def tail(b, part):
                if part == 0:
                    act.wait_ge(pv_done, b * G + G)
                    wait(act, t1_done, b)
                    nc.scalar.copy(osb[:], ps[:, OUT, 0:4 * T]).then_inc(o_read, 1)
                elif part == 1:
                    act.wait_ge(t2_done, b + 1)
                    nc.scalar.copy(o[:].rearrange("p a b -> p (a b)"), ps[:, TAIL, 0:DC * T]).then_inc(o_ready, 1)
                else:
                    act.wait_ge(xt_done, b + 1)
                    nc.scalar.copy(xt[:, :, ds(b * T, T)], ps[:, TAIL, 0:DC * T].rearrange("p (a b) -> p a b", a=DC))\
                        .then_inc(xt_ready, 1)

            def batch(b, parity, first, last):
                for g in range(G):
                    if not last and g == 0:
                        front(b + 1, 1 - parity, 0)
                    exponent(b, g)
                    if g == 0 and not first:
                        evacuate(b - 1, G - 1)
                        tail(b - 1, 0)
                    if g >= 1:
                        evacuate(b, g - 1)
                    if not last and g in (0, 2):
                        front(b + 1, 1 - parity, 1 + g // 2)
                    if not first and g == 2:
                        tail(b - 1, 1)
                if not first:
                    tail(b - 1, 2)

            for u in range(3):
                front(0, 0, u)
            over_batches(act, batch)
            evacuate(B - 1, G - 1)
            for part in range(3):
                tail(B - 1, part)

        @block.vector
        def _(dve):
            dve.wait_ge(const_loaded, 16 * LOADS)
            nc.vector.tensor_scalar_mul(lam4[:], lam4[:], 4.0).then_inc(const_ready, 1)
            dve.wait_ge(const_ready, 2)
            dve.wait_ge(v_zero, 1)

            def front(b, parity, u):
                if u == 0:
                    dve.wait_ge(v_done, b + 1)
                    nc.vector.tensor_add(vv[parity][:, :, 0:HD], ps[0:T, FRONT + 1, 0:D].rearrange("p (h d) -> p h d", d=HD),
                                         v_bias[:].rearrange("p (h d) -> p h d", d=HD)).then_inc(v_ready, 1)
                else:
                    dve.wait_ge(tanh_ready, 2 * b + 2)
                    for h in range(HP):
                        nc.vector.tensor_scalar(km[parity][:, :, h, :], k32[:], head_mask[:, h:h + 1], None, ALU.mult)
                        last = nc.vector.tensor_scalar(knm[parity][:, :, h, :], kn[:], head_mask[:, h:h + 1], None, ALU.mult)
                    last.then_inc(k_ready, 1)

            def shift(b, g, ch):
                dve.wait_ge(s_done, b * G + g + 1)
                bank = ps[0:T, SCORES + g % 2, 0:GH * T].rearrange("p (a b) -> p a b", a=GH)
                ch.link(nc.vector.reduce_max(mx[:, g % NB], bank, axis=AX.X))
                wait(dve, exped, b * G + g - NB + 1)
                nc.vector.tensor_tensor(sc[:, g % NB], bank, mx[:, g % NB].unsqueeze(2).broadcast_to([T, GH, T]),
                                        ALU.subtract).then_inc(shifted, 1)

            def total(b, parity, g):
                dve.wait_ge(exped, b * G + g + 1)
                nc.vector.reduce_sum(rs[parity][:, g * GH:(g + 1) * GH], pr[:, g % NB], axis=AX.X).then_inc(summed, 1)

            def tail(b, parity, part, ch):
                if part == 0:
                    dve.wait_ge(summed, b * G + G)
                    ch.link(nc.vector.reciprocal(ri[:], rs[parity][:]))
                    dve.wait_ge(t1_done, b + 1)
                    nc.vector.tensor_tensor(otok[:], ps[0:T, TAIL, :].rearrange("p (h e) -> p h e", e=32)[:, :, 0:HD],
                                            ri[:].unsqueeze(2).broadcast_to([T, H, HD]), ALU.mult).then_inc(otok_ready, 1)
                elif part == 1:
                    ch.link(nc.vector.tensor_add(y[:].unsqueeze(1), x[:, ds(b, 1), :], o_bias[:].unsqueeze(1)))
                    dve.wait_ge(y_done, b + 1)
                    ch.link(nc.vector.tensor_add(y[:], ps[0:T, TAIL, 0:D], y[:]))
                    ch.link(nc.vector.bn_stats(st[:], y[:]), dve_passed)
                    ch.link(nc.vector.bn_aggr(mv[:], st[:]))
                    nc.vector.tensor_scalar_add(var[:], mv[:, 1:2], EPS).then_inc(var_ready, 1)
                else:
                    dve.wait_ge(rstd_ready, b + 1)
                    wait(dve, x_stored, b)
                    nc.vector.tensor_scalar(xn[:], y[:], mv[:, 0:1], rstd[:], ALU.subtract, ALU.mult).then_inc(xn_ready, 1)

            def batch(b, parity, first, last):
                ch = Chain(dve, chain, b * CHAIN if first else b * CHAIN - 5)
                for g in range(G):
                    shift(b, g, ch)
                    if g == 0 and not first:
                        total(b - 1, 1 - parity, G - 1)
                    if g >= 1:
                        total(b, parity, g - 1)
                    if not first and g == 1:
                        tail(b - 1, 1 - parity, 0, ch)
                    if not last and g == 1:
                        front(b + 1, 1 - parity, 0)
                        front(b + 1, 1 - parity, 1)
                    if not first and g == 3:
                        tail(b - 1, 1 - parity, 1, ch)
                        tail(b - 1, 1 - parity, 2, ch)

            for u in range(2):
                front(0, 0, u)
            over_batches(dve, batch)
            total(B - 1, 1, G - 1)
            ch = Chain(dve, chain, B * CHAIN - 5)
            for part in range(3):
                tail(B - 1, 1, part, ch)


def split_tokens(nc, s, act, dve, xt, xh, xl, high_ready, low_ready):
    for c in range(NC):
        cols = slice(c * CT, (c + 1) * CT)
        if act is not None:
            nc.scalar.copy(xh[:, :, cols], xt[:, :, cols]).then_inc(high_ready, 1)
        if dve is not None:
            dve.wait_ge(high_ready, c + 1)
            nc.vector.tensor_sub(xl[:, :, cols], xt[:, :, cols], xh[:, :, cols].bitcast(F32)).then_inc(low_ready, 1)


def top_two(nc, chain, ramp, values, best, second, sel1, sel2, work, groups, E):
    def wide(v):
        return v[:].unsqueeze(2).broadcast_to([T, groups, E])

    for n, (top, sel) in enumerate(((best, sel1), (second, sel2))):
        chain.link(nc.vector.reduce_max(top[:], values[:], axis=AX.X))
        chain.link(nc.vector.tensor_tensor(sel[:], values[:], wide(top), ALU.is_equal))
        chain.link(nc.vector.tensor_tensor(sel[:], sel[:], ramp[:].unsqueeze(1).broadcast_to([T, groups, E]), ALU.mult))
        chain.link(nc.vector.reduce_max(work[:], sel[:], axis=AX.X))
        chain.link(nc.vector.tensor_tensor(sel[:], sel[:], wide(work), ALU.is_equal))
        if n == 0:
            chain.link(nc.vector.scalar_tensor_tensor(out=values[:], in0=sel[:], scalar=-3e38, in1=values[:],
                                                      op0=ALU.mult, op1=ALU.add))


def stage_moe_routes(nc, x, xt, ident, gate_w, gate_b, b2, bs2, comb_t, acc, E):
    with Stage(nc, "routes") as s:
        gw = s.sb("gw", [P, DC, E])
        gb = s.sb("gb", [T, E])
        b2_all = s.sb("b2_all", [E + 1, D])
        ramp = s.sb("ramp", [T, E])
        logits = s.sb("logits", [T, B, E])
        best, second, work, share, rest = (s.sb(n, [T, B]) for n in ("best", "second", "work", "share", "rest"))
        sel1, sel2 = (s.sb(n, [T, B, E]) for n in ("sel1", "sel2"))
        comb = s.sb("comb", [T, B, E + 1])
        ps = s.banks("ps", 8)
        loaded, ramp_ready, logits_done, chain_sem = (s.sem(n) for n in ("loaded", "ramp_ready", "logits_done", "chain"))
        gap_ready, exped, comb_ready, turned, comb_t_ready, bias_done, acc_ready = (
            s.sem(n) for n in ("gap_ready", "exped", "comb_ready", "turned", "comb_t_ready", "bias_done", "acc_ready"))
        block = s.block()

        @block.sync
        def _(sp):
            sp.dma_start(gw[:], gate_w.rearrange("(c p) e -> p c e", p=P)).then_inc(loaded, 16)
            sp.dma_start(gb[:], rows(gate_b, T)).then_inc(loaded, 16)
            sp.dma_start(b2_all[0:E, :], b2).then_inc(loaded, 16)
            sp.dma_start(b2_all[E:E + 1, :], bs2.rearrange("(a n) -> a n", a=1)).then_inc(loaded, 16)

        @block.gpsimd
        def _(pool):
            pool.iota(ramp[:], pattern=[[-1, E]], base=E, channel_multiplier=0,
                      allow_small_or_imprecise_dtypes=True)
            pool.memset(comb[:], 1.0).then_inc(ramp_ready, 1)

        @block.tensor
        def _(pe):
            pe.wait_ge(loaded, 64)
            for b in range(B):
                for k in range(DC):
                    last = nc.tensor.matmul(ps[0:T, 0, b * E:(b + 1) * E], xt[:, k, b * T:(b + 1) * T], gw[:, k, :],
                                            start=k == 0, stop=k == DC - 1)
            last.then_inc(logits_done, 1)
            pe.wait_ge(comb_ready, 1)
            for b in range(B):
                last = nc.tensor.transpose(ps[0:E + 1, 1 + b // CB, b % CB * T:(b % CB + 1) * T], comb[:, b, :], ident[0:T, 0:T])
                if b % CB == CB - 1:
                    last.then_inc(turned, 1)
            for c in range(NC):
                pe.wait_ge(comb_t_ready, c + 1)
                for m in range(DC):
                    n = c * DC + m
                    if n >= 2:
                        pe.wait_ge(acc_ready, n - 1)
                    nc.tensor.matmul(ps[:, 5 + n % 2, 0:CT], b2_all[:, m * P:(m + 1) * P], comb_t[:, c * CT:(c + 1) * CT],
                                     start=True, stop=True).then_inc(bias_done, 1)

        @block.scalar
        def _(act):
            act.wait_ge(gap_ready, 1)
            nc.scalar.activation(share[:], work[:], ACT.Exp).then_inc(exped, 1)
            for c in range(NC):
                act.wait_ge(turned, c + 1)
                nc.scalar.copy(comb_t[:, c * CT:(c + 1) * CT], ps[0:E + 1, 1 + c, 0:CT]).then_inc(comb_t_ready, 1)

        @block.vector
        def _(dve):
            c = Chain(dve, chain_sem)
            dve.wait_ge(ramp_ready, 1)
            dve.wait_ge(loaded, 64)
            dve.wait_ge(logits_done, 1)
            c.link(nc.vector.tensor_tensor(logits[:], ps[0:T, 0, 0:B * E].rearrange("p (b e) -> p b e", e=E),
                                           gb[:].unsqueeze(1).broadcast_to([T, B, E]), ALU.add))
            top_two(nc, c, ramp, logits, best, second, sel1, sel2, work, B, E)
            nc.vector.tensor_sub(work[:], second[:], best[:]).then_inc(gap_ready, 1)
            dve.wait_ge(exped, 1)
            c.link(nc.vector.tensor_scalar_add(rest[:], share[:], 1.0))
            c.link(nc.vector.reciprocal(rest[:], rest[:]))
            c.link(nc.vector.tensor_mul(share[:], share[:], rest[:]))
            c.link(nc.vector.tensor_tensor(sel1[:], sel1[:], rest[:].unsqueeze(2).broadcast_to([T, B, E]), ALU.mult))
            c.link(nc.vector.tensor_tensor(sel2[:], sel2[:], share[:].unsqueeze(2).broadcast_to([T, B, E]), ALU.mult))
            nc.vector.tensor_add(comb[:, :, 0:E], sel1[:], sel2[:]).then_inc(comb_ready, 1)
            for n in range(NC * DC):
                dve.wait_ge(bias_done, n + 1)
                cols = slice(n // DC * CT, (n // DC + 1) * CT)
                nc.vector.tensor_add(acc[:, n % DC, cols], ps[:, 5 + n % 2, 0:CT], xt[:, n % DC, cols]).then_inc(acc_ready, 1)


def stage_moe(nc, x, xt, ident, w1, b1, w2, ws1, bs1, ws2, comb_t, acc, E, HID):
    HT = HID // P
    with Stage(nc, "moe") as s:
        xh, xl = (s.sb(n, [P, DC, TOK], F32R) for n in ("xh", "xl"))
        w1_raw = s.sb("w1_raw", [P, DC, HID])
        w2_raw = s.sb("w2_raw", [P, HT, D])
        w1s = [[s.sb(f"w1_{b}{i}", [P, DC, HID], F32R) for i in range(2)] for b in range(2)]
        w2s = [[s.sb(f"w2_{b}{i}", [P, HT, D], F32R) for i in range(2)] for b in range(2)]
        b1_rows = s.sb("b1_rows", [(E + 1) * HT, P])
        b1_all = s.sb("b1_all", [P, (E + 1) * HT])
        b1c = [s.sb(f"b1c{b}", [P, HT]) for b in range(2)]
        ones = s.sb("ones", [E + 1, P])
        cm = s.sb("cm", [E + 1, TOK])
        gate = s.sb("gate", [P, 2, CT])
        h32 = s.sb("h32", [P, 2, CT])
        hh, hl = (s.sb(n, [P, HT, CT], F32R) for n in ("hh", "hl"))
        part = s.sb("part", [P, DC, CT])
        ps = s.banks("ps", 8)
        UP, GATE, DOWN = 0, 2, 4
        b_loaded, ones_ready, b_turned, b_ready = (s.sem(n) for n in ("b_loaded", "ones_ready", "b_turned", "b_ready"))
        w_loaded, w_high, w_low, bc_ready, cm_ready = (s.sem(n) for n in ("w_loaded", "w_high", "w_low", "bc_ready", "cm_ready"))
        x_high, x_low, up_done, gelu_done, chain, h_ready, down_done = (
            s.sem(n) for n in ("x_high", "x_low", "up_done", "gelu_done", "chain", "h_ready", "down_done"))
        gate_done, gate_ready, item_done, added = (s.sem(n) for n in ("gate_done", "gate_ready", "item_done", "added"))
        PIECES = 4
        ITEM_LINKS = HT + 1
        block = s.block()

        def pieces(parity):
            half = HT // 2
            return [(w1_raw[:, k, :], w1s[parity][0][:, k, :], w1s[parity][1][:, k, :]) for k in range(DC)] + \
                   [(w2_raw[:, n:n + half, :], w2s[parity][0][:, n:n + half, :], w2s[parity][1][:, n:n + half, :])
                    for n in (0, half)]

        def over_experts(engine, turn):
            turn(0, 0, True, False)
            with engine.Fori(0, (E - 2) // 2) as i:
                turn(i * 2 + 1, 1, False, False)
                turn(i * 2 + 2, 0, False, False)
            turn(E - 1, 1, False, False)
            turn(E, 0, False, True)

        @block.sync
        def _(sp):
            sp.dma_start(w1_raw[:], ws1.rearrange("(c p) n -> p c n", p=P)).then_inc(w_loaded, 16)
            sp.dma_start(w2_raw[:], ws2.rearrange("(m p) n -> p m n", p=P)).then_inc(w_loaded, 16)
            sp.dma_start(b1_rows[0:E * HT, :], b1.rearrange("e (m p) -> (e m) p", p=P)).then_inc(b_loaded, 16)
            sp.dma_start(b1_rows[E * HT:(E + 1) * HT, :], bs1.rearrange("(m p) -> m p", p=P)).then_inc(b_loaded, 16)
            with sp.Fori(0, E) as e:
                sp.wait_ge(w_low, e * PIECES + PIECES)
                sp.dma_start(w1_raw[:].unsqueeze(1), w1[ds(e, 1)].rearrange("a (c p) n -> p a c n", p=P)).then_inc(w_loaded, 16)
                sp.dma_start(w2_raw[:].unsqueeze(1), w2[ds(e, 1)].rearrange("a (m p) n -> p a m n", p=P)).then_inc(w_loaded, 16)

        @block.gpsimd
        def _(pool):
            pool.memset(ones[:], 1.0).then_inc(ones_ready, 1)

        @block.tensor
        def _(pe):
            pe.wait_ge(b_loaded, 32)
            nc.tensor.transpose(ps[:, GATE, 0:(E + 1) * HT], b1_rows[:], ident[0:(E + 1) * HT, 0:(E + 1) * HT]).then_inc(b_turned, 1)
            pe.wait_ge(b_ready, 1)
            pe.wait_ge(ones_ready, 1)
            pe.wait_ge(x_low, NC)

            def up(t, parity, c, j):
                wait(pe, gelu_done, (t * NC + c) * HT + j - 1)
                for k in range(DC):
                    last = split_product(nc, ps[:, UP + j % 2, 0:CT], [w[:, k, j * P:(j + 1) * P] for w in w1s[parity]],
                                         [a[:, k, c * CT:(c + 1) * CT] for a in (xh, xl)], k == 0, k == DC - 1)
                last.then_inc(up_done, 1)

            def down(t, parity, c, j):
                n = t * NC + c
                pe.wait_ge(h_ready, n * HT + j + 1)
                if j == 0:
                    wait(pe, added, n - 1)
                for m in range(DC):
                    last = split_product(nc, ps[:, DOWN + 2 * (c % 2) + m, 0:CT],
                                         [w[:, j, m * P:(m + 1) * P] for w in w2s[parity]], [hh[:, j, :], hl[:, j, :]],
                                         j == 0, j == HT - 1)
                last.then_inc(down_done, 1)

            def turn(t, parity, first, last):
                pe.wait_ge(w_low, t * PIECES + PIECES)
                for c in range(NC):
                    pe.wait_ge(cm_ready, t + 1)
                    wait(pe, gate_ready, t * NC + c)
                    nc.tensor.matmul(ps[:, GATE, 0:CT], ones[:], cm[:, c * CT:(c + 1) * CT], start=True, stop=True)\
                        .then_inc(gate_done, 1)
                    for j in range(HT):
                        up(t, parity, c, j)
                        if c > 0:
                            down(t, parity, c - 1, j)
                        elif not first:
                            down(t - 1, 1 - parity, NC - 1, j)

            over_experts(pe, turn)
            for j in range(HT):
                down(E, 0, NC - 1, j)

        def next_piece(c, j):
            return {(1, 1): 0, (1, 4): 1, (2, 1): 2, (2, 4): 3}.get((c, j))

        @block.scalar
        def _(act):
            act.wait_ge(w_loaded, 32)
            split_tokens(nc, s, act, None, xt, xh, xl, x_high, x_low)
            for raw, high, low in pieces(0):
                nc.scalar.copy(high, raw).then_inc(w_high, 1)
            act.wait_ge(b_turned, 1)
            nc.scalar.copy(b1_all[:], ps[:, GATE, 0:(E + 1) * HT]).then_inc(b_ready, 1)
            act.wait_ge(b_ready, 1)

            def turn(t, parity, first, last):
                wait(act, gelu_done, t * NC * HT - NC * HT + 1)
                e = E if first else t - 1
                nc.scalar.copy(b1c[parity][:], b1_all[:, ds(e * HT, HT)]).then_inc(bc_ready, 1)
                act.wait_ge(bc_ready, t + 1)
                for c in range(NC):
                    for j in range(HT):
                        n = (t * NC + c) * HT + j
                        act.wait_ge(up_done, n + 1)
                        wait(act, h_ready, n - 1)
                        nc.scalar.activation(h32[:, j % 2, :], ps[:, UP + j % 2, 0:CT], ACT.Gelu,
                                             bias=b1c[parity][:, j:j + 1]).then_inc(gelu_done, 1)
                        if j == 3:
                            act.wait_ge(gate_done, t * NC + c + 1)
                            wait(act, added, t * NC + c - 1)
                            nc.scalar.copy(gate[:, c % 2, :], ps[:, GATE, 0:CT]).then_inc(gate_ready, 1)
                        piece = next_piece(c, j)
                        if not last and piece is not None:
                            if piece == 0:
                                act.wait_ge(w_loaded, t * 32 + 64)
                                wait(act, down_done, t * NC * HT)
                            raw, high, low = pieces(1 - parity)[piece]
                            nc.scalar.copy(high, raw).then_inc(w_high, 1)

            over_experts(act, turn)

        @block.vector
        def _(dve):
            nc.vector.tensor_scalar(cm[:], comb_t[:], ident[0:E + 1, E:E + 1], None, ALU.mult).then_inc(cm_ready, 1)
            split_tokens(nc, s, None, dve, xt, xh, xl, x_high, x_low)
            for n, (raw, high, low) in enumerate(pieces(0)):
                dve.wait_ge(w_high, n + 1)
                nc.vector.tensor_sub(low, raw, high.bitcast(F32)).then_inc(w_low, 1)

            def add(t, c, ch):
                n = t * NC + c
                dve.wait_ge(down_done, n * HT + HT)
                dve.wait_ge(gate_ready, n + 1)
                wait(dve, added, n)
                ch.link(nc.vector.tensor_tensor(part[:], ps[:, DOWN + 2 * (c % 2):DOWN + 2 * (c % 2) + 2, 0:CT],
                                                gate[:, c % 2, :].unsqueeze(1).broadcast_to([P, DC, CT]), ALU.mult))
                cols = slice(c * CT, (c + 1) * CT)
                nc.vector.tensor_add(acc[:, :, cols], acc[:, :, cols], part[:]).then_inc(added, 1)

            def turn(t, parity, first, last):
                for c in range(NC):
                    n = t * NC + c
                    ch = Chain(dve, chain, n * ITEM_LINKS - (min(n, 2) if first else 2))
                    for j in range(HT):
                        dve.wait_ge(gelu_done, n * HT + j + 1)
                        wait(dve, down_done, n * HT + j + 1 - HT)
                        ch.link(nc.vector.tensor_copy(hh[:, j, :], h32[:, j % 2, :]))
                        nc.vector.tensor_sub(hl[:, j, :], h32[:, j % 2, :], hh[:, j, :].bitcast(F32)).then_inc(h_ready, 1)
                        piece = next_piece(c, j)
                        if not last and piece is not None:
                            raw, high, low = pieces(1 - parity)[piece]
                            dve.wait_ge(w_high, t * PIECES + PIECES + piece + 1)
                            nc.vector.tensor_sub(low, raw, high.bitcast(F32)).then_inc(w_low, 1)
                        if c == NC - 1 and j == HT - 1 and not last:
                            dve.wait_ge(gate_done, n + 1)
                            nc.vector.tensor_scalar(cm[:], comb_t[:], ident[0:E + 1, ds(t, 1)], None, ALU.mult)\
                                .then_inc(cm_ready, 1)
                        if j == 1 and c > 1:
                            add(t, c - 2, ch)
                        elif j == 1 and not first:
                            add(t - 1, NC - 2 + c, ch)

            over_experts(dve, turn)
            ch = Chain(dve, chain, (E + 1) * NC * ITEM_LINKS - 2)
            for c in (NC - 2, NC - 1):
                add(E, c, ch)


def stage_moe_norm(nc, x, xt, ident, acc):
    with Stage(nc, "moenorm") as s:
        half = s.sb("half", [T, B])
        st = s.sb("st", [T, B, 6])
        mv = s.sb("mv", [T, B, 2])
        var = s.sb("var", [T, B])
        rstd = s.sb("rstd", [T, B])
        ps = s.banks("ps", 8)
        turned, chain, half_ready, var_ready, rstd_ready, x_ready, xt_done, xt_ready = (
            s.sem(n) for n in ("turned", "chain", "half_ready", "var_ready", "rstd_ready", "x_ready", "xt_done", "xt_ready"))
        block = s.block()

        def token_major(b):
            return ps[0:T, b // 2, (b % 2) * D:(b % 2 + 1) * D]

        @block.gpsimd
        def _(pool):
            pool.memset(half[:], -0.5).then_inc(half_ready, 1)
            pool.wait_ge(half_ready, 1)
            for c in range(NC):
                pool.wait_ge(var_ready, c + 1)
                pool.tensor_tensor(rstd[:, c * CB:(c + 1) * CB], var[:, c * CB:(c + 1) * CB],
                                   half[:, c * CB:(c + 1) * CB], ALU.pow).then_inc(rstd_ready, 1)

        @block.tensor
        def _(pe):
            for b in range(B):
                for k in range(DC):
                    last = nc.tensor.transpose(token_major(b)[:, k * P:(k + 1) * P], acc[:, k, b * T:(b + 1) * T], ident[:])
                if b % 2:
                    last.then_inc(turned, 1)
            for c in range(NC):
                pe.wait_ge(x_ready, c + 1)
                for k in range(DC):
                    for j in range(CB):
                        last = nc.tensor.transpose(ps[:, 2 * c + k, j * T:(j + 1) * T],
                                                   x[:, c * CB + j, k * P:(k + 1) * P], ident[0:T, 0:T])
                    last.then_inc(xt_done, 1)

        @block.scalar
        def _(act):
            for c in range(NC):
                for k in range(DC):
                    act.wait_ge(xt_done, c * DC + k + 1)
                    nc.scalar.copy(xt[:, k, c * CT:(c + 1) * CT], ps[:, 2 * c + k, 0:CT]).then_inc(xt_ready, 1)

        @block.vector
        def _(dve):
            ch = Chain(dve, chain)

            def statistics(c):
                for j in range(CB):
                    b = c * CB + j
                    if b % 2 == 0:
                        dve.wait_ge(turned, b // 2 + 1)
                    last = nc.vector.bn_stats(st[:, b, :], token_major(b))
                ch.link(last)
                for b in range(c * CB, c * CB + CB):
                    last = nc.vector.bn_aggr(mv[:, b, :], st[:, b, :])
                ch.link(last)
                nc.vector.tensor_scalar_add(var[:, c * CB:(c + 1) * CB], mv[:, c * CB:(c + 1) * CB, 1], EPS)\
                    .then_inc(var_ready, 1)

            def scale(c):
                dve.wait_ge(rstd_ready, c + 1)
                for b in range(c * CB, c * CB + CB):
                    last = nc.vector.tensor_scalar(x[:, b, :], token_major(b), mv[:, b, 0:1], rstd[:, b:b + 1],
                                                   ALU.subtract, ALU.mult)
                last.then_inc(x_ready, 1)

            for c in range(NC):
                statistics(c)
                if c:
                    scale(c - 1)
            scale(NC - 1)


def stage_switch_routes(nc, xt, ident, sel_v_w, sel_o_w, route_scale, gates, groups, E):
    GR = B * groups
    with Stage(nc, "switchroutes") as s:
        sel_rows = s.sb("sel_rows", [P, D])
        sel = s.sb("sel", [P, DC, P])
        scale = s.sb("scale", [T, 1])
        ramp = s.sb("ramp", [T, E])
        ex = s.sb("ex", [T, GR, E])
        best, second, work = (s.sb(n, [T, GR]) for n in ("best", "second", "work"))
        sel1, sel2 = (s.sb(n, [T, GR, E]) for n in ("sel1", "sel2"))
        ps = s.banks("ps", 5)
        loaded, ramp_ready, sel_turned, sel_ready, logits_done, exped, chain = (
            s.sem(n) for n in ("loaded", "ramp_ready", "sel_turned", "sel_ready", "logits_done", "exped", "chain"))
        block = s.block()

        @block.sync
        def _(sp):
            sp.dma_start(sel_rows[0:P // 2, :], sel_v_w).then_inc(loaded, 16)
            sp.dma_start(sel_rows[P // 2:P, :], sel_o_w).then_inc(loaded, 16)
            sp.dma_start(scale[:], rows(route_scale, T)).then_inc(loaded, 16)

        @block.gpsimd
        def _(pool):
            pool.iota(ramp[:], pattern=[[-1, E]], base=E, channel_multiplier=0,
                      allow_small_or_imprecise_dtypes=True).then_inc(ramp_ready, 1)

        @block.tensor
        def _(pe):
            pe.wait_ge(loaded, 48)
            for k in range(DC):
                last = nc.tensor.transpose(ps[:, 4, k * P:(k + 1) * P], sel_rows[:, k * P:(k + 1) * P], ident[:])
            last.then_inc(sel_turned, 1)
            pe.wait_ge(sel_ready, 1)
            for b in range(B):
                for k in range(DC):
                    last = nc.tensor.matmul(ps[0:T, b // CB, b % CB * P:(b % CB + 1) * P], xt[:, k, b * T:(b + 1) * T],
                                            sel[:, k, :], start=k == 0, stop=k == DC - 1)
                if b % CB == CB - 1:
                    last.then_inc(logits_done, 1)

        @block.scalar
        def _(act):
            act.wait_ge(sel_turned, 1)
            nc.scalar.copy(sel[:].rearrange("p a b -> p (a b)"), ps[:, 4, 0:D]).then_inc(sel_ready, 1)
            n = GR // NC
            for c in range(NC):
                act.wait_ge(logits_done, c + 1)
                nc.scalar.activation(ex[:, c * n:(c + 1) * n, :].rearrange("p a b -> p (a b)"), ps[0:T, c, :], ACT.Exp,
                                     scale=-1.0).then_inc(exped, 1)

        @block.vector
        def _(dve):
            c = Chain(dve, chain)
            dve.wait_ge(ramp_ready, 1)
            dve.wait_ge(loaded, 48)
            dve.wait_ge(exped, NC)
            c.link(nc.vector.tensor_scalar_add(ex[:], ex[:], 1.0))
            c.link(nc.vector.reciprocal(ex[:], ex[:]))
            top_two(nc, c, ramp, ex, best, second, sel1, sel2, work, GR, E)
            c.link(nc.vector.tensor_add(work[:], best[:], second[:]))
            c.link(nc.vector.tensor_scalar_max(work[:], work[:], 1e-9))
            c.link(nc.vector.reciprocal(work[:], work[:]))
            c.link(nc.vector.tensor_scalar(work[:], work[:], scale[:], None, ALU.mult))
            for sel_n, value in ((sel1, best), (sel2, second)):
                c.link(nc.vector.tensor_mul(value[:], value[:], work[:]))
                c.link(nc.vector.tensor_tensor(sel_n[:], sel_n[:], value[:].unsqueeze(2).broadcast_to([T, GR, E]), ALU.mult))
            c.link(nc.vector.tensor_add(gates[:].rearrange("p b (g e) -> p (b g) e", e=E), sel1[:], sel2[:]))


def stage_switch(nc, x, xt, ident, q_w, k_w, v_w, o_w, gates, HS, E, PW):
    SCALE = float(PW) ** -0.5
    EH = E // 2
    with Stage(nc, "switch") as s:
        xh, xl = (s.sb(n, [P, DC, TOK], F32R) for n in ("xh", "xl"))
        v_raw = s.sb("v_raw", [P, DC, E, PW])
        o_raw = s.sb("o_raw", [P, E, D])
        qk_raw = s.sb("qk_raw", [P, 2, D])
        vw = [[s.sb(f"vw{b}{i}", [P, DC, E * PW], F32R) for i in range(2)] for b in range(2)]
        ow = [[s.sb(f"ow{b}{i}", [P, E, D], F32R) for i in range(2)] for b in range(2)]
        qkw = [s.sb(f"qkw{i}", [P, DC, 2 * P], F32R) for i in range(2)]
        qk = s.sb("qk", [P, 2, TOK])
        cth, ctl = (s.sb(n, [P, TOK], F32R) for n in ("cth", "ctl"))
        v = s.sb("v", [T, B, PW])
        vt = s.sb("vt", [T, 2, E, PW])
        gv = s.sb("gv", [T, B, E])
        go = s.sb("go", [T, B, E])
        mx = s.sb("mx", [T, CB])
        sc = s.sb("sc", [T, CB, T])
        pr = s.sb("pr", [T, CB, T])
        pt = s.sb("pt", [T, CB, T])
        rs = s.sb("rs", [T, CB])
        ri = s.sb("ri", [T, CB])
        ps = s.banks("ps", 8)
        VALUES, OUTPUTS, QUERIES, SCORES, TURNED = 0, 2, 4, 6, 7
        names = ("v_loaded", "o_loaded", "qk_loaded", "x_high", "x_low", "vw_high", "vw_low", "ow_high", "ow_low",
                 "qkw_turned", "qkw_high", "qkw_low", "gv_ready", "qk_done", "qk_ready", "values_done", "v_act", "v_dve",
                 "v_ready", "s_done", "mx_ready", "shifted", "exped", "summed", "ri_ready", "go_ready", "t_done",
                 "pt_ready", "c_done", "ct_high", "ct_low", "out_done", "out_step")
        (v_loaded, o_loaded, qk_loaded, x_high, x_low, vw_high, vw_low, ow_high, ow_low, qkw_turned, qkw_high, qkw_low,
         gv_ready, qk_done, qk_ready, values_done, v_act, v_dve, v_ready, s_done, mx_ready, shifted, exped, summed,
         ri_ready, go_ready, t_done, pt_ready, c_done, ct_high, ct_low, out_done, out_step) = (s.sem(n) for n in names)
        block = s.block()

        def over_heads(engine, head, drain):
            head(0, 0, True, False)
            with engine.Fori(0, (HS - 2) // 2) as i:
                head(i * 2 + 1, 1, False, False)
                head(i * 2 + 2, 0, False, False)
            head(HS - 1, 1, False, True)
            drain()

        def chunk_of(h, b):
            c, step = b // CB - 1, b % CB
            return h * NC + c, c % NC, step

        def v_pieces(parity):
            return [(v_raw[:, k].rearrange("p e d -> p (e d)"), vw[parity][0][:, k, :], vw[parity][1][:, k, :])
                    for k in range(DC)]

        def o_pieces(parity):
            return [(o_raw[:, n:n + EH, :], ow[parity][0][:, n:n + EH, :], ow[parity][1][:, n:n + EH, :])
                    for n in (0, EH)]

        V_AT, O_AT, QK_AT = {3: 0, 5: 1}, {7: 0, 9: 1}, 14

        @block.sync
        def _(sp):
            def load_v(h):
                for k in range(DC):
                    sp.dma_start(v_raw[:, k], v_w[ds(h * E, E), k * P:(k + 1) * P, :].rearrange("e p d -> p e d"))\
                        .then_inc(v_loaded, 16)

            def load_qk(h):
                sp.dma_start(qk_raw[:, 0, :], q_w[ds(h * PW, PW)]).then_inc(qk_loaded, 16)
                sp.dma_start(qk_raw[:, 1, :], k_w[ds(h * PW, PW)]).then_inc(qk_loaded, 16)

            def load_o(h):
                sp.dma_start(o_raw[:], o_w[ds(h * E, E)].rearrange("e p d -> p e d")).then_inc(o_loaded, 16)

            load_v(0)
            load_qk(0)
            load_o(0)
            with sp.Fori(1, HS) as h:
                sp.wait_ge(vw_low, h * DC)
                load_v(h)
                sp.wait_ge(qkw_turned, h)
                load_qk(h)
                sp.wait_ge(ow_low, h * 2)
                load_o(h)

        @block.tensor
        def _(pe):
            pe.wait_ge(x_low, NC)

            def turn_weights(h):
                pe.wait_ge(qk_loaded, h * 32 + 32)
                wait(pe, qk_ready, h * NC * 2)
                for k in range(DC):
                    for n in range(2):
                        last = nc.tensor.transpose(ps[:, QUERIES, k * 2 * P + n * P:k * 2 * P + (n + 1) * P],
                                                   qk_raw[:, n, k * P:(k + 1) * P], ident[:])
                last.then_inc(qkw_turned, 1)

            def queries(h, c):
                pe.wait_ge(qkw_low, h + 1)
                for n in range(2):
                    wait(pe, qk_ready, (h * NC + c) * 2 + n - 1)
                    for k in range(DC):
                        last = split_product(nc, ps[:, QUERIES + n, 0:CT], [a[:, k, n * P:(n + 1) * P] for a in qkw],
                                             [a[:, k, c * CT:(c + 1) * CT] for a in (xh, xl)], k == 0, k == DC - 1)
                    last.then_inc(qk_done, 1)

            def values(h, parity, b):
                slot = h * B + b
                if b == 0:
                    pe.wait_ge(vw_low, h * DC + DC)
                for n in range(2):
                    wait(pe, (v_dve, v_act)[n], slot)
                    for k in range(DC):
                        last = split_product(nc, ps[0:T, VALUES + n, :], [a[:, k, b * T:(b + 1) * T] for a in (xh, xl)],
                                             [a[:, k, n * EH * PW:(n + 1) * EH * PW] for a in vw[parity]],
                                             k == 0, k == DC - 1)
                    last.then_inc(values_done, 1)

            def outputs(h, parity, b):
                slot = h * B + b
                if b % CB == 0:
                    pe.wait_ge(ct_low, h * NC + b // CB + 1)
                if b == 0:
                    pe.wait_ge(ow_low, h * 2 + 2)
                for n in range(EH):
                    pe.wait_ge(out_step, slot * E + 2 * n + 2)
                    split_product(nc, ps[0:T, OUTPUTS + n % 2, :], [a[:, b * T:(b + 1) * T] for a in (cth, ctl)],
                                  [a[:, 2 * n:2 * n + 2, :].rearrange("p e d -> p (e d)") for a in ow[parity]])\
                        .then_inc(out_done, 1)

            def attend(chunk, c, step):
                if step == 0:
                    pe.wait_ge(qk_ready, chunk * 2 + 2)
                    wait(pe, shifted, chunk)
                    for j in range(CB):
                        cols = slice((c * CB + j) * T, (c * CB + j + 1) * T)
                        last = nc.tensor.matmul(ps[0:T, SCORES, j * T:(j + 1) * T], qk[:, 0, cols], qk[:, 1, cols],
                                                start=True, stop=True)
                    last.then_inc(s_done, 1)
                elif step == 1:
                    pe.wait_ge(exped, chunk + 1)
                    wait(pe, ct_low, chunk)
                    for j in range(CB):
                        last = nc.tensor.transpose(ps[0:T, TURNED, j * T:(j + 1) * T], pr[:, j, :], ident[0:T, 0:T])
                    last.then_inc(t_done, 1)
                elif step == 2:
                    pe.wait_ge(pt_ready, chunk + 1)
                    pe.wait_ge(v_ready, (chunk + 1) * CB)
                    for j in range(CB):
                        last = nc.tensor.matmul(ps[:, TURNED, j * T:(j + 1) * T], v[:, c * CB + j, :], pt[:, j, :],
                                                start=True, stop=True)
                    last.then_inc(c_done, 1)

            def head(h, parity, first, last):
                for b in range(B):
                    if not first or b >= CB:
                        attend(*chunk_of(h, b))
                    if b == QK_AT and not last:
                        turn_weights(h + 1)
                    if b % CB == 1:
                        queries(h, b // CB)
                    values(h, parity, b)
                    if not first:
                        outputs(h - 1, 1 - parity, b)

            def drain():
                for b in range(B):
                    if b < CB:
                        attend(*chunk_of(HS, b))
                    outputs(HS - 1, 1, b)

            turn_weights(0)
            over_heads(pe, head, drain)

        @block.scalar
        def _(act):
            split_tokens(nc, s, act, None, xt, xh, xl, x_high, x_low)
            act.wait_ge(v_loaded, DC * 16)
            for raw, high, low in v_pieces(0):
                nc.scalar.copy(high, raw).then_inc(vw_high, 1)

            def weights_turned(h):
                act.wait_ge(qkw_turned, h + 1)
                nc.scalar.copy(qkw[0][:].rearrange("p a b -> p (a b)"), ps[:, QUERIES, :]).then_inc(qkw_high, 1)

            def queries(h, c):
                for n in range(2):
                    act.wait_ge(qk_done, (h * NC + c) * 2 + n + 1)
                    nc.scalar.copy(qk[:, n, c * CT:(c + 1) * CT], ps[:, QUERIES + n, 0:CT]).then_inc(qk_ready, 1)

            def values(h, b):
                slot = h * B + b
                if b == 0:
                    act.wait_ge(gv_ready, h + 1)
                act.wait_ge(values_done, slot * 2 + 2)
                wait(act, v_ready, slot - 1)
                for e in range(EH):
                    last = nc.scalar.activation(vt[:, b % 2, EH + e, :], ps[0:T, VALUES + 1, e * PW:(e + 1) * PW], ACT.Copy,
                                                scale=gv[:, b, EH + e:EH + e + 1])
                last.then_inc(v_act, 1)

            def attend(chunk, c, step):
                if step == 0:
                    act.wait_ge(shifted, chunk + 1)
                    wait(act, t_done, chunk)
                    wait(act, summed, chunk)
                    nc.scalar.activation(pr[:], sc[:], ACT.Exp, scale=SCALE).then_inc(exped, 1)
                elif step == 1:
                    act.wait_ge(t_done, chunk + 1)
                    wait(act, c_done, chunk)
                    nc.scalar.copy(pt[:].rearrange("p a b -> p (a b)"), ps[0:T, TURNED, 0:CT]).then_inc(pt_ready, 1)
                elif step == 2:
                    act.wait_ge(c_done, chunk + 1)
                    nc.scalar.copy(cth[:, c * CT:(c + 1) * CT], ps[:, TURNED, 0:CT]).then_inc(ct_high, 1)

            def head(h, parity, first, last):
                for b in range(B):
                    if not first or b >= CB:
                        attend(*chunk_of(h, b))
                    if b == QK_AT and not last:
                        weights_turned(h + 1)
                    if b % CB == 1:
                        queries(h, b // CB)
                    values(h, b)
                    if b in V_AT and not last:
                        if V_AT[b] == 0:
                            act.wait_ge(v_loaded, (h + 2) * DC * 16)
                        raw, high, low = v_pieces(1 - parity)[V_AT[b]]
                        nc.scalar.copy(high, raw).then_inc(vw_high, 1)
                    if b in O_AT:
                        if O_AT[b] == 0:
                            act.wait_ge(o_loaded, h * 16 + 16)
                        raw, high, low = o_pieces(parity)[O_AT[b]]
                        nc.scalar.copy(high, raw).then_inc(ow_high, 1)

            def drain():
                for b in range(CB):
                    attend(*chunk_of(HS, b))

            weights_turned(0)
            over_heads(act, head, drain)

        @block.vector
        def _(dve):
            split_tokens(nc, s, None, dve, xt, xh, xl, x_high, x_low)
            for n, (raw, high, low) in enumerate(v_pieces(0)):
                dve.wait_ge(vw_high, n + 1)
                nc.vector.tensor_sub(low, raw, high.bitcast(F32)).then_inc(vw_low, 1)

            def weights_turned(h):
                dve.wait_ge(qkw_high, h + 1)
                nc.vector.tensor_sub(qkw[1][:].rearrange("p a b -> p (a b)"), ps[:, QUERIES, :],
                                     qkw[0][:].bitcast(F32).rearrange("p a b -> p (a b)")).then_inc(qkw_low, 1)

            def values(h, b):
                slot = h * B + b
                dve.wait_ge(values_done, slot * 2 + 1)
                nc.vector.tensor_tensor(vt[:, b % 2, 0:EH, :], ps[0:T, VALUES, :].rearrange("p (e d) -> p e d", e=EH),
                                        gv[:, b, 0:EH].unsqueeze(2).broadcast_to([T, EH, PW]), ALU.mult).then_inc(v_dve, 1)

            def values_sum(h, b):
                slot = h * B + b
                dve.wait_ge(v_dve, slot + 1)
                dve.wait_ge(v_act, slot + 1)
                nc.vector.reduce_sum(v[:, b, :], vt[:, b % 2].rearrange("p e d -> p d e"), axis=AX.X).then_inc(v_ready, 1)

            def outputs(h, b, pairs):
                slot = h * B + b
                for n in pairs:
                    dve.wait_ge(out_done, slot * EH + n + 1)
                    for i in range(2):
                        e = 2 * n + i
                        dve.wait_ge(out_step, slot * E + e + 4)
                        nc.vector.scalar_tensor_tensor(out=x[:, b, :], in0=ps[0:T, OUTPUTS + n % 2, i * D:(i + 1) * D],
                                                       scalar=go[:, b, e:e + 1], in1=x[:, b, :], op0=ALU.mult,
                                                       op1=ALU.add).then_inc(out_step, 1)

            def attend(chunk, c, step, h):
                if step == 0:
                    dve.wait_ge(s_done, chunk + 1)
                    wait(dve, shifted, chunk)
                    bank = ps[0:T, SCORES, 0:CT].rearrange("p (a b) -> p a b", a=CB)
                    nc.vector.reduce_max(mx[:], bank, axis=AX.X).then_inc(mx_ready, 1)
                    dve.wait_ge(mx_ready, chunk + 1)
                    wait(dve, exped, chunk)
                    nc.vector.tensor_tensor(sc[:], bank, mx[:].unsqueeze(2).broadcast_to([T, CB, T]), ALU.subtract)\
                        .then_inc(shifted, 1)
                elif step == 1:
                    dve.wait_ge(exped, chunk + 1)
                    nc.vector.reduce_sum(rs[:], pr[:], axis=AX.X).then_inc(summed, 1)
                    dve.wait_ge(summed, chunk + 1)
                    nc.vector.reciprocal(ri[:], rs[:]).then_inc(ri_ready, 1)
                    dve.wait_ge(ri_ready, chunk + 1)
                    nc.vector.tensor_tensor(go[:, c * CB:(c + 1) * CB, :],
                                            gates[:, c * CB:(c + 1) * CB, ds((h + HS) * E, E)],
                                            ri[:].unsqueeze(2).broadcast_to([T, CB, E]), ALU.mult).then_inc(go_ready, 1)
                elif step == 2:
                    dve.wait_ge(ct_high, chunk + 1)
                    nc.vector.tensor_sub(ctl[:, c * CT:(c + 1) * CT], ps[:, TURNED, 0:CT],
                                         cth[:, c * CT:(c + 1) * CT].bitcast(F32)).then_inc(ct_low, 1)

            def head(h, parity, first, last):
                wait(dve, v_act, h * B)
                nc.vector.tensor_copy(gv[:], gates[:, :, ds(h * E, E)]).then_inc(gv_ready, 1)
                dve.wait_ge(gv_ready, h + 1)
                for b in range(B):
                    if not first or b >= CB:
                        attend(*chunk_of(h, b), h if b >= CB else h - 1)
                    if b == QK_AT and not last:
                        weights_turned(h + 1)
                    values(h, b)
                    if not first:
                        if b % CB == 0:
                            dve.wait_ge(go_ready, (h - 1) * NC + b // CB + 1)
                        outputs(h - 1, b, (0, 1))
                    values_sum(h, b)
                    if not first:
                        outputs(h - 1, b, (2, 3))
                    if b in V_AT and not last:
                        raw, high, low = v_pieces(1 - parity)[V_AT[b]]
                        dve.wait_ge(vw_high, h * DC + DC + V_AT[b] + 1)
                        nc.vector.tensor_sub(low, raw, high.bitcast(F32)).then_inc(vw_low, 1)
                    if b in O_AT:
                        raw, high, low = o_pieces(parity)[O_AT[b]]
                        dve.wait_ge(ow_high, h * 2 + O_AT[b] + 1)
                        nc.vector.tensor_sub(low, raw, high.bitcast(F32)).then_inc(ow_low, 1)

            def drain():
                for b in range(B):
                    if b < CB:
                        attend(*chunk_of(HS, b), HS - 1)
                    if b % CB == 0:
                        dve.wait_ge(go_ready, (HS - 1) * NC + b // CB + 1)
                    outputs(HS - 1, b, range(EH))

            dve.sem_inc(out_step, 4)
            weights_turned(0)
            over_heads(dve, head, drain)


def stage_final_norm(nc, x, out):
    with Stage(nc, "final") as s:
        half = s.sb("half", [T, B])
        st = s.sb("st", [T, B, 6])
        mv = s.sb("mv", [T, B, 2])
        var = s.sb("var", [T, B])
        rstd = s.sb("rstd", [T, B])
        half_ready, chain, var_ready, rstd_ready, y_ready, stored = (
            s.sem(n) for n in ("half_ready", "chain", "var_ready", "rstd_ready", "y_ready", "stored"))
        block = s.block()

        @block.gpsimd
        def _(pool):
            pool.memset(half[:], -0.5).then_inc(half_ready, 1)
            pool.wait_ge(half_ready, 1)
            for c in range(NC):
                part = slice(c * CB, (c + 1) * CB)
                pool.wait_ge(var_ready, c + 1)
                pool.tensor_tensor(rstd[:, part], var[:, part], half[:, part], ALU.pow).then_inc(rstd_ready, 1)

        @block.vector
        def _(dve):
            ch = Chain(dve, chain)
            for c in range(NC):
                for b in range(c * CB, (c + 1) * CB):
                    last = nc.vector.bn_stats(st[:, b, :], x[:, b, :])
                ch.link(last)
                for b in range(c * CB, (c + 1) * CB):
                    last = nc.vector.bn_aggr(mv[:, b, :], st[:, b, :])
                ch.link(last)
                part = slice(c * CB, (c + 1) * CB)
                nc.vector.tensor_scalar_add(var[:, part], mv[:, part, 1], EPS).then_inc(var_ready, 1)
            for c in range(NC):
                dve.wait_ge(rstd_ready, c + 1)
                for b in range(c * CB, (c + 1) * CB):
                    last = nc.vector.tensor_scalar(x[:, b, :], x[:, b, :], mv[:, b, 0:1], rstd[:, b:b + 1],
                                                   ALU.subtract, ALU.mult)
                last.then_inc(y_ready, 1)

        @block.sync
        def _(sp):
            for c in range(NC):
                part = slice(c * CB, (c + 1) * CB)
                sp.wait_ge(y_ready, c + 1)
                sp.dma_start(out[part].rearrange("b t d -> t b d"), x[:, part, :]).then_inc(stored, 16)
            sp.wait_ge(stored, 16 * NC)


def stage_store(nc, x, out):
    with Stage(nc, "store") as s:
        stored = s.sem("stored")
        block = s.block()

        @block.sync
        def _(sp):
            sp.dma_start(out.rearrange("b t d -> t b d"), x[:]).then_inc(stored, 16)
            sp.wait_ge(stored, 16)


def build(nc, i, out, stages=(1, 2, 3, 4, 5, 6)):
    with Stage(nc, "all") as s:
        x = s.sb("x", [T, B, D])
        xt = s.sb("xt", [P, DC, TOK])
        ident = s.sb("ident", [P, P])
        stage_load(nc, i["x"], x, xt, ident)
        if 1 in stages:
            stage_decay_attention(nc, x, xt, ident, i["L0_attn_Wqkv"], i["L0_attn_bqkv"], i["L0_attn_Wproj"],
                                  i["L0_attn_bproj"], i["L0_attn_gamma"])
        if 2 in stages:
            stage_cross_attention(nc, "cross0", x, xt, ident, i["ctx_1024"],
                                  [i["L0_xattn_W_" + n] for n in "qkvo"], [True] * 4, None,
                                  i["mask_1x1xSxS2_if1"].rearrange("a b s t -> (a b s) t"), False)
        if 3 in stages:
            E, _, HID = i["L0_ffn_w1"].shape
            with Stage(nc, "experts") as f:
                comb_t = f.sb("comb_t", [E + 1, TOK])
                acc = f.sb("acc", [P, DC, TOK])
                stage_moe_routes(nc, x, xt, ident, i["L0_ffn_gate_w"], i["L0_ffn_gate_b"], i["L0_ffn_b2"],
                                 i["L0_ffn_bs2"], comb_t, acc, E)
                stage_moe(nc, x, xt, ident, i["L0_ffn_w1"], i["L0_ffn_b1"], i["L0_ffn_w2"], i["L0_ffn_ws1"],
                          i["L0_ffn_bs1"], i["L0_ffn_ws2"], comb_t, acc, E, HID)
                stage_moe_norm(nc, x, xt, ident, acc)
        if 4 in stages:
            stage_coupled_attention(nc, x, xt, ident, [i["L1_attn_W" + n] for n in "qkvo"],
                                    [i["L1_attn_b" + n] for n in "qkvo"], i["L1_attn_J_attn"],
                                    i["L1_attn_lambda_attn"])
        if 5 in stages:
            kv, kvb = i["L1_xattn_W_kv"], i["L1_xattn_b_kv"]
            stage_cross_attention(nc, "cross1", x, xt, ident, i["ctx_1024"],
                                  [i["L1_xattn_W_q"], kv[:, 0:D], kv[:, D:2 * D], i["L1_xattn_W_o"]], [False] * 4,
                                  [i["L1_xattn_b_q"], kvb[0:D], kvb[D:2 * D], i["L1_xattn_b_o"]],
                                  i["mask_BxS2_bf1"], True)
        if 6 in stages:
            HE, _, PW = i["L1_ffn_v_w"].shape
            HS = i["L1_ffn_q_w"].shape[0] // PW
            E = HE // HS
            with Stage(nc, "switchgates") as f:
                gates = f.sb("gates", [T, B, 2 * HE])
                stage_switch_routes(nc, xt, ident, i["L1_ffn_sel_v_w"], i["L1_ffn_sel_o_w"], i["L1_ffn_route_scale"],
                                    gates, 2 * HS, E)
                stage_switch(nc, x, xt, ident, i["L1_ffn_q_w"], i["L1_ffn_k_w"], i["L1_ffn_v_w"], i["L1_ffn_o_w"],
                             gates, HS, E, PW)
            stage_final_norm(nc, x, out)
        else:
            stage_store(nc, x, out)


_INS = [
    "x", "ctx_1024", "mask_1x1xSxS2_if1", "mask_BxS2_bf1", "L0_attn_Wqkv", "L0_attn_bqkv", "L0_attn_Wproj",
    "L0_attn_bproj", "L0_attn_gamma", "L0_xattn_W_q", "L0_xattn_W_k", "L0_xattn_W_v", "L0_xattn_W_o",
    "L0_ffn_gate_w", "L0_ffn_gate_b", "L0_ffn_w1", "L0_ffn_b1", "L0_ffn_w2", "L0_ffn_b2", "L0_ffn_ws1", "L0_ffn_bs1",
    "L0_ffn_ws2", "L0_ffn_bs2", "L1_attn_Wq", "L1_attn_bq", "L1_attn_Wk", "L1_attn_bk", "L1_attn_Wv", "L1_attn_bv",
    "L1_attn_Wo", "L1_attn_bo", "L1_attn_J_attn", "L1_attn_lambda_attn", "L1_xattn_W_q", "L1_xattn_b_q",
    "L1_xattn_W_kv", "L1_xattn_b_kv", "L1_xattn_W_o", "L1_xattn_b_o", "L1_ffn_q_w", "L1_ffn_k_w", "L1_ffn_v_w",
    "L1_ffn_o_w", "L1_ffn_sel_v_w", "L1_ffn_sel_o_w", "L1_ffn_route_scale",
]


def kernel(**inputs):
    import numpy as _np
    import concourse.bacc as _bacc
    from concourse import mybir as _mybir
    from concourse.bass_utils import run_bass_kernel_spmd as _run

    nc = _bacc.Bacc("TRN2", target_bir_lowering=False, num_devices=1)
    arrays, args = {}, {}
    for name in _INS:
        a = _np.ascontiguousarray(inputs[name])
        a = a.reshape(a.shape or (1,))
        arrays[f"in_{name}_dram"] = a
        args[name] = nc.dram_tensor(f"in_{name}_dram", a.shape, _mybir.dt.from_np(a.dtype), kind="ExternalInput").ap()
    out = nc.dram_tensor("out_0_dram", (B, T, D), F32, kind="ExternalOutput").ap()
    build(nc, args, out)
    r = _run(nc, [arrays], core_ids=[0])
    return r.results[0]["out_0_dram"]
```

```python
from contextlib import ExitStack

import concourse.bass as bass
from concourse import mybir

F32 = mybir.dt.float32
F32R = mybir.dt.float32r
U8 = mybir.dt.uint8
I32 = mybir.dt.int32
ALU = mybir.AluOpType
ACT = mybir.ActivationFunctionType
AX = mybir.AxisListType

B, T, D = 16, 112, 256
TOK = B * T
P = 128
DC = D // P
S2 = 375
KT, KP = 3, 125
CB = 4
NC = B // CB
CT = CB * T
H, HD = 16, 16
EPS = 1e-5
NEG = 4.0e9
ds = bass.ds


class Stage:

    def __init__(self, nc, name):
        self.nc, self.name, self.stack, self.sems = nc, name, ExitStack(), []

    def __enter__(self):
        self.stack.__enter__()
        return self

    def __exit__(self, *error):
        self.stack.__exit__(*error)
        if self.sems:
            self.nc.clear_and_free_semaphores(self.sems)
            self.nc.all_engine_barrier()

    def sb(self, name, shape, dt=F32):
        return self.stack.enter_context(self.nc.sbuf_tensor(f"{self.name}_{name}", shape, dt))

    def dram(self, name, shape, dt=F32):
        return self.nc.dram_tensor(f"{self.name}_{name}", shape, dt).ap()

    def banks(self, name, n):
        return self.stack.enter_context(self.nc.psum_tensor(f"{self.name}_{name}", [P, n, 512], F32))

    def sem(self, name):
        self.sems.append(self.nc.alloc_semaphore(f"{self.name}_{name}"))
        return self.sems[-1]

    def block(self):
        return self.stack.enter_context(self.nc.Block())


class Chain:

    def __init__(self, engine, sem, base=0):
        self.engine, self.sem, self.base, self.n = engine, sem, base, 0

    def link(self, instruction, passed=None):
        self.n += 1
        instruction.then_inc(self.sem, 1)
        if passed is None:
            self.engine.wait_ge(self.sem, self.base + self.n)
        else:
            wait_apart(self.engine, passed, (self.sem, self.base + self.n))


def wait(engine, sem, count):
    if not isinstance(count, int) or count > 0:
        engine.wait_ge(sem, count)


def wait_apart(engine, passed, *waits):
    for sem, count in waits:
        wait(engine, sem, count)
    if not all(isinstance(count, int) for sem, count in waits):
        engine.sem_inc(passed, 1)


def split_product(nc, out, w, x, first=True, last=True):
    nc.tensor.matmul(out, w[0], x[0], start=first, stop=False)
    nc.tensor.matmul(out, w[0], x[1], start=False, stop=False)
    return nc.tensor.matmul(out, w[1], x[0], start=False, stop=last)


def rows(ap, n):
    return ap.rearrange("(a n) -> a n", a=1).broadcast_to([n, ap.shape[0]])


def column(ap, m):
    return ap[m * P:(m + 1) * P].rearrange("(p a) -> p a", a=1)



def stage_load(nc, x_in, x, xt, ident, pairs):
    with Stage(nc, "load") as s:
        ps = s.banks("ps", 4)
        loaded = [s.sem(f"loaded{c}") for c in range(NC)]
        pairs_loaded, ident_zero, ident_ready = s.sem("pairs_loaded"), s.sem("ident_zero"), s.sem("ident_ready")
        transposed, xt_ready = s.sem("transposed"), s.sem("xt_ready")
        block = s.block()

        @block.sync
        def _(sp):
            for c in range(NC):
                part = slice(c * CB, (c + 1) * CB)
                sp.dma_start(x[:, part, :], x_in[part].rearrange("b t d -> t b d")).then_inc(loaded[c], 16)
            for tile, source in pairs:
                sp.dma_start(tile, source).then_inc(pairs_loaded, 16)
            if pairs:
                sp.wait_ge(pairs_loaded, 16 * len(pairs))

        @block.gpsimd
        def _(pool):
            pool.memset(ident[:], 0.0).then_inc(ident_zero, 1)
            pool.wait_ge(ident_zero, 1)
            pool.affine_select(out=ident[:], in_=ident[:], compare_op=ALU.not_equal, fill=1.0, base=0,
                               pattern=[[-1, P]], channel_multiplier=1).then_inc(ident_ready, 1)

        @block.tensor
        def _(pe):
            pe.wait_ge(ident_ready, 1)
            for c in range(NC):
                pe.wait_ge(loaded[c], 16)
                for d in range(DC):
                    n = c * DC + d
                    if n >= 4:
                        pe.wait_ge(xt_ready, n - 3)
                    for j in range(CB):
                        last = nc.tensor.transpose(ps[:, n % 4, j * T:(j + 1) * T],
                                                   x[:, c * CB + j, d * P:(d + 1) * P], ident[0:T, 0:T])
                    last.then_inc(transposed, 1)

        @block.scalar
        def _(act):
            for n in range(NC * DC):
                c, d = n // DC, n % DC
                act.wait_ge(transposed, n + 1)
                nc.scalar.copy(xt[:, d, c * CT:(c + 1) * CT], ps[:, n % 4, 0:CT]).then_inc(xt_ready, 1)


def stage_decay_attention(nc, x, xt, ident, w, wp, qk_bias, v_bias, y_bias, gam):
    with Stage(nc, "decay") as s:
        power = s.sb("power", [T, T])
        mask = s.sb("mask", [T, T])
        half = s.sb("half", [T, CB])
        xs = s.sb("xs", [P, DC, CT])
        qk = s.sb("qk", [P, 4, CT])
        v = s.sb("v", [T, CB, D])
        sc = s.sb("sc", [T, CB, T])
        mx = s.sb("mx", [T, CB])
        e = s.sb("e", [T, CB, T])
        rs = s.sb("rs", [T, CB])
        ri = s.sb("ri", [T, CB])
        pr = s.sb("pr", [T, CB, T])
        pt = s.sb("pt", [T, CB, T])
        o = s.sb("o", [P, DC, CT])
        y = s.sb("y", [T, CB, D])
        st = s.sb("st", [T, CB, 6])
        mv = s.sb("mv", [T, CB, 2])
        var = s.sb("var", [T, CB])
        rstd = s.sb("rstd", [T, CB])
        xn = s.sb("xn", [T, CB, D])
        ps = s.banks("ps", 8)
        act_passed, dve_passed = s.sem("act_passed"), s.sem("dve_passed")
        mask_ready, pool_chain = s.sem("mask_ready"), s.sem("pool_chain")
        half_ready = s.sem("half_ready")
        xs_ready, qk_done, v_done, qk_ready = (s.sem(n) for n in ("xs_ready", "qk_done", "v_done", "qk_ready"))
        chain = s.sem("chain")
        s_done, shifted, exped, normed = s.sem("s_done"), s.sem("shifted"), s.sem("exped"), s.sem("normed")
        t_done, pt_ready, o_done, o_ready = (s.sem(n) for n in ("t_done", "pt_ready", "o_done", "o_ready"))
        y_done, var_ready, rstd_ready, xn_ready = (s.sem(n) for n in ("y_done", "var_ready", "rstd_ready", "xn_ready"))
        xt_done, xt_ready, x_stored = s.sem("xt_done"), s.sem("xt_ready"), s.sem("x_stored")
        block = s.block()
        CHAIN = 12

        def over_chunks(engine, step):
            step(0, True, False)
            with engine.Fori(1, NC - 1) as c:
                step(c, False, False)
            step(NC - 1, False, True)

        @block.gpsimd
        def _(pool):
            c = Chain(pool, pool_chain)
            pool.memset(half[:], -0.5).then_inc(half_ready, 1)
            c.link(pool.iota(power[:], pattern=[[-1, T]], base=0, channel_multiplier=1,
                             allow_small_or_imprecise_dtypes=True))
            c.link(pool.tensor_scalar_max(power[:], power[:], 0.0))
            c.link(pool.tensor_tensor(mask[:], gam[:].broadcast_to([T, T]), power[:], ALU.pow))
            pool.affine_select(out=mask[:], in_=mask[:], compare_op=ALU.is_ge, fill=0.0, base=0,
                               pattern=[[-1, T]], channel_multiplier=1).then_inc(mask_ready, 1)
            with pool.Fori(0, NC) as c:
                pool.wait_ge(var_ready, c + 1)
                pool.tensor_tensor(rstd[:], var[:], half[:], ALU.pow).then_inc(rstd_ready, 1)
                pool.wait_ge(xn_ready, c + 1)
                pool.tensor_copy(x[:, ds(c * CB, CB), :], xn[:]).then_inc(x_stored, 1)

        @block.tensor
        def _(pe):

            def project(c):
                pe.wait_ge(xs_ready, c + 1)
                for m in range(4):
                    for k in range(DC):
                        last = nc.tensor.matmul(ps[:, m, 0:CT], w[:, k, m * P:(m + 1) * P], xs[:, k, :],
                                                start=k == 0, stop=k == DC - 1)
                    last.then_inc(qk_done, 1)
                wait(pe, xt_ready, DC * c - DC)
                if isinstance(c, int) and c == 1:
                    pe.wait_ge(chain, CB)
                for j in range(CB):
                    for k in range(DC):
                        last = nc.tensor.matmul(ps[0:T, 4 + j // 2, (j % 2) * D:(j % 2 + 1) * D],
                                                xs[:, k, j * T:(j + 1) * T], w[:, k, 2 * D:3 * D],
                                                start=k == 0, stop=k == DC - 1)
                last.then_inc(v_done, 1)

            def turn_out(c):
                pe.wait_ge(xn_ready, c + 1)
                for d in range(DC):
                    for j in range(CB):
                        last = nc.tensor.transpose(ps[:, 4 + d, j * T:(j + 1) * T],
                                                   xn[:, j, d * P:(d + 1) * P], ident[0:T, 0:T])
                    last.then_inc(xt_done, 1)

            def step(c, first, last_chunk):
                pe.wait_ge(qk_ready, 4 * c + 4)
                for j in range(CB):
                    for k in range(DC):
                        last = nc.tensor.matmul(ps[0:T, 6, j * T:(j + 1) * T], qk[:, k, j * T:(j + 1) * T],
                                                qk[:, 2 + k, j * T:(j + 1) * T], start=k == 0, stop=k == DC - 1)
                last.then_inc(s_done, 1)
                if not first:
                    turn_out(c - 1)
                if not last_chunk:
                    project(c + 1)
                pe.wait_ge(normed, c + 1)
                for j in range(CB):
                    last = nc.tensor.transpose(ps[0:T, 7, j * T:(j + 1) * T], pr[:, j, :], ident[0:T, 0:T])
                last.then_inc(t_done, 1)
                if not last_chunk:
                    pe.wait_ge(qk_ready, 4 * c + 8)
                pe.wait_ge(pt_ready, c + 1)
                for d in range(DC):
                    for j in range(CB):
                        last = nc.tensor.matmul(ps[:, d, j * T:(j + 1) * T], v[:, j, d * P:(d + 1) * P],
                                                pt[:, j, :], start=True, stop=True)
                    last.then_inc(o_done, 1)
                pe.wait_ge(o_ready, DC * c + DC)
                for j in range(CB):
                    for k in range(DC):
                        last = nc.tensor.matmul(ps[0:T, 2 + j // 2, (j % 2) * D:(j % 2 + 1) * D],
                                                o[:, k, j * T:(j + 1) * T], wp[:, k, :],
                                                start=k == 0, stop=k == DC - 1)
                last.then_inc(y_done, 1)

            project(0)
            over_chunks(pe, step)
            turn_out(NC - 1)

        @block.scalar
        def _(act):

            def queries_keys(c):
                for m in range(4):
                    act.wait_ge(qk_done, 4 * c + m + 1)
                    if m == 0:
                        wait(act, s_done, c)
                    nc.scalar.activation(qk[:, m, :], ps[:, m, 0:CT], ACT.Identity,
                                         bias=qk_bias[:, m:m + 1]).then_inc(qk_ready, 1)

            def store_turned(c):
                for d in range(DC):
                    wait_apart(act, act_passed, (xt_done, DC * c + d + 1))
                    nc.scalar.copy(xt[:, d, ds(c * CT, CT)], ps[:, 4 + d, 0:CT]).then_inc(xt_ready, 1)

            def step(c, first, last_chunk):
                if not last_chunk:
                    wait_apart(act, act_passed, (v_done, c + 1))
                    nc.scalar.copy(xs[:], xt[:, :, ds((c + 1) * CT, CT)]).then_inc(xs_ready, 1)
                if not first:
                    store_turned(c - 1)
                act.wait_ge(shifted, c + 1)
                nc.scalar.activation(e[:], sc[:], ACT.Exp, scale=1.0 / 16.0).then_inc(exped, 1)
                if not last_chunk:
                    queries_keys(c + 1)
                act.wait_ge(t_done, c + 1)
                nc.scalar.copy(pt[:].rearrange("p a b -> p (a b)"), ps[0:T, 7, 0:CT]).then_inc(pt_ready, 1)
                for d in range(DC):
                    act.wait_ge(o_done, DC * c + d + 1)
                    nc.scalar.copy(o[:, d, :], ps[:, d, 0:CT]).then_inc(o_ready, 1)

            nc.scalar.copy(xs[:], xt[:, :, 0:CT]).then_inc(xs_ready, 1)
            queries_keys(0)
            over_chunks(act, step)
            store_turned(NC - 1)

        @block.vector
        def _(dve):

            def values(c, ch):
                dve.wait_ge(v_done, c + 1)
                for j in range(CB):
                    ch.link(nc.vector.tensor_add(v[:, j, :], ps[0:T, 4 + j // 2, (j % 2) * D:(j % 2 + 1) * D], v_bias[:]))

            def step(c, first, last_chunk):
                ch = Chain(dve, chain, CB + c * CHAIN)
                dve.wait_ge(s_done, c + 1)
                ch.link(nc.vector.tensor_tensor(sc[:], ps[0:T, 6, 0:CT].rearrange("p (a b) -> p a b", a=CB),
                                                mask[:].unsqueeze(1).broadcast_to([T, CB, T]), ALU.mult))
                ch.link(nc.vector.reduce_max(mx[:], sc[:], axis=AX.X))
                nc.vector.tensor_tensor(sc[:], sc[:], mx[:].unsqueeze(2).broadcast_to([T, CB, T]),
                                        ALU.subtract).then_inc(shifted, 1)
                dve.wait_ge(exped, c + 1)
                ch.link(nc.vector.reduce_sum(rs[:], e[:], axis=AX.X))
                ch.link(nc.vector.reciprocal(ri[:], rs[:]))
                nc.vector.tensor_tensor(pr[:], e[:], ri[:].unsqueeze(2).broadcast_to([T, CB, T]),
                                        ALU.mult).then_inc(normed, 1)
                ch.link(nc.vector.tensor_tensor(y[:], x[:, ds(c * CB, CB), :],
                                                y_bias[:].unsqueeze(1).broadcast_to([T, CB, D]), ALU.add))
                if not last_chunk:
                    dve.wait_ge(o_done, DC * c + DC)
                    values(c + 1, ch)
                dve.wait_ge(y_done, c + 1)
                ch.link(nc.vector.tensor_add(y[:].rearrange("p (a b) d -> p a (b d)", a=2), ps[0:T, 2:4, :],
                                             y[:].rearrange("p (a b) d -> p a (b d)", a=2)))
                for j in range(CB):
                    last = nc.vector.bn_stats(st[:, j, :], y[:, j, :])
                ch.link(last, dve_passed)
                for j in range(CB):
                    last = nc.vector.bn_aggr(mv[:, j, :], st[:, j, :])
                ch.link(last)
                nc.vector.tensor_scalar_add(var[:], mv[:, :, 1], EPS).then_inc(var_ready, 1)
                dve.wait_ge(rstd_ready, c + 1)
                if not first:
                    dve.wait_ge(xt_done, DC * c)
                for j in range(CB):
                    last = nc.vector.tensor_scalar(xn[:, j, :], y[:, j, :], mv[:, j, 0:1], rstd[:, j:j + 1],
                                                   ALU.subtract, ALU.mult)
                last.then_inc(xn_ready, 1)
                dve.wait_ge(x_stored, c + 1)
                assert ch.n == CHAIN - (CB if last_chunk else 0), ch.n

            values(0, Chain(dve, chain))
            dve.wait_ge(mask_ready, 1)
            dve.wait_ge(half_ready, 1)
            over_chunks(dve, step)


def stage_cross_attention(nc, name, x, xt, ident, ctx, weights, transposed, biases, mask, mask_by_batch):
    with Stage(nc, name) as s:
        QW, KW, VW, OW = range(4)
        wraw = s.sb("wraw", [P, 4, DC, D])
        wt = [s.sb(f"w{n}", [P, DC, D]) for n in range(4)]
        w = [wt[n] if transposed[n] else wraw[:, n] for n in range(4)]
        qk_bias = s.sb("qk_bias", [P, 2, DC])
        v_bias = s.sb("v_bias", [P, D])
        o_bias = s.sb("o_bias", [T, D])
        half = s.sb("half", [T, 1])
        cx_raw = [s.sb(f"cx_raw{i}", [KP, KT, D]) for i in range(2)]
        cx = s.sb("cx", [P, DC, S2])
        PAIR = 2 * HD
        KEYS = S2 + S2 % 2
        ks = s.sb("ks", [P, 2 * DC, S2], F32R)
        qs = s.sb("qs", [P, 2 * DC, T], F32R)
        k_dram = [s.dram(f"k_dram{b}", [2 * D, S2]) for b in range(2)]
        q_dram = [s.dram(f"q_dram{b}", [2 * D, T]) for b in range(2)]
        kk = [s.sb(f"k{b}", [3 * PAIR, H // 2, KEYS], F32R) for b in range(2)]
        q = [s.sb(f"q{b}", [3 * PAIR, H // 2, 2, T], F32R) for b in range(2)]
        vv = [s.sb(f"v{b}", [KP, KT, H, 32]) for b in range(2)]
        mask_raw = [s.sb(f"mask_raw{i}", [T, S2], U8 if mask_by_batch else I32) for i in range(2)]
        masked = [s.sb(f"masked{i}", [T, S2]) for i in range(2)]
        NB = 8
        sc = s.sb("sc", [T, NB, S2])
        mn = [s.sb(f"mn{b}", [T, H]) for b in range(2)]
        pr = s.sb("pr", [T, NB, S2])
        rs = [s.sb(f"rs{b}", [T, H]) for b in range(2)]
        pt = s.sb("pt", [KP, NB, KT * T])
        osb = s.sb("osb", [P, 4 * T])
        ri = s.sb("ri", [T, H])
        otok = s.sb("otok", [T, H, HD])
        o = s.sb("o", [P, DC, T])
        y = s.sb("y", [T, D])
        st = s.sb("st", [T, 6])
        mv = s.sb("mv", [T, 2])
        var = s.sb("var", [T, 1])
        rstd = s.sb("rstd", [T, 1])
        xn = s.sb("xn", [T, D])
        ps = s.banks("ps", 8)
        FRONT, SCORES, TURNED, OUT, TAIL = 0, 2, 4, 6, 7

        dve_passed, sp_passed, pool_passed = s.sem("dve_passed"), s.sem("sp_passed"), s.sem("pool_passed")
        w_loaded, const_loaded, w_turned, w_ready = (s.sem(n) for n in ("w_loaded", "const_loaded", "w_turned", "w_ready"))
        const_ready, mask_ready, v_zero = (s.sem(n) for n in ("const_ready", "mask_ready", "v_zero"))
        mask_loaded = [s.sem(f"mask_loaded{i}") for i in range(2)]
        ctx_loaded = [s.sem(f"ctx_loaded{i}") for i in range(2)]
        f_done, f_act, f_dve, stack_zero = (s.sem(n) for n in ("f_done", "f_act", "f_dve", "stack_zero"))
        q_stored, k_stored = s.sem("q_stored"), s.sem("k_stored")
        q_stacked, k_stacked = s.sem("q_stacked"), s.sem("k_stacked")
        x_stored = s.sem("x_stored")
        s_done, s_max, exped, t_done = (s.sem(n) for n in ("s_done", "s_max", "exped", "t_done"))
        pt_act, pt_dve, pv_done = (s.sem(n) for n in ("pt_act", "pt_dve", "pv_done"))
        o_read, t1_done, otok_ready, t2_done = (s.sem(n) for n in ("o_read", "t1_done", "otok_ready", "t2_done"))
        o_ready, y_done, var_ready, rstd_ready = (s.sem(n) for n in ("o_ready", "y_done", "var_ready", "rstd_ready"))
        xn_ready, xt_done, xt_ready, chain = (s.sem(n) for n in ("xn_ready", "xt_done", "xt_ready", "chain"))
        CHAIN = 5
        UNITS, ACT_UNITS, DVE_UNITS = 6, 5, 4
        TL, EL, VL = 3, 3, 5
        Q_PARTS, K_PARTS = 6, 3
        block = s.block()

        def over_batches(engine, batch):
            batch(0, 0, True, False)
            with engine.Fori(0, (B - 2) // 2) as i:
                batch(i * 2 + 1, 1, False, False)
                batch(i * 2 + 2, 0, False, False)
            batch(B - 1, 1, False, True)

        def wait_front_read(engine, b, u):
            if u < 0:
                b, u = b - 1, u + UNITS
            if isinstance(b, int) and b < 0:
                return
            if u < 2:
                engine.wait_ge(f_act, b * ACT_UNITS + u + 1)
            else:
                engine.wait_ge(f_dve, b * DVE_UNITS + u - 1)

        def wait_turned_read(engine, b, h):
            if h < 0:
                b, h = b - 1, h + H
            if isinstance(b, int) and b < 0:
                return
            engine.wait_ge(pt_act if h % 2 == 1 else pt_dve, b * (H // 2) + h // 2 + 1)

        @block.sync
        def _(sp):
            def load(b, parity):
                wait_apart(sp, sp_passed, (f_done, b * UNITS - 2 * UNITS + DC))
                sp.dma_start(cx_raw[parity][:], ctx[ds(b, 1)].rearrange("a (k p) d -> p (a k) d", p=KP))\
                  .then_inc(ctx_loaded[parity], 16)
                if mask_by_batch:
                    wait_apart(sp, sp_passed, (mask_ready, b - 1))
                    sp.dma_start(mask_raw[parity][:], mask[ds(b, 1)].broadcast_to([T, S2]))\
                      .then_inc(mask_loaded[parity], 16)

            def stack(b, parity):
                wait_apart(sp, sp_passed, (f_dve, b * DVE_UNITS + 1))
                wait_apart(sp, sp_passed, (q_stacked, (b - 1) * Q_PARTS * 16))
                sp.dma_start(q_dram[parity][:].rearrange("(c p) t -> p c t", p=P), qs[:].bitcast(F32))\
                    .then_inc(q_stored, 16)
                wait_apart(sp, sp_passed, (f_dve, b * DVE_UNITS + 3))
                wait_apart(sp, sp_passed, (k_stacked, (b - 1) * K_PARTS * 16))
                sp.dma_start(k_dram[parity][:].rearrange("(c p) s -> p c s", p=P), ks[:].bitcast(F32))\
                    .then_inc(k_stored, 16)
                wait_apart(sp, sp_passed, (q_stored, (b + 1) * 16))
                wait_apart(sp, sp_passed, (s_done, (b - 1) * H))
                if isinstance(b, int) and b < 2:
                    sp.wait_ge(stack_zero, 1)
                for part, source in enumerate((0, 0, D)):
                    for i in range(2):
                        r = part * PAIR + i * HD
                        sp.dma_start(q[parity][r:r + HD, :, i, :].bitcast(F32),
                                     q_dram[parity][source:source + D, :]
                                     .rearrange("(j i d) t -> i d j t", i=2, d=HD)[i]).then_inc(q_stacked, 16)
                wait_apart(sp, sp_passed, (k_stored, (b + 1) * 16))
                for part, source in enumerate((0, D, 0)):
                    sp.dma_start(kk[parity][part * PAIR:(part + 1) * PAIR, :, 0:S2].bitcast(F32),
                                 k_dram[parity][source:source + D, :].rearrange("(j r) s -> r j s", r=PAIR))\
                        .then_inc(k_stacked, 16)

            load(0, 0)
            for n in range(4):
                sp.dma_start(wraw[:, n], weights[n].rearrange("(c p) n -> p c n", p=P)).then_inc(w_loaded, 16)
            if biases:
                for n in range(2):
                    for m in range(DC):
                        sp.dma_start(qk_bias[:, n, m:m + 1], column(biases[n], m)).then_inc(const_loaded, 16)
                sp.dma_start(v_bias[:], rows(biases[2], P)).then_inc(const_loaded, 16)
                sp.dma_start(o_bias[:], rows(biases[3], T)).then_inc(const_loaded, 16)
            if not mask_by_batch:
                sp.dma_start(mask_raw[0][:], mask).then_inc(mask_loaded[0], 16)
            load(1, 1)
            stack(0, 0)
            load(2, 0)
            with sp.Fori(0, (B - 4) // 2) as i:
                stack(i * 2 + 1, 1)
                load(i * 2 + 3, 1)
                stack(i * 2 + 2, 0)
                load(i * 2 + 4, 0)
            stack(B - 3, 1)
            load(B - 1, 1)
            stack(B - 2, 0)
            stack(B - 1, 1)

        @block.gpsimd
        def _(pool):
            for b in range(2):
                pool.memset(q[b][:].bitcast(F32), 0.0)
                last = pool.memset(kk[b][:, :, S2:].bitcast(F32), 0.0)
            last.then_inc(stack_zero, 1)
            for b in range(2):
                last = pool.memset(vv[b][:], 0.0)
            last.then_inc(v_zero, 1)
            if not biases:
                pool.memset(qk_bias[:], 0.0)
                pool.memset(v_bias[:], 0.0)
                pool.memset(o_bias[:], 0.0)
            pool.memset(half[:], -0.5).then_inc(const_ready, 1)

            def convert_mask(b, parity):
                wait_apart(pool, pool_passed, (mask_loaded[parity], (b - parity) * 8 + 16), (s_max, (b - 1) * H))
                pool.tensor_scalar(masked[parity][:], mask_raw[parity][:], -1.0, NEG * 1e20, ALU.add, ALU.mult)\
                    .then_inc(mask_ready, 1)

            if mask_by_batch:
                convert_mask(0, 0)

            def batch(b, parity, first, last):
                if mask_by_batch and not last:
                    convert_mask(b + 1, 1 - parity)
                if not first:
                    normalise(b - 1)

            def normalise(b):
                pool.wait_ge(var_ready, b + 1)
                pool.tensor_tensor(rstd[:], var[:], half[:], ALU.pow).then_inc(rstd_ready, 1)
                pool.wait_ge(xn_ready, b + 1)
                pool.tensor_copy(x[:, ds(b, 1), :], xn[:].unsqueeze(1)).then_inc(x_stored, 1)

            over_batches(pool, batch)
            normalise(B - 1)

        @block.tensor
        def _(pe):
            pe.wait_ge(w_loaded, 16 * 4)
            for n in range(4):
                if transposed[n]:
                    for k in range(DC):
                        for m in range(DC):
                            last = nc.tensor.transpose(ps[:, n, k * D + m * P:k * D + (m + 1) * P],
                                                       wraw[:, n, m, k * P:(k + 1) * P], ident[:])
                    last.then_inc(w_turned, 1)
            pe.wait_ge(w_ready, sum(transposed))

            def front(b, parity, u):
                bank = ps[:, FRONT + u % 2, :]
                wait_front_read(pe, b, u - 2)
                if u < 2:
                    if u == 0:
                        pe.wait_ge(ctx_loaded[parity], (b - parity) * 8 + 16)
                    for t in range(KT):
                        last = nc.tensor.transpose(bank[:, t * KP:(t + 1) * KP],
                                                   cx_raw[parity][:, t, u * P:(u + 1) * P], ident[0:KP, 0:KP])
                elif u in (2, 5):
                    if u == 2:
                        wait_front_read(pe, b, 1)
                    for t in (2,) if u == 2 else (0, 1):
                        for k in range(DC):
                            last = nc.tensor.matmul(bank[0:KP, t % 2 * D:(t % 2 + 1) * D],
                                                    cx[:, k, t * KP:(t + 1) * KP], w[VW][:, k, :],
                                                    start=k == 0, stop=k == DC - 1)
                    if u == 2:
                        for m in range(DC):
                            for k in range(DC):
                                last = nc.tensor.matmul(bank[:, D + m * T:D + (m + 1) * T],
                                                        w[QW][:, k, m * P:(m + 1) * P], xt[:, k, ds(b * T, T)],
                                                        start=k == 0, stop=k == DC - 1)
                else:
                    for k in range(DC):
                        last = nc.tensor.matmul(bank[:, 0:S2], w[KW][:, k, (u - 3) * P:(u - 2) * P], cx[:, k, :],
                                                start=k == 0, stop=k == DC - 1)
                last.then_inc(f_done, 1)

            def scores(b, parity, h):
                if h == 0:
                    wait_front_read(pe, b, UNITS - 1)
                    pe.wait_ge(q_stacked, (b + 1) * Q_PARTS * 16)
                    pe.wait_ge(k_stacked, (b + 1) * K_PARTS * 16)
                wait(pe, s_max, b * H + h - 1)
                nc.tensor.matmul(ps[0:T, SCORES + h % 2, 0:KEYS], q[parity][:, h // 2, h % 2, :],
                                 kk[parity][:, h // 2, :], start=True, stop=True).then_inc(s_done, 1)

            def turn(b, h):
                pe.wait_ge(exped, b * H + h + 1)
                wait_turned_read(pe, b, h - 2)
                for t in range(KT):
                    last = nc.tensor.transpose(ps[0:KP, TURNED + h % 2, t * T:(t + 1) * T],
                                               pr[:, h % NB, t * KP:(t + 1) * KP], ident[0:T, 0:T])
                last.then_inc(t_done, 1)

            def values(b, parity, h):
                wait_turned_read(pe, b, h)
                if h == 0:
                    wait(pe, o_read, b)
                r = h % 4 * 32
                for t in range(KT):
                    last = nc.tensor.matmul(ps[r:r + 32, OUT, h // 4 * T:(h // 4 + 1) * T], vv[parity][:, t, h, :],
                                            pt[:, h % NB, t * T:(t + 1) * T], start=t == 0, stop=t == KT - 1)
                last.then_inc(pv_done, 1)

            def tail(b, part):
                if part == 0:
                    pe.wait_ge(o_read, b + 1)
                    for g in range(4):
                        last = nc.tensor.transpose(ps[0:T, TAIL, g * P:(g + 1) * P], osb[:, g * T:(g + 1) * T], ident[:])
                    last.then_inc(t1_done, 1)
                elif part == 1:
                    pe.wait_ge(otok_ready, b + 1)
                    for k in range(DC):
                        last = nc.tensor.transpose(ps[:, TAIL, k * T:(k + 1) * T],
                                                   otok[:, k * 8:(k + 1) * 8, :].rearrange("p a b -> p (a b)"), ident[0:T, 0:T])
                    last.then_inc(t2_done, 1)
                elif part == 2:
                    pe.wait_ge(o_ready, b + 1)
                    for k in range(DC):
                        last = nc.tensor.matmul(ps[0:T, TAIL, 0:D], o[:, k, :], w[OW][:, k, :],
                                                start=k == 0, stop=k == DC - 1)
                    last.then_inc(y_done, 1)
                else:
                    pe.wait_ge(xn_ready, b + 1)
                    for k in range(DC):
                        last = nc.tensor.transpose(ps[:, TAIL, k * T:(k + 1) * T], xn[:, k * P:(k + 1) * P], ident[0:T, 0:T])
                    last.then_inc(xt_done, 1)

            TAIL_AT = {6: 0, 8: 1, 10: 2, 14: 3}
            FRONT_AT = {0: 0, 1: 1, 4: 2, 5: 3, 7: 4, 10: 5}

            def batch(b, parity, first, last):
                for i in range(H):
                    scores(b, parity, i)
                    if i >= TL:
                        turn(b, i - TL)
                    elif not first:
                        turn(b - 1, i - TL + H)
                    if not last and i in FRONT_AT:
                        front(b + 1, 1 - parity, FRONT_AT[i])
                    if not first and i in TAIL_AT:
                        tail(b - 1, TAIL_AT[i])
                    if i >= VL:
                        values(b, parity, i - VL)
                    elif not first:
                        values(b - 1, 1 - parity, i - VL + H)

            for u in range(UNITS):
                front(0, 0, u)
            over_batches(pe, batch)
            for h in range(H - TL, H):
                turn(B - 1, h)
            for h in range(H - VL, H):
                values(B - 1, 1, h)
            for part in range(4):
                tail(B - 1, part)

        @block.scalar
        def _(act):
            turned = [n for n in range(4) if transposed[n]]
            for i, n in enumerate(turned):
                act.wait_ge(w_turned, i + 1)
                nc.scalar.copy(w[n][:].rearrange("p a b -> p (a b)"), ps[:, n, :]).then_inc(w_ready, 1)
            if biases:
                act.wait_ge(const_loaded, 16 * 6)
            act.wait_ge(const_ready, 1)

            def front(b, parity, u):
                act.wait_ge(f_done, b * UNITS + u + 1)
                bank = ps[:, FRONT + u % 2, :]
                if u < 2:
                    nc.scalar.copy(cx[:, u, :], bank[:, 0:S2]).then_inc(f_act, 1)
                elif u == 2:
                    wait(act, q_stored, b * 16)
                    for m in range(DC):
                        last = nc.scalar.activation(qs[:, m, :], bank[:, D + m * T:D + (m + 1) * T], ACT.Identity,
                                                    bias=qk_bias[:, 0, m:m + 1])
                    last.then_inc(f_act, 1)
                else:
                    wait(act, k_stored, b * 16)
                    nc.scalar.activation(ks[:, u - 3, :], bank[:, 0:S2], ACT.Identity,
                                         bias=qk_bias[:, 1, u - 3:u - 2]).then_inc(f_act, 1)

            def exponent(b, parity, h):
                act.wait_ge(s_max, b * H + h + 1)
                wait(act, t_done, b * H + h - NB + 1)
                nc.scalar.activation(pr[:, h % NB, :], sc[:, h % NB, :], ACT.Exp, bias=mn[parity][:, h:h + 1],
                                     scale=-1.0, accum_out=rs[parity][:, h:h + 1]).then_inc(exped, 1)

            def evacuate(b, h):
                act.wait_ge(t_done, b * H + h + 1)
                wait(act, pv_done, b * H + h - NB + 1)
                nc.scalar.copy(pt[:, h % NB, :], ps[0:KP, TURNED + h % 2, 0:KT * T]).then_inc(pt_act, 1)

            def tail(b, part):
                if part == 0:
                    act.wait_ge(pv_done, b * H + H)
                    wait(act, t1_done, b)
                    nc.scalar.copy(osb[:], ps[:, OUT, 0:4 * T]).then_inc(o_read, 1)
                elif part == 1:
                    act.wait_ge(t2_done, b + 1)
                    nc.scalar.copy(o[:].rearrange("p a b -> p (a b)"), ps[:, TAIL, 0:DC * T]).then_inc(o_ready, 1)
                else:
                    act.wait_ge(xt_done, b + 1)
                    nc.scalar.copy(xt[:, :, ds(b * T, T)], ps[:, TAIL, 0:DC * T].rearrange("p (a b) -> p a b", a=DC))\
                        .then_inc(xt_ready, 1)

            TAIL_AT = {5: 0, 9: 1, 15: 2}
            FRONT_AT = {0: 0, 1: 1, 4: 2, 5: 3, 7: 4}

            def batch(b, parity, first, last):
                for i in range(H):
                    if not first and TAIL_AT.get(i) == 0:
                        tail(b - 1, 0)
                    if (i - EL) % 2 == 1:
                        if i >= EL:
                            evacuate(b, i - EL)
                        elif not first:
                            evacuate(b - 1, i - EL + H)
                    exponent(b, parity, i)
                    if not last and i in FRONT_AT:
                        front(b + 1, 1 - parity, FRONT_AT[i])
                    if not first and TAIL_AT.get(i, 0) > 0:
                        tail(b - 1, TAIL_AT[i])

            for u in range(ACT_UNITS):
                front(0, 0, u)
            over_batches(act, batch)
            for h in range(H - EL, H):
                if h % 2 == 1:
                    evacuate(B - 1, h)
            for part in range(3):
                tail(B - 1, part)

        @block.vector
        def _(dve):
            pre = Chain(dve, chain)
            dve.wait_ge(const_ready, 1)
            if biases:
                dve.wait_ge(const_loaded, 16 * 6)
            dve.wait_ge(v_zero, 1)
            if not mask_by_batch:
                dve.wait_ge(mask_loaded[0], 16)
                pre.link(nc.vector.tensor_scalar(masked[0][:], mask_raw[0][:], 0, NEG, ALU.not_equal, ALU.mult))
                pre.link(nc.vector.tensor_scalar_add(masked[0][:], masked[0][:], -NEG))
            before = pre.n

            def front(b, parity, u):
                if u == 5:
                    dve.wait_ge(f_done, b * UNITS + u + 1)
                else:
                    dve.wait_ge(f_act, b * ACT_UNITS + u + 1)
                bank = ps[:, FRONT + u % 2, :]
                if u == 2:
                    for m in range(DC):
                        nc.vector.scalar_tensor_tensor(out=qs[:, DC + m, :], in0=bank[:, D + m * T:D + (m + 1) * T],
                                                       scalar=qk_bias[:, 0, m:m + 1], in1=qs[:, m, :].bitcast(F32),
                                                       op0=ALU.add, op1=ALU.subtract)
                if u in (2, 5):
                    wait(dve, pv_done, (b - 1) * H)
                    for t in (2,) if u == 2 else (0, 1):
                        last = nc.vector.tensor_add(vv[parity][:, t, :, 0:HD],
                                                    bank[0:KP, t % 2 * D:(t % 2 + 1) * D]
                                                    .rearrange("p (h d) -> p h d", d=HD),
                                                    v_bias[0:KP].rearrange("p (h d) -> p h d", d=HD))
                else:
                    last = nc.vector.scalar_tensor_tensor(out=ks[:, DC + u - 3, :], in0=bank[:, 0:S2],
                                                          scalar=qk_bias[:, 1, u - 3:u - 2],
                                                          in1=ks[:, u - 3, :].bitcast(F32),
                                                          op0=ALU.add, op1=ALU.subtract)
                last.then_inc(f_dve, 1)

            def maximum(b, parity, h):
                wait_apart(dve, dve_passed, (s_done, b * H + h + 1), (exped, b * H + h - NB + 1))
                mask_of = masked[parity if mask_by_batch else 0]
                nc.vector.tensor_tensor_reduce(out=sc[:, h % NB, :], in0=ps[0:T, SCORES + h % 2, 0:S2], in1=mask_of[:],
                                               scale=-0.25, scalar=3e38, op0=ALU.add, op1=ALU.min,
                                               accum_out=mn[parity][:, h:h + 1]).then_inc(s_max, 1)

            def evacuate(b, h):
                dve.wait_ge(t_done, b * H + h + 1)
                wait(dve, pv_done, b * H + h - NB + 1)
                nc.vector.tensor_copy(pt[:, h % NB, :], ps[0:KP, TURNED + h % 2, 0:KT * T]).then_inc(pt_dve, 1)

            def tail(b, parity, part, ch):
                if part == 0:
                    dve.wait_ge(exped, b * H + H)
                    ch.link(nc.vector.reciprocal(ri[:], rs[parity][:]))
                    dve.wait_ge(t1_done, b + 1)
                    nc.vector.tensor_tensor(otok[:], ps[0:T, TAIL, :].rearrange("p (h e) -> p h e", e=32)[:, :, 0:HD],
                                            ri[:].unsqueeze(2).broadcast_to([T, H, HD]), ALU.mult).then_inc(otok_ready, 1)
                elif part == 1:
                    ch.link(nc.vector.tensor_add(y[:].unsqueeze(1), x[:, ds(b, 1), :], o_bias[:].unsqueeze(1)))
                    dve.wait_ge(y_done, b + 1)
                    ch.link(nc.vector.tensor_add(y[:], ps[0:T, TAIL, 0:D], y[:]))
                    ch.link(nc.vector.bn_stats(st[:], y[:]), dve_passed)
                    ch.link(nc.vector.bn_aggr(mv[:], st[:]))
                    nc.vector.tensor_scalar_add(var[:], mv[:, 1:2], EPS).then_inc(var_ready, 1)
                else:
                    dve.wait_ge(rstd_ready, b + 1)
                    wait(dve, x_stored, b)
                    nc.vector.tensor_scalar(xn[:], y[:], mv[:, 0:1], rstd[:], ALU.subtract, ALU.mult).then_inc(xn_ready, 1)

            TAIL_AT = {7: 0, 11: 1, 13: 2}
            FRONT_AT = {5: 2, 6: 3, 8: 4, 10: 5}

            def batch(b, parity, first, last):
                ch = Chain(dve, chain, before if first else before + (b - 1) * CHAIN)
                for i in range(H):
                    if mask_by_batch and i == 0:
                        dve.wait_ge(mask_ready, b + 1)
                    maximum(b, parity, i)
                    if not last and i in FRONT_AT:
                        front(b + 1, 1 - parity, FRONT_AT[i])
                    if not first and i in TAIL_AT:
                        tail(b - 1, 1 - parity, TAIL_AT[i], ch)
                    if (i - EL) % 2 == 0:
                        if i >= EL:
                            evacuate(b, i - EL)
                        elif not first:
                            evacuate(b - 1, i - EL + H)
                assert ch.n == (0 if first else CHAIN), ch.n

            for u in range(2, UNITS):
                front(0, 0, u)
            over_batches(dve, batch)
            for h in range(H - EL, H):
                if h % 2 == 0:
                    evacuate(B - 1, h)
            ch = Chain(dve, chain, before + (B - 1) * CHAIN)
            for part in range(3):
                tail(B - 1, 1, part, ch)


def stage_coupled_attention(nc, x, xt, ident, weights, biases, J, lam):
    with Stage(nc, "coupled") as s:
        QW, KW, VW, OW = range(4)
        GH = 4
        G = H // GH
        HP = P // HD
        wraw = s.sb("wraw", [P, 4, DC, D])
        w = [s.sb(f"w{n}", [P, DC, D]) for n in range(4)]
        qk_bias = s.sb("qk_bias", [P, 2, DC])
        v_bias = s.sb("v_bias", [T, D])
        o_bias = s.sb("o_bias", [T, D])
        Jd = s.sb("Jd", [P, DC, P])
        lam4 = s.sb("lam4", [P, 1])
        head_mask = s.sb("head_mask", [P, HP])
        half = s.sb("half", [T, 1])
        xs = s.sb("xs", [P, DC, T])
        k32 = s.sb("k32", [P, DC, T])
        qn = s.sb("qn", [P, DC, T])
        q = [s.sb(f"q{b}", [P, DC, T]) for b in range(2)]
        qj = [s.sb(f"qj{b}", [P, DC, T]) for b in range(2)]
        km = [s.sb(f"km{b}", [P, DC, HP, T]) for b in range(2)]
        knm = [s.sb(f"knm{b}", [P, DC, HP, T]) for b in range(2)]
        vv = [s.sb(f"v{b}", [T, H, 32]) for b in range(2)]
        NB = 2
        sc = s.sb("sc", [T, NB, GH, T])
        mx = s.sb("mx", [T, NB, GH])
        pr = s.sb("pr", [T, NB, GH, T])
        rs = [s.sb(f"rs{b}", [T, H]) for b in range(2)]
        pt = s.sb("pt", [T, NB, GH, T])
        osb = s.sb("osb", [P, 4 * T])
        ri = s.sb("ri", [T, H])
        otok = s.sb("otok", [T, H, HD])
        o = s.sb("o", [P, DC, T])
        y = s.sb("y", [T, D])
        st = s.sb("st", [T, 6])
        mv = s.sb("mv", [T, 2])
        var = s.sb("var", [T, 1])
        rstd = s.sb("rstd", [T, 1])
        xn = s.sb("xn", [T, D])
        ps = s.banks("ps", 8)
        FRONT, SCORES, TURNED, OUT, TAIL = 0, 2, 4, 6, 7

        dve_passed, w_loaded, J_loaded = s.sem("dve_passed"), s.sem("w_loaded"), s.sem("J_loaded")
        const_loaded, w_turned, w_ready, J_zero = (s.sem(n) for n in ("const_loaded", "w_turned", "w_ready", "J_zero"))
        pool_chain, const_ready, v_zero, x_stored = (s.sem(n) for n in ("pool_chain", "const_ready", "v_zero", "x_stored"))
        xs_ready, qk_done, v_done, j_done = (s.sem(n) for n in ("xs_ready", "qk_done", "v_done", "j_done"))
        qk_ready, tanh_ready, v_ready, qj_ready, k_ready = (s.sem(n) for n in ("qk_ready", "tanh_ready", "v_ready", "qj_ready", "k_ready"))
        s_done, shifted, exped, summed, t_done, pt_ready, pv_done = (
            s.sem(n) for n in ("s_done", "shifted", "exped", "summed", "t_done", "pt_ready", "pv_done"))
        o_read, t1_done, otok_ready, t2_done = (s.sem(n) for n in ("o_read", "t1_done", "otok_ready", "t2_done"))
        o_ready, y_done, var_ready, rstd_ready = (s.sem(n) for n in ("o_ready", "y_done", "var_ready", "rstd_ready"))
        xn_ready, xt_done, xt_ready, chain = (s.sem(n) for n in ("xn_ready", "xt_done", "xt_ready", "chain"))
        CHAIN = G + 5
        LOADS = 2 * DC + 3
        block = s.block()

        def over_batches(engine, batch):
            batch(0, 0, 0, False)
            batch(1, 1, 1, False)
            with engine.Fori(0, (B - 4) // 2) as i:
                batch(i * 2 + 2, 0, 2, False)
                batch(i * 2 + 3, 1, 2, False)
            batch(B - 2, 0, 2, False)
            batch(B - 1, 1, 2, True)

        @block.sync
        def _(sp):
            for n in range(4):
                sp.dma_start(wraw[:, n], weights[n].rearrange("(c p) n -> p c n", p=P)).then_inc(w_loaded, 16)
            for n in range(2):
                for m in range(DC):
                    sp.dma_start(qk_bias[:, n, m:m + 1], column(biases[n], m)).then_inc(const_loaded, 16)
            sp.dma_start(v_bias[:], rows(biases[2], T)).then_inc(const_loaded, 16)
            sp.dma_start(o_bias[:], rows(biases[3], T)).then_inc(const_loaded, 16)
            sp.dma_start(lam4[:], rows(lam, P)).then_inc(const_loaded, 16)
            sp.wait_ge(J_zero, 1)
            for h in range(H):
                r = h % HP * HD
                sp.dma_start(Jd[r:r + HD, h // HP, r:r + HD], J[h]).then_inc(J_loaded, 16)

        @block.gpsimd
        def _(pool):
            c = Chain(pool, pool_chain)
            pool.memset(Jd[:], 0.0).then_inc(J_zero, 1)
            pool.memset(half[:], -0.5)
            for b in range(2):
                last = pool.memset(vv[b][:], 0.0)
            last.then_inc(v_zero, 1)
            c.link(pool.memset(head_mask[:], 1.0))
            c.link(pool.affine_select(out=head_mask[:], in_=head_mask[:], compare_op=ALU.is_ge, fill=0.0, base=0,
                                      pattern=[[-HD, HP]], channel_multiplier=1))
            pool.affine_select(out=head_mask[:], in_=head_mask[:], compare_op=ALU.is_ge, fill=0.0, base=HD - 1,
                               pattern=[[HD, HP]], channel_multiplier=-1).then_inc(const_ready, 1)

            def normalise(b):
                pool.wait_ge(var_ready, b + 1)
                pool.tensor_tensor(rstd[:], var[:], half[:], ALU.pow).then_inc(rstd_ready, 1)
                pool.wait_ge(xn_ready, b + 1)
                pool.tensor_copy(x[:, ds(b, 1), :], xn[:].unsqueeze(1)).then_inc(x_stored, 1)

            def batch(b, parity, before, last):
                if before:
                    normalise(b - 1)

            over_batches(pool, batch)
            normalise(B - 1)

        @block.tensor
        def _(pe):
            pe.wait_ge(w_loaded, 16 * 4)
            for n in range(4):
                for k in range(DC):
                    for m in range(DC):
                        last = nc.tensor.transpose(ps[:, n, k * D + m * P:k * D + (m + 1) * P],
                                                   wraw[:, n, m, k * P:(k + 1) * P], ident[:])
                last.then_inc(w_turned, 1)
            pe.wait_ge(w_ready, 4)

            def front(b, parity, u, which=(0, 1)):
                bank = ps[:, FRONT + u % 2, :]
                if u == 0:
                    pe.wait_ge(xs_ready, b + 1)
                    wait(pe, qj_ready, b)
                    for n in which:
                        for m in range(DC):
                            for k in range(DC):
                                last = nc.tensor.matmul(bank[:, (n * DC + m) * T:(n * DC + m + 1) * T],
                                                        w[(QW, KW)[n]][:, k, m * P:(m + 1) * P], xs[:, k, :],
                                                        start=k == 0, stop=k == DC - 1)
                    if 1 in which:
                        last.then_inc(qk_done, 1)
                elif u == 1:
                    wait(pe, v_ready, b)
                    for k in range(DC):
                        last = nc.tensor.matmul(bank[0:T, 0:D], xs[:, k, :], w[VW][:, k, :],
                                                start=k == 0, stop=k == DC - 1)
                    last.then_inc(v_done, 1)
                else:
                    pe.wait_ge(tanh_ready, 2 * b + 1)
                    if isinstance(b, int) and b == 0:
                        pe.wait_ge(J_loaded, 16 * H)
                    for m in range(DC):
                        last = nc.tensor.matmul(bank[:, m * T:(m + 1) * T], Jd[:, m, :], qn[:, m, :], start=True, stop=True)
                    last.then_inc(j_done, 1)

            def scores(b, parity, g):
                if g == 0:
                    pe.wait_ge(k_ready, b + 1)
                    pe.wait_ge(tanh_ready, 2 * b + 2)
                    pe.wait_ge(qj_ready, b + 1)
                wait(pe, shifted, b * G + g - 1)
                c, h = g * GH // HP, g * GH % HP
                bank = ps[0:T, SCORES + g % 2, 0:GH * T]
                nc.tensor.matmul(bank, q[parity][:, c, :], km[parity][:, c, h:h + GH, :].rearrange("p a b -> p (a b)"),
                                 start=True, stop=False)
                nc.tensor.matmul(bank, qj[parity][:, c, :], knm[parity][:, c, h:h + GH, :].rearrange("p a b -> p (a b)"),
                                 start=False, stop=True).then_inc(s_done, 1)

            def turn(b, g):
                pe.wait_ge(exped, b * G + g + 1)
                wait(pe, pt_ready, b * G + g - 1)
                for j in range(GH):
                    last = nc.tensor.transpose(ps[0:T, TURNED + g % 2, j * T:(j + 1) * T], pr[:, g % NB, j, :], ident[0:T, 0:T])
                last.then_inc(t_done, 1)

            def values(b, parity, g):
                pe.wait_ge(pt_ready, b * G + g + 1)
                if g == 0:
                    wait(pe, o_read, b)
                    pe.wait_ge(v_ready, b + 1)
                for j in range(GH):
                    last = nc.tensor.matmul(ps[j * 32:j * 32 + 32, OUT, g * T:(g + 1) * T], vv[parity][:, g * GH + j, :],
                                            pt[:, g % NB, j, :], start=True, stop=True)
                last.then_inc(pv_done, 1)

            def tail(b, part):
                if part == 0:
                    pe.wait_ge(o_read, b + 1)
                    for g in range(4):
                        last = nc.tensor.transpose(ps[0:T, TAIL, g * P:(g + 1) * P], osb[:, g * T:(g + 1) * T], ident[:])
                    last.then_inc(t1_done, 1)
                elif part == 1:
                    pe.wait_ge(otok_ready, b + 1)
                    for k in range(DC):
                        last = nc.tensor.transpose(ps[:, TAIL, k * T:(k + 1) * T],
                                                   otok[:, k * 8:(k + 1) * 8, :].rearrange("p a b -> p (a b)"), ident[0:T, 0:T])
                    last.then_inc(t2_done, 1)
                elif part == 2:
                    pe.wait_ge(o_ready, b + 1)
                    for k in range(DC):
                        last = nc.tensor.matmul(ps[0:T, TAIL, 0:D], o[:, k, :], w[OW][:, k, :],
                                                start=k == 0, stop=k == DC - 1)
                    last.then_inc(y_done, 1)
                else:
                    pe.wait_ge(xn_ready, b + 1)
                    for k in range(DC):
                        last = nc.tensor.transpose(ps[:, TAIL, k * T:(k + 1) * T], xn[:, k * P:(k + 1) * P], ident[0:T, 0:T])
                    last.then_inc(xt_done, 1)

            for u in range(3):
                front(0, 0, u)

            def steps(b, parity, before, last):
                for g in range(G):
                    scores(b, parity, g)
                    if g >= 1:
                        turn(b, g - 1)
                    elif before:
                        turn(b - 1, G - 1)
                    if g == 0:
                        if before == 2:
                            tail(b - 2, 3)
                        if before:
                            values(b - 1, 1 - parity, G - 2)
                        if not last:
                            front(b + 1, 1 - parity, 0, (0,))
                        if before:
                            values(b - 1, 1 - parity, G - 1)
                        if not last:
                            front(b + 1, 1 - parity, 0, (1,))
                    else:
                        if not last and g < 3:
                            front(b + 1, 1 - parity, g)
                        if g >= 2:
                            values(b, parity, g - 2)
                        if before:
                            tail(b - 1, g - 1)

            over_batches(pe, steps)
            turn(B - 1, G - 1)
            tail(B - 2, 3)
            values(B - 1, 1, G - 2)
            values(B - 1, 1, G - 1)
            for part in range(4):
                tail(B - 1, part)

        @block.scalar
        def _(act):
            for n in range(4):
                act.wait_ge(w_turned, n + 1)
                nc.scalar.copy(w[n][:].rearrange("p a b -> p (a b)"), ps[:, n, :]).then_inc(w_ready, 1)
            act.wait_ge(const_ready, 2)

            def front(b, parity, u):
                bank = ps[:, FRONT + u % 2, :]
                if u == 0:
                    wait(act, v_done, b)
                    nc.scalar.copy(xs[:], xt[:, :, ds(b * T, T)]).then_inc(xs_ready, 1)
                elif u == 1:
                    act.wait_ge(qk_done, b + 1)
                    wait(act, k_ready, b)
                    wait(act, tanh_ready, 2 * b)
                    for m in range(DC):
                        nc.scalar.activation(q[parity][:, m, :], bank0[:, m * T:(m + 1) * T], ACT.Identity,
                                             bias=qk_bias[:, 0, m:m + 1])
                    for m in range(DC):
                        last = nc.scalar.activation(k32[:, m, :], bank0[:, (DC + m) * T:(DC + m + 1) * T], ACT.Identity,
                                                    bias=qk_bias[:, 1, m:m + 1])
                    last.then_inc(qk_ready, 1)
                    act.wait_ge(qk_ready, b + 1)
                    nc.scalar.activation(qn[:], q[parity][:], ACT.Tanh).then_inc(tanh_ready, 1)
                elif u in (2, 3):
                    wait(act, s_done, (b - 1) * G)
                    for h in range((u - 2) * HP // 2, (u - 1) * HP // 2):
                        last = nc.scalar.activation(knm[parity][:, :, h, :], k32[:], ACT.Tanh, scale=head_mask[:, h:h + 1])
                    if u == 3:
                        last.then_inc(tanh_ready, 1)
                else:
                    act.wait_ge(j_done, b + 1)
                    nc.scalar.activation(qj[parity][:].rearrange("p a b -> p (a b)"), bank0[:, 0:DC * T], ACT.Identity,
                                         scale=lam4[:]).then_inc(qj_ready, 1)

            bank0 = ps[:, FRONT, :]

            def exponent(b, g):
                act.wait_ge(shifted, b * G + g + 1)
                wait(act, t_done, b * G + g - NB + 1)
                wait(act, summed, b * G + g - NB + 1)
                nc.scalar.activation(pr[:, g % NB], sc[:, g % NB], ACT.Exp, scale=0.25).then_inc(exped, 1)

            def evacuate(b, g):
                act.wait_ge(t_done, b * G + g + 1)
                wait(act, pv_done, b * G + g - NB + 1)
                nc.scalar.copy(pt[:, g % NB].rearrange("p a b -> p (a b)"), ps[0:T, TURNED + g % 2, 0:GH * T])\
                    .then_inc(pt_ready, 1)

            def tail(b, part):
                if part == 0:
                    act.wait_ge(pv_done, b * G + G)
                    wait(act, t1_done, b)
                    nc.scalar.copy(osb[:], ps[:, OUT, 0:4 * T]).then_inc(o_read, 1)
                elif part == 1:
                    act.wait_ge(t2_done, b + 1)
                    nc.scalar.copy(o[:].rearrange("p a b -> p (a b)"), ps[:, TAIL, 0:DC * T]).then_inc(o_ready, 1)
                else:
                    act.wait_ge(xt_done, b + 1)
                    nc.scalar.copy(xt[:, :, ds(b * T, T)], ps[:, TAIL, 0:DC * T].rearrange("p (a b) -> p a b", a=DC))\
                        .then_inc(xt_ready, 1)

            def batch(b, parity, before, last):
                for g in range(G):
                    if not last and g == 0:
                        front(b + 1, 1 - parity, 0)
                    exponent(b, g)
                    if g >= 1:
                        evacuate(b, g - 1)
                    elif before:
                        evacuate(b - 1, G - 1)
                    if g == 0 and before == 2:
                        tail(b - 2, 2)
                    if g == 0 and before:
                        tail(b - 1, 0)
                    if not last:
                        for u in ((), (1, 2), (4, 3), ())[g]:
                            front(b + 1, 1 - parity, u)
                    if before and g == 2:
                        tail(b - 1, 1)

            for u in (0, 1, 2, 4, 3):
                front(0, 0, u)
            over_batches(act, batch)
            evacuate(B - 1, G - 1)
            tail(B - 2, 2)
            for part in range(3):
                tail(B - 1, part)

        @block.vector
        def _(dve):
            dve.wait_ge(const_loaded, 16 * LOADS)
            nc.vector.tensor_scalar_mul(lam4[:], lam4[:], 4.0).then_inc(const_ready, 1)
            dve.wait_ge(const_ready, 2)
            dve.wait_ge(v_zero, 1)

            def front(b, parity, u):
                if u == 0:
                    dve.wait_ge(v_done, b + 1)
                    nc.vector.tensor_add(vv[parity][:, :, 0:HD], ps[0:T, FRONT + 1, 0:D].rearrange("p (h d) -> p h d", d=HD),
                                         v_bias[:].rearrange("p (h d) -> p h d", d=HD)).then_inc(v_ready, 1)
                else:
                    dve.wait_ge(qk_ready, b + 1)
                    for h in range(HP):
                        last = nc.vector.tensor_scalar(km[parity][:, :, h, :], k32[:], head_mask[:, h:h + 1], None, ALU.mult)
                    last.then_inc(k_ready, 1)

            def shift(b, g, ch):
                dve.wait_ge(s_done, b * G + g + 1)
                bank = ps[0:T, SCORES + g % 2, 0:GH * T].rearrange("p (a b) -> p a b", a=GH)
                ch.link(nc.vector.reduce_max(mx[:, g % NB], bank, axis=AX.X))
                wait(dve, exped, b * G + g - NB + 1)
                nc.vector.tensor_tensor(sc[:, g % NB], bank, mx[:, g % NB].unsqueeze(2).broadcast_to([T, GH, T]),
                                        ALU.subtract).then_inc(shifted, 1)

            def total(b, parity, g):
                dve.wait_ge(exped, b * G + g + 1)
                nc.vector.reduce_sum(rs[parity][:, g * GH:(g + 1) * GH], pr[:, g % NB], axis=AX.X).then_inc(summed, 1)

            def tail(b, parity, part, ch):
                if part == 0:
                    dve.wait_ge(summed, b * G + G)
                    ch.link(nc.vector.reciprocal(ri[:], rs[parity][:]))
                    dve.wait_ge(t1_done, b + 1)
                    nc.vector.tensor_tensor(otok[:], ps[0:T, TAIL, :].rearrange("p (h e) -> p h e", e=32)[:, :, 0:HD],
                                            ri[:].unsqueeze(2).broadcast_to([T, H, HD]), ALU.mult).then_inc(otok_ready, 1)
                elif part == 1:
                    ch.link(nc.vector.tensor_add(y[:].unsqueeze(1), x[:, ds(b, 1), :], o_bias[:].unsqueeze(1)))
                    dve.wait_ge(y_done, b + 1)
                    ch.link(nc.vector.tensor_add(y[:], ps[0:T, TAIL, 0:D], y[:]))
                    ch.link(nc.vector.bn_stats(st[:], y[:]), dve_passed)
                    ch.link(nc.vector.bn_aggr(mv[:], st[:]))
                    nc.vector.tensor_scalar_add(var[:], mv[:, 1:2], EPS).then_inc(var_ready, 1)
                else:
                    dve.wait_ge(rstd_ready, b + 1)
                    wait(dve, x_stored, b)
                    nc.vector.tensor_scalar(xn[:], y[:], mv[:, 0:1], rstd[:], ALU.subtract, ALU.mult).then_inc(xn_ready, 1)

            def batch(b, parity, before, last):
                ch = Chain(dve, chain, b * CHAIN - 5 if before else 0)
                for g in range(G):
                    if g == 0 and before == 2:
                        tail(b - 2, parity, 2, ch)
                    shift(b, g, ch)
                    if g >= 1:
                        total(b, parity, g - 1)
                    elif before:
                        total(b - 1, 1 - parity, G - 1)
                    if before and g == 1:
                        tail(b - 1, 1 - parity, 0, ch)
                    if not last and g in (1, 2):
                        front(b + 1, 1 - parity, g - 1)
                    if before and g == 3:
                        tail(b - 1, 1 - parity, 1, ch)

            for u in range(2):
                front(0, 0, u)
            over_batches(dve, batch)
            total(B - 1, 1, G - 1)
            ch = Chain(dve, chain, B * CHAIN - 5)
            tail(B - 2, 0, 2, ch)
            for part in range(3):
                tail(B - 1, 1, part, ch)


def split_tokens(nc, act, dve, xt, xh, xl, high_ready, low_ready):
    for c in range(NC):
        cols = slice(c * CT, (c + 1) * CT)
        if act is not None:
            nc.scalar.copy(xh[:, :, cols], xt[:, :, cols]).then_inc(high_ready, 1)
        if dve is not None:
            dve.wait_ge(high_ready, c + 1)
            nc.vector.tensor_sub(xl[:, :, cols], xt[:, :, cols], xh[:, :, cols].bitcast(F32)).then_inc(low_ready, 1)


def top_two(nc, chain, ramp, values, best, second, sel1, sel2, work, groups, E):
    def wide(v):
        return v[:].unsqueeze(2).broadcast_to([T, groups, E])

    for n, (top, sel) in enumerate(((best, sel1), (second, sel2))):
        chain.link(nc.vector.reduce_max(top[:], values[:], axis=AX.X))
        yield
        chain.link(nc.vector.tensor_tensor(sel[:], values[:], wide(top), ALU.is_equal))
        yield
        chain.link(nc.vector.tensor_tensor(sel[:], sel[:], ramp[:].unsqueeze(1).broadcast_to([T, groups, E]), ALU.mult))
        yield
        chain.link(nc.vector.reduce_max(work[:], sel[:], axis=AX.X))
        yield
        chain.link(nc.vector.tensor_tensor(sel[:], sel[:], wide(work), ALU.is_equal))
        yield
        if n == 0:
            chain.link(nc.vector.scalar_tensor_tensor(out=values[:], in0=sel[:], scalar=-3e38, in1=values[:],
                                                      op0=ALU.mult, op1=ALU.add))
            yield


def stage_moe_routes(nc, xt, xh, xl, ident, gate_w, gate_b, b2, bs2, ws1, ws2, w1_raw, w2_raw, comb_t, acc, E):
    with Stage(nc, "routes") as s:
        gw = s.sb("gw", [P, DC, E])
        gb = s.sb("gb", [T, E])
        b2_all = s.sb("b2_all", [E + 1, D])
        ramp = s.sb("ramp", [T, E])
        logits = s.sb("logits", [T, B, E])
        best, second, work, share, rest = (s.sb(n, [T, B]) for n in ("best", "second", "work", "share", "rest"))
        sel1, sel2 = (s.sb(n, [T, B, E]) for n in ("sel1", "sel2"))
        comb = s.sb("comb", [T, B, E + 1])
        ps = s.banks("ps", 8)
        loaded, ramp_ready, logits_done, chain_sem = (s.sem(n) for n in ("loaded", "ramp_ready", "logits_done", "chain"))
        gap_ready, exped, comb_ready, turned, comb_t_ready, bias_done, acc_ready = (
            s.sem(n) for n in ("gap_ready", "exped", "comb_ready", "turned", "comb_t_ready", "bias_done", "acc_ready"))
        block = s.block()

        x_high, x_low, shared_loaded = s.sem("x_high"), s.sem("x_low"), s.sem("shared_loaded")

        @block.sync
        def _(sp):
            sp.dma_start(gw[:], gate_w.rearrange("(c p) e -> p c e", p=P)).then_inc(loaded, 16)
            sp.dma_start(gb[:], rows(gate_b, T)).then_inc(loaded, 16)
            sp.dma_start(b2_all[0:E, :], b2).then_inc(loaded, 16)
            sp.dma_start(b2_all[E:E + 1, :], bs2.rearrange("(a n) -> a n", a=1)).then_inc(loaded, 16)
            sp.dma_start(w1_raw[:], ws1.rearrange("(c p) n -> p c n", p=P)).then_inc(shared_loaded, 16)
            sp.dma_start(w2_raw[:], ws2.rearrange("(m p) n -> p m n", p=P)).then_inc(shared_loaded, 16)
            sp.wait_ge(shared_loaded, 32)

        @block.gpsimd
        def _(pool):
            pool.iota(ramp[:], pattern=[[-1, E]], base=E, channel_multiplier=0,
                      allow_small_or_imprecise_dtypes=True)
            pool.memset(comb[:], 1.0).then_inc(ramp_ready, 1)

        @block.tensor
        def _(pe):
            pe.wait_ge(loaded, 64)
            for b in range(B):
                for k in range(DC):
                    last = nc.tensor.matmul(ps[0:T, 0, b * E:(b + 1) * E], xt[:, k, b * T:(b + 1) * T], gw[:, k, :],
                                            start=k == 0, stop=k == DC - 1)
            last.then_inc(logits_done, 1)
            pe.wait_ge(comb_ready, 1)
            for b in range(B):
                last = nc.tensor.transpose(ps[0:E + 1, 1 + b // CB, b % CB * T:(b % CB + 1) * T], comb[:, b, :], ident[0:T, 0:T])
                if b % CB == CB - 1:
                    last.then_inc(turned, 1)
            for c in range(NC):
                pe.wait_ge(comb_t_ready, c + 1)
                for m in range(DC):
                    n = c * DC + m
                    if n >= 2:
                        pe.wait_ge(acc_ready, n - 1)
                    nc.tensor.matmul(ps[:, 5 + n % 2, 0:CT], b2_all[:, m * P:(m + 1) * P], comb_t[:, c * CT:(c + 1) * CT],
                                     start=True, stop=True).then_inc(bias_done, 1)

        @block.scalar
        def _(act):
            split_tokens(nc, act, None, xt, xh, xl, x_high, x_low)
            act.wait_ge(gap_ready, 1)
            nc.scalar.activation(share[:], work[:], ACT.Exp).then_inc(exped, 1)
            for c in range(NC):
                act.wait_ge(turned, c + 1)
                nc.scalar.copy(comb_t[:, c * CT:(c + 1) * CT], ps[0:E + 1, 1 + c, 0:CT]).then_inc(comb_t_ready, 1)

        @block.vector
        def _(dve):
            c = Chain(dve, chain_sem)
            split_tokens(nc, None, dve, xt, xh, xl, x_high, x_low)
            dve.wait_ge(ramp_ready, 1)
            dve.wait_ge(loaded, 64)
            dve.wait_ge(logits_done, 1)
            c.link(nc.vector.tensor_tensor(logits[:], ps[0:T, 0, 0:B * E].rearrange("p (b e) -> p b e", e=E),
                                           gb[:].unsqueeze(1).broadcast_to([T, B, E]), ALU.add))
            for _ in top_two(nc, c, ramp, logits, best, second, sel1, sel2, work, B, E):
                pass
            nc.vector.tensor_sub(work[:], second[:], best[:]).then_inc(gap_ready, 1)
            dve.wait_ge(exped, 1)
            c.link(nc.vector.tensor_scalar_add(rest[:], share[:], 1.0))
            c.link(nc.vector.reciprocal(rest[:], rest[:]))
            c.link(nc.vector.tensor_mul(share[:], share[:], rest[:]))
            c.link(nc.vector.tensor_tensor(sel1[:], sel1[:], rest[:].unsqueeze(2).broadcast_to([T, B, E]), ALU.mult))
            c.link(nc.vector.tensor_tensor(sel2[:], sel2[:], share[:].unsqueeze(2).broadcast_to([T, B, E]), ALU.mult))
            nc.vector.tensor_add(comb[:, :, 0:E], sel1[:], sel2[:]).then_inc(comb_ready, 1)
            for n in range(NC * DC):
                dve.wait_ge(bias_done, n + 1)
                cols = slice(n // DC * CT, (n // DC + 1) * CT)
                nc.vector.tensor_add(acc[:, n % DC, cols], ps[:, 5 + n % 2, 0:CT], xt[:, n % DC, cols]).then_inc(acc_ready, 1)


def stage_moe(nc, xh, xl, ident, w1, b1, w2, bs1, w1_raw, w2_raw, comb_t, acc, E, HID):
    HT = HID // P
    with Stage(nc, "moe") as s:
        w1s = [[s.sb(f"w1_{b}{i}", [P, DC, HID], F32R) for i in range(2)] for b in range(2)]
        w2s = [[s.sb(f"w2_{b}{i}", [P, HT, D], F32R) for i in range(2)] for b in range(2)]
        b1_rows = s.sb("b1_rows", [(E + 1) * HT, P])
        b1_all = s.sb("b1_all", [P, (E + 1) * HT])
        b1c = [s.sb(f"b1c{b}", [P, HT]) for b in range(2)]
        ones = s.sb("ones", [E + 1, P])
        cm = s.sb("cm", [E + 1, TOK])
        gate = s.sb("gate", [P, 2, CT])
        h32 = s.sb("h32", [P, 2, CT])
        hh, hl = (s.sb(n, [P, HT, CT], F32R) for n in ("hh", "hl"))
        part = s.sb("part", [P, DC, CT])
        ps = s.banks("ps", 8)
        UP, GATE, DOWN = 0, 2, 4
        b_loaded, ones_ready, b_turned, b_ready = (s.sem(n) for n in ("b_loaded", "ones_ready", "b_turned", "b_ready"))
        w_loaded, w_high, w_low, bc_ready, cm_ready = (s.sem(n) for n in ("w_loaded", "w_high", "w_low", "bc_ready", "cm_ready"))
        up_done, gelu_done, chain, h_ready, down_done = (
            s.sem(n) for n in ("up_done", "gelu_done", "chain", "h_ready", "down_done"))
        gate_done, gate_ready, added = (s.sem(n) for n in ("gate_done", "gate_ready", "added"))
        PIECES = 4
        ITEM_LINKS = HT + 1
        block = s.block()

        def pieces(parity):
            half = HT // 2
            return [(w1_raw[:, k, :], w1s[parity][0][:, k, :], w1s[parity][1][:, k, :]) for k in range(DC)] + \
                   [(w2_raw[:, n:n + half, :], w2s[parity][0][:, n:n + half, :], w2s[parity][1][:, n:n + half, :])
                    for n in (0, half)]

        def over_experts(engine, turn):
            turn(0, 0, True, False)
            with engine.Fori(0, (E - 2) // 2) as i:
                turn(i * 2 + 1, 1, False, False)
                turn(i * 2 + 2, 0, False, False)
            turn(E - 1, 1, False, False)
            turn(E, 0, False, True)

        @block.sync
        def _(sp):
            sp.dma_start(b1_rows[0:E * HT, :], b1.rearrange("e (m p) -> (e m) p", p=P)).then_inc(b_loaded, 16)
            sp.dma_start(b1_rows[E * HT:(E + 1) * HT, :], bs1.rearrange("(m p) -> m p", p=P)).then_inc(b_loaded, 16)
            with sp.Fori(0, E) as e:
                sp.wait_ge(w_low, e * PIECES + PIECES)
                sp.dma_start(w1_raw[:].unsqueeze(1), w1[ds(e, 1)].rearrange("a (c p) n -> p a c n", p=P)).then_inc(w_loaded, 16)
                sp.dma_start(w2_raw[:].unsqueeze(1), w2[ds(e, 1)].rearrange("a (m p) n -> p a m n", p=P)).then_inc(w_loaded, 16)

        @block.gpsimd
        def _(pool):
            pool.memset(ones[:], 1.0).then_inc(ones_ready, 1)

        @block.tensor
        def _(pe):
            pe.wait_ge(b_loaded, 32)
            nc.tensor.transpose(ps[:, GATE, 0:(E + 1) * HT], b1_rows[:], ident[0:(E + 1) * HT, 0:(E + 1) * HT]).then_inc(b_turned, 1)
            pe.wait_ge(b_ready, 1)
            pe.wait_ge(ones_ready, 1)

            def up(t, parity, c, j):
                wait(pe, gelu_done, (t * NC + c) * HT + j - 1)
                for k in range(DC):
                    last = split_product(nc, ps[:, UP + j % 2, 0:CT], [w[:, k, j * P:(j + 1) * P] for w in w1s[parity]],
                                         [a[:, k, c * CT:(c + 1) * CT] for a in (xh, xl)], k == 0, k == DC - 1)
                last.then_inc(up_done, 1)

            def down(t, parity, c, j):
                n = t * NC + c
                pe.wait_ge(h_ready, n * HT + j + 1)
                if j == 0:
                    wait(pe, added, n - 1)
                for m in range(DC):
                    last = split_product(nc, ps[:, DOWN + 2 * (c % 2) + m, 0:CT],
                                         [w[:, j, m * P:(m + 1) * P] for w in w2s[parity]], [hh[:, j, :], hl[:, j, :]],
                                         j == 0, j == HT - 1)
                last.then_inc(down_done, 1)

            def turn(t, parity, first, last):
                pe.wait_ge(w_low, t * PIECES + PIECES)
                for c in range(NC):
                    pe.wait_ge(cm_ready, t + 1)
                    wait(pe, gate_ready, t * NC + c)
                    nc.tensor.matmul(ps[:, GATE, 0:CT], ones[:], cm[:, c * CT:(c + 1) * CT], start=True, stop=True)\
                        .then_inc(gate_done, 1)
                    for j in range(HT):
                        up(t, parity, c, j)
                        if c > 0:
                            down(t, parity, c - 1, j)
                        elif not first:
                            down(t - 1, 1 - parity, NC - 1, j)

            over_experts(pe, turn)
            for j in range(HT):
                down(E, 0, NC - 1, j)

        def next_piece(c, j):
            return {(1, 1): 0, (1, 4): 1, (2, 1): 2, (2, 4): 3}.get((c, j))

        @block.scalar
        def _(act):
            for raw, high, low in pieces(0):
                nc.scalar.copy(high, raw).then_inc(w_high, 1)
            act.wait_ge(b_turned, 1)
            nc.scalar.copy(b1_all[:], ps[:, GATE, 0:(E + 1) * HT]).then_inc(b_ready, 1)
            act.wait_ge(b_ready, 1)

            def turn(t, parity, first, last):
                wait(act, gelu_done, t * NC * HT - NC * HT + 1)
                e = E if first else t - 1
                nc.scalar.copy(b1c[parity][:], b1_all[:, ds(e * HT, HT)]).then_inc(bc_ready, 1)
                act.wait_ge(bc_ready, t + 1)
                for c in range(NC):
                    for j in range(HT):
                        n = (t * NC + c) * HT + j
                        act.wait_ge(up_done, n + 1)
                        wait(act, h_ready, n - 1)
                        nc.scalar.activation(h32[:, j % 2, :], ps[:, UP + j % 2, 0:CT], ACT.Gelu,
                                             bias=b1c[parity][:, j:j + 1]).then_inc(gelu_done, 1)
                        if j == 3:
                            act.wait_ge(gate_done, t * NC + c + 1)
                            wait(act, added, t * NC + c - 1)
                            nc.scalar.copy(gate[:, c % 2, :], ps[:, GATE, 0:CT]).then_inc(gate_ready, 1)
                        piece = next_piece(c, j)
                        if not last and piece is not None:
                            if piece == 0:
                                act.wait_ge(w_loaded, t * 32 + 32)
                                wait(act, down_done, t * NC * HT)
                            raw, high, low = pieces(1 - parity)[piece]
                            nc.scalar.copy(high, raw).then_inc(w_high, 1)

            over_experts(act, turn)

        @block.vector
        def _(dve):
            nc.vector.tensor_scalar(cm[:], comb_t[:], ident[0:E + 1, E:E + 1], None, ALU.mult).then_inc(cm_ready, 1)
            for n, (raw, high, low) in enumerate(pieces(0)):
                dve.wait_ge(w_high, n + 1)
                nc.vector.tensor_sub(low, raw, high.bitcast(F32)).then_inc(w_low, 1)

            def add(t, c, ch):
                n = t * NC + c
                dve.wait_ge(down_done, n * HT + HT)
                dve.wait_ge(gate_ready, n + 1)
                wait(dve, added, n)
                ch.link(nc.vector.tensor_tensor(part[:], ps[:, DOWN + 2 * (c % 2):DOWN + 2 * (c % 2) + 2, 0:CT],
                                                gate[:, c % 2, :].unsqueeze(1).broadcast_to([P, DC, CT]), ALU.mult))
                cols = slice(c * CT, (c + 1) * CT)
                nc.vector.tensor_add(acc[:, :, cols], acc[:, :, cols], part[:]).then_inc(added, 1)

            def turn(t, parity, first, last):
                for c in range(NC):
                    n = t * NC + c
                    ch = Chain(dve, chain, n * ITEM_LINKS - (min(n, 2) if first else 2))
                    for j in range(HT):
                        dve.wait_ge(gelu_done, n * HT + j + 1)
                        wait(dve, down_done, n * HT + j + 1 - HT)
                        ch.link(nc.vector.tensor_copy(hh[:, j, :], h32[:, j % 2, :]))
                        nc.vector.tensor_sub(hl[:, j, :], h32[:, j % 2, :], hh[:, j, :].bitcast(F32)).then_inc(h_ready, 1)
                        piece = next_piece(c, j)
                        if not last and piece is not None:
                            raw, high, low = pieces(1 - parity)[piece]
                            dve.wait_ge(w_high, t * PIECES + PIECES + piece + 1)
                            nc.vector.tensor_sub(low, raw, high.bitcast(F32)).then_inc(w_low, 1)
                        if c == NC - 1 and j == HT - 1 and not last:
                            dve.wait_ge(gate_done, n + 1)
                            nc.vector.tensor_scalar(cm[:], comb_t[:], ident[0:E + 1, ds(t, 1)], None, ALU.mult)\
                                .then_inc(cm_ready, 1)
                        if j == 1 and c > 1:
                            add(t, c - 2, ch)
                        elif j == 1 and not first:
                            add(t - 1, NC - 2 + c, ch)

            over_experts(dve, turn)
            ch = Chain(dve, chain, (E + 1) * NC * ITEM_LINKS - 2)
            for c in (NC - 2, NC - 1):
                add(E, c, ch)


def stage_moe_norm(nc, x, xt, ident, acc):
    with Stage(nc, "moenorm") as s:
        half = s.sb("half", [T, B])
        st = s.sb("st", [T, B, 6])
        mv = s.sb("mv", [T, B, 2])
        var = s.sb("var", [T, B])
        rstd = s.sb("rstd", [T, B])
        ps = s.banks("ps", 8)
        turned, chain, half_ready, var_ready, rstd_ready, x_ready, xt_done, xt_ready = (
            s.sem(n) for n in ("turned", "chain", "half_ready", "var_ready", "rstd_ready", "x_ready", "xt_done", "xt_ready"))
        block = s.block()

        def token_major(b):
            return ps[0:T, b // 2, (b % 2) * D:(b % 2 + 1) * D]

        @block.gpsimd
        def _(pool):
            pool.memset(half[:], -0.5).then_inc(half_ready, 1)
            pool.wait_ge(half_ready, 1)
            for c in range(NC):
                pool.wait_ge(var_ready, c + 1)
                pool.tensor_tensor(rstd[:, c * CB:(c + 1) * CB], var[:, c * CB:(c + 1) * CB],
                                   half[:, c * CB:(c + 1) * CB], ALU.pow).then_inc(rstd_ready, 1)

        @block.tensor
        def _(pe):
            for b in range(B):
                for k in range(DC):
                    last = nc.tensor.transpose(token_major(b)[:, k * P:(k + 1) * P], acc[:, k, b * T:(b + 1) * T], ident[:])
                if b % 2:
                    last.then_inc(turned, 1)
            for c in range(NC):
                pe.wait_ge(x_ready, c + 1)
                for k in range(DC):
                    for j in range(CB):
                        last = nc.tensor.transpose(ps[:, 2 * c + k, j * T:(j + 1) * T],
                                                   x[:, c * CB + j, k * P:(k + 1) * P], ident[0:T, 0:T])
                    last.then_inc(xt_done, 1)

        @block.scalar
        def _(act):
            for c in range(NC):
                for k in range(DC):
                    act.wait_ge(xt_done, c * DC + k + 1)
                    nc.scalar.copy(xt[:, k, c * CT:(c + 1) * CT], ps[:, 2 * c + k, 0:CT]).then_inc(xt_ready, 1)

        @block.vector
        def _(dve):
            ch = Chain(dve, chain)

            def statistics(c):
                for j in range(CB):
                    b = c * CB + j
                    if b % 2 == 0:
                        dve.wait_ge(turned, b // 2 + 1)
                    last = nc.vector.bn_stats(st[:, b, :], token_major(b))
                ch.link(last)
                for b in range(c * CB, c * CB + CB):
                    last = nc.vector.bn_aggr(mv[:, b, :], st[:, b, :])
                ch.link(last)
                nc.vector.tensor_scalar_add(var[:, c * CB:(c + 1) * CB], mv[:, c * CB:(c + 1) * CB, 1], EPS)\
                    .then_inc(var_ready, 1)

            def scale(c):
                dve.wait_ge(rstd_ready, c + 1)
                for b in range(c * CB, c * CB + CB):
                    last = nc.vector.tensor_scalar(x[:, b, :], token_major(b), mv[:, b, 0:1], rstd[:, b:b + 1],
                                                   ALU.subtract, ALU.mult)
                last.then_inc(x_ready, 1)

            for c in range(NC):
                statistics(c)
                if c:
                    scale(c - 1)
            scale(NC - 1)


def stage_switch_logits(nc, xt, xh, xl, ident, sel_v_w, sel_o_w, ex):
    with Stage(nc, "switchlogits") as s:
        sel_rows = s.sb("sel_rows", [P, D])
        sel = s.sb("sel", [P, DC, P])
        ps = s.banks("ps", 5)
        loaded, sel_turned, sel_ready, logits_done, x_high, x_low = (
            s.sem(n) for n in ("loaded", "sel_turned", "sel_ready", "logits_done", "x_high", "x_low"))
        block = s.block()

        @block.sync
        def _(sp):
            sp.dma_start(sel_rows[0:P // 2, :], sel_v_w).then_inc(loaded, 16)
            sp.dma_start(sel_rows[P // 2:P, :], sel_o_w).then_inc(loaded, 16)

        @block.tensor
        def _(pe):
            pe.wait_ge(loaded, 32)
            for k in range(DC):
                last = nc.tensor.transpose(ps[:, 4, k * P:(k + 1) * P], sel_rows[:, k * P:(k + 1) * P], ident[:])
            last.then_inc(sel_turned, 1)
            pe.wait_ge(sel_ready, 1)
            for b in range(B):
                for k in range(DC):
                    last = nc.tensor.matmul(ps[0:T, b // CB, b % CB * P:(b % CB + 1) * P], xt[:, k, b * T:(b + 1) * T],
                                            sel[:, k, :], start=k == 0, stop=k == DC - 1)
                if b % CB == CB - 1:
                    last.then_inc(logits_done, 1)

        @block.scalar
        def _(act):
            act.wait_ge(sel_turned, 1)
            nc.scalar.copy(sel[:].rearrange("p a b -> p (a b)"), ps[:, 4, 0:D]).then_inc(sel_ready, 1)
            split_tokens(nc, act, None, xt, xh, xl, x_high, x_low)
            for c in range(NC):
                act.wait_ge(logits_done, c + 1)
                nc.scalar.activation(ex[:, c * CB:(c + 1) * CB, :].rearrange("p a b -> p (a b)"), ps[0:T, c, :], ACT.Exp,
                                     scale=-1.0)

        @block.vector
        def _(dve):
            split_tokens(nc, None, dve, xt, xh, xl, x_high, x_low)

LINKS = 22


def choose_gates(nc, chain, ramp, scale, ex, h, gate, best, second, work, sel1, sel2, chosen, E):
    groups = 2 * B
    chain.link(nc.vector.tensor_scalar_add(gate[:].rearrange("p (b o) e -> p b o e", o=2),
                                           ex[:].rearrange("p b (o g) -> p b o g", o=2)[:, :, :, ds(h * E, E)], 1.0))
    yield
    chain.link(nc.vector.reciprocal(gate[:], gate[:]))
    yield
    yield from top_two(nc, chain, ramp, gate, best, second, sel1, sel2, work, groups, E)
    chain.link(nc.vector.tensor_add(work[:], best[:], second[:]))
    yield
    chain.link(nc.vector.tensor_scalar_max(work[:], work[:], 1e-9))
    yield
    chain.link(nc.vector.reciprocal(work[:], work[:]))
    yield
    chain.link(nc.vector.tensor_scalar(work[:], work[:], scale[:], None, ALU.mult))
    yield
    for sel, value in ((sel1, best), (sel2, second)):
        chain.link(nc.vector.tensor_mul(value[:], value[:], work[:]))
        yield
        chain.link(nc.vector.tensor_tensor(sel[:], sel[:], value[:].unsqueeze(2).broadcast_to([T, groups, E]), ALU.mult))
        yield
    chain.link(nc.vector.tensor_add(chosen[:].rearrange("p b o e -> p (b o) e"), sel1[:], sel2[:]))
    yield


def stage_switch(nc, x, x_odd, xt, xh, xl, ident, q_w, k_w, v_w, o_w, route_scale, ex, HS, E, PW):
    SCALE = float(PW) ** -0.5
    EH = E // 2
    with Stage(nc, "switch") as s:
        scale = s.sb("scale", [T, 1])
        ramp = s.sb("ramp", [T, E])
        gate, sel1, sel2 = (s.sb(n, [T, 2 * B, E]) for n in ("gate", "sel1", "sel2"))
        best, second, work = (s.sb(n, [T, 2 * B]) for n in ("best", "second", "work"))
        chosen = [s.sb(f"chosen{i}", [T, B, 2, E]) for i in range(2)]
        raw = s.sb("raw", [P, E * D])
        v_raw = raw[:].rearrange("p (c e d) -> p c e d", c=DC, e=E)
        o_raw = raw[:].rearrange("p (e d) -> p e d", e=E)
        qk_raw = s.sb("qk_raw", [P, 2, D])
        vw = [[s.sb(f"vw{b}{i}", [P, DC, E * PW], F32R) for i in range(2)] for b in range(2)]
        ow = [[s.sb(f"ow{b}{i}", [P, E, D], F32R) for i in range(2)] for b in range(2)]
        qkw = [s.sb(f"qkw{i}", [P, DC, 2 * P], F32R) for i in range(2)]
        qk = xt
        cth, ctl = (s.sb(n, [P, TOK], F32R) for n in ("cth", "ctl"))
        v = s.sb("v", [T, B, PW])
        vt = s.sb("vt", [T, 2, E, PW])
        go = s.sb("go", [T, B, E])
        mx = s.sb("mx", [T, CB])
        sc = s.sb("sc", [T, CB, T])
        pr = s.sb("pr", [T, CB, T])
        pt = s.sb("pt", [T, CB, T])
        rs = s.sb("rs", [T, CB])
        ri = s.sb("ri", [T, CB])
        ps = s.banks("ps", 8)
        VALUES, OUTPUTS, QUERIES, SCORES, TURNED = 0, 2, 4, 6, 7
        names = ("v_loaded", "o_loaded", "qk_loaded", "scale_loaded", "ramp_ready", "odd_zero", "vw_high", "vw_low", "ow_high", "ow_low",
                 "qkw_turned", "qkw_high", "qkw_low", "chain", "qk_done", "qk_ready", "values_done", "v_act",
                 "v_ready", "s_done", "mx_ready", "shifted", "exped", "summed", "ri_ready", "go_ready", "t_done",
                 "pt_ready", "c_done", "ct_high", "ct_low", "out_done", "out_step")
        (v_loaded, o_loaded, qk_loaded, scale_loaded, ramp_ready, odd_zero, vw_high, vw_low, ow_high, ow_low, qkw_turned, qkw_high, qkw_low,
         chain, qk_done, qk_ready, values_done, v_act, v_ready, s_done, mx_ready, shifted, exped, summed,
         ri_ready, go_ready, t_done, pt_ready, c_done, ct_high, ct_low, out_done, out_step) = (s.sem(n) for n in names)
        block = s.block()

        def over_heads(engine, head, drain):
            head(0, 0, True, False)
            with engine.Fori(0, (HS - 2) // 2) as i:
                head(i * 2 + 1, 1, False, False)
                head(i * 2 + 2, 0, False, False)
            head(HS - 1, 1, False, True)
            drain()

        def chunk_of(h, b):
            c, step = b // CB - 1, b % CB
            return h * NC + c, c % NC, step

        def v_pieces(parity):
            return [(v_raw[:, k].rearrange("p e d -> p (e d)"), vw[parity][0][:, k, :], vw[parity][1][:, k, :])
                    for k in range(DC)]

        def o_pieces(parity):
            return [(o_raw[:, n:n + EH, :], ow[parity][0][:, n:n + EH, :], ow[parity][1][:, n:n + EH, :])
                    for n in (0, EH)]

        CHOOSE_AT = range(1, 12)
        V_AT, O_AT, QK_AT = {3: 0, 5: 1}, {7: 0, 9: 1}, 14

        @block.sync
        def _(sp):
            def load_v(h):
                for k in range(DC):
                    sp.dma_start(v_raw[:, k], v_w[ds(h * E, E), k * P:(k + 1) * P, :].rearrange("e p d -> p e d"))\
                        .then_inc(v_loaded, 16)

            def load_qk(h):
                sp.dma_start(qk_raw[:, 0, :], q_w[ds(h * PW, PW)]).then_inc(qk_loaded, 16)
                sp.dma_start(qk_raw[:, 1, :], k_w[ds(h * PW, PW)]).then_inc(qk_loaded, 16)

            def load_o(h):
                sp.dma_start(o_raw, o_w[ds(h * E, E)].rearrange("e p d -> p e d")).then_inc(o_loaded, 16)

            sp.dma_start(scale[:], rows(route_scale, T)).then_inc(scale_loaded, 16)
            load_v(0)
            load_qk(0)
            sp.wait_ge(vw_low, DC)
            load_v(1)
            sp.wait_ge(vw_low, 2 * DC)
            load_o(0)
            with sp.Fori(1, HS - 1) as h:
                sp.wait_ge(ow_low, h * 2)
                load_v(h + 1)
                sp.wait_ge(qkw_turned, h)
                load_qk(h)
                sp.wait_ge(vw_low, (h + 2) * DC)
                load_o(h)
            sp.wait_ge(qkw_turned, HS - 1)
            load_qk(HS - 1)
            sp.wait_ge(ow_low, (HS - 1) * 2)
            load_o(HS - 1)

        @block.gpsimd
        def _(pool):
            pool.iota(ramp[:], pattern=[[-1, E]], base=E, channel_multiplier=0,
                      allow_small_or_imprecise_dtypes=True).then_inc(ramp_ready, 1)
            pool.memset(x_odd[:], 0.0).then_inc(odd_zero, 1)

        @block.tensor
        def _(pe):
            def turn_weights(h):
                pe.wait_ge(qk_loaded, h * 32 + 32)
                wait(pe, qk_ready, h * NC * 2)
                for k in range(DC):
                    for n in range(2):
                        last = nc.tensor.transpose(ps[:, QUERIES, k * 2 * P + n * P:k * 2 * P + (n + 1) * P],
                                                   qk_raw[:, n, k * P:(k + 1) * P], ident[:])
                last.then_inc(qkw_turned, 1)

            def queries(h, c):
                pe.wait_ge(qkw_low, h + 1)
                for n in range(2):
                    wait(pe, qk_ready, (h * NC + c) * 2 + n - 1)
                    for k in range(DC):
                        last = split_product(nc, ps[:, QUERIES + n, 0:CT], [a[:, k, n * P:(n + 1) * P] for a in qkw],
                                             [a[:, k, c * CT:(c + 1) * CT] for a in (xh, xl)], k == 0, k == DC - 1)
                    last.then_inc(qk_done, 1)

            def values(h, parity, b, halves):
                slot = h * B + b
                if b == 0:
                    pe.wait_ge(vw_low, h * DC + DC)
                for n in halves:
                    wait(pe, v_act, slot * 2 + n - 1)
                    for k in range(DC):
                        last = split_product(nc, ps[0:T, VALUES + n, :], [a[:, k, b * T:(b + 1) * T] for a in (xh, xl)],
                                             [a[:, k, n * EH * PW:(n + 1) * EH * PW] for a in vw[parity]],
                                             k == 0, k == DC - 1)
                    last.then_inc(values_done, 1)

            def outputs(h, parity, b, pairs):
                slot = h * B + b
                if b % CB == 0:
                    pe.wait_ge(ct_low, h * NC + b // CB + 1)
                if b == 0:
                    pe.wait_ge(ow_low, h * 2 + 2)
                for n in pairs:
                    pe.wait_ge(out_step, slot * E + 2 * n + 2)
                    split_product(nc, ps[0:T, OUTPUTS + n % 2, :], [a[:, b * T:(b + 1) * T] for a in (cth, ctl)],
                                  [a[:, 2 * n:2 * n + 2, :].rearrange("p e d -> p (e d)") for a in ow[parity]])\
                        .then_inc(out_done, 1)

            def attend(chunk, c, step):
                if step == 0:
                    pe.wait_ge(qk_ready, chunk * 2 + 2)
                    wait(pe, shifted, chunk)
                    for j in range(CB):
                        cols = slice((c * CB + j) * T, (c * CB + j + 1) * T)
                        last = nc.tensor.matmul(ps[0:T, SCORES, j * T:(j + 1) * T], qk[:, 0, cols], qk[:, 1, cols],
                                                start=True, stop=True)
                    last.then_inc(s_done, 1)
                elif step == 1:
                    pe.wait_ge(exped, chunk + 1)
                    wait(pe, ct_low, chunk)
                    for j in range(CB):
                        last = nc.tensor.transpose(ps[0:T, TURNED, j * T:(j + 1) * T], pr[:, j, :], ident[0:T, 0:T])
                    last.then_inc(t_done, 1)
                elif step == 2:
                    pe.wait_ge(pt_ready, chunk + 1)
                    pe.wait_ge(v_ready, (chunk + 1) * CB)
                    for j in range(CB):
                        last = nc.tensor.matmul(ps[:, TURNED, j * T:(j + 1) * T], v[:, c * CB + j, :], pt[:, j, :],
                                                start=True, stop=True)
                    last.then_inc(c_done, 1)

            def head(h, parity, first, last):
                for b in range(B):
                    if not first or b >= CB:
                        attend(*chunk_of(h, b))
                    if b == QK_AT and not last:
                        turn_weights(h + 1)
                    if b % CB == 1:
                        queries(h, b // CB)
                    for half in range(2):
                        values(h, parity, b, (half,))
                        if not first:
                            outputs(h - 1, 1 - parity, b, range(half * EH // 2, (half + 1) * EH // 2))

            def drain():
                for b in range(B):
                    if b < CB:
                        attend(*chunk_of(HS, b))
                    outputs(HS - 1, 1, b, range(EH))

            turn_weights(0)
            over_heads(pe, head, drain)

        @block.scalar
        def _(act):
            act.wait_ge(v_loaded, DC * 16)
            for raw, high, low in v_pieces(0):
                nc.scalar.copy(high, raw).then_inc(vw_high, 1)

            def weights_turned(h):
                act.wait_ge(qkw_turned, h + 1)
                nc.scalar.copy(qkw[0][:].rearrange("p a b -> p (a b)"), ps[:, QUERIES, :]).then_inc(qkw_high, 1)

            def queries(h, c):
                for n in range(2):
                    act.wait_ge(qk_done, (h * NC + c) * 2 + n + 1)
                    nc.scalar.copy(qk[:, n, c * CT:(c + 1) * CT], ps[:, QUERIES + n, 0:CT]).then_inc(qk_ready, 1)

            def values(h, parity, b):
                slot = h * B + b
                if b == 0:
                    act.wait_ge(chain, (h + 1) * LINKS)
                wait(act, v_ready, slot - 1)
                for n in range(2):
                    act.wait_ge(values_done, slot * 2 + n + 1)
                    for e in range(EH):
                        last = nc.scalar.activation(vt[:, b % 2, n * EH + e, :],
                                                    ps[0:T, VALUES + n, e * PW:(e + 1) * PW], ACT.Copy,
                                                    scale=chosen[parity][:, b, 0, n * EH + e:n * EH + e + 1])
                    last.then_inc(v_act, 1)

            def attend(chunk, c, step):
                if step == 0:
                    act.wait_ge(shifted, chunk + 1)
                    wait(act, t_done, chunk)
                    wait(act, summed, chunk)
                    nc.scalar.activation(pr[:], sc[:], ACT.Exp, scale=SCALE).then_inc(exped, 1)
                elif step == 1:
                    act.wait_ge(t_done, chunk + 1)
                    wait(act, c_done, chunk)
                    nc.scalar.copy(pt[:].rearrange("p a b -> p (a b)"), ps[0:T, TURNED, 0:CT]).then_inc(pt_ready, 1)
                elif step == 2:
                    act.wait_ge(c_done, chunk + 1)
                    nc.scalar.copy(cth[:, c * CT:(c + 1) * CT], ps[:, TURNED, 0:CT]).then_inc(ct_high, 1)

            def head(h, parity, first, last):
                for b in range(B):
                    if not first or b >= CB:
                        attend(*chunk_of(h, b))
                    if b == QK_AT and not last:
                        weights_turned(h + 1)
                    if b % CB == 1:
                        queries(h, b // CB)
                    values(h, parity, b)
                    if b in V_AT and not last:
                        if V_AT[b] == 0:
                            act.wait_ge(v_loaded, (h + 2) * DC * 16)
                        raw, high, low = v_pieces(1 - parity)[V_AT[b]]
                        nc.scalar.copy(high, raw).then_inc(vw_high, 1)
                    if b in O_AT:
                        if O_AT[b] == 0:
                            act.wait_ge(o_loaded, h * 16 + 16)
                        raw, high, low = o_pieces(parity)[O_AT[b]]
                        nc.scalar.copy(high, raw).then_inc(ow_high, 1)

            def drain():
                for b in range(CB):
                    attend(*chunk_of(HS, b))

            weights_turned(0)
            over_heads(act, head, drain)

        @block.vector
        def _(dve):
            def choose(h, parity):
                return choose_gates(nc, Chain(dve, chain, h * LINKS), ramp, scale, ex, h, gate, best, second, work,
                                    sel1, sel2, chosen[parity], E)

            dve.wait_ge(scale_loaded, 16)
            dve.wait_ge(ramp_ready, 1)
            dve.wait_ge(odd_zero, 1)
            for _ in choose(0, 0):
                pass
            for n, (raw, high, low) in enumerate(v_pieces(0)):
                dve.wait_ge(vw_high, n + 1)
                nc.vector.tensor_sub(low, raw, high.bitcast(F32)).then_inc(vw_low, 1)

            def weights_turned(h):
                dve.wait_ge(qkw_high, h + 1)
                nc.vector.tensor_sub(qkw[1][:].rearrange("p a b -> p (a b)"), ps[:, QUERIES, :],
                                     qkw[0][:].bitcast(F32).rearrange("p a b -> p (a b)")).then_inc(qkw_low, 1)

            def values_sum(h, b):
                slot = h * B + b
                dve.wait_ge(v_act, slot * 2 + 2)
                nc.vector.reduce_sum(v[:, b, :], vt[:, b % 2].rearrange("p e d -> p d e"), axis=AX.X).then_inc(v_ready, 1)

            def outputs(h, b, pairs):
                slot = h * B + b
                for n in pairs:
                    dve.wait_ge(out_done, slot * EH + n + 1)
                    for i in range(2):
                        e, total = 2 * n + i, (x, x_odd)[i]
                        dve.wait_ge(out_step, slot * E + e + 3)
                        nc.vector.scalar_tensor_tensor(out=total[:, b, :],
                                                       in0=ps[0:T, OUTPUTS + n % 2, i * D:(i + 1) * D],
                                                       scalar=go[:, b, e:e + 1], in1=total[:, b, :], op0=ALU.mult,
                                                       op1=ALU.add).then_inc(out_step, 1)

            def attend(chunk, c, step, parity):
                if step == 0:
                    dve.wait_ge(s_done, chunk + 1)
                    wait(dve, shifted, chunk)
                    bank = ps[0:T, SCORES, 0:CT].rearrange("p (a b) -> p a b", a=CB)
                    nc.vector.reduce_max(mx[:], bank, axis=AX.X).then_inc(mx_ready, 1)
                    dve.wait_ge(mx_ready, chunk + 1)
                    wait(dve, exped, chunk)
                    nc.vector.tensor_tensor(sc[:], bank, mx[:].unsqueeze(2).broadcast_to([T, CB, T]), ALU.subtract)\
                        .then_inc(shifted, 1)
                elif step == 1:
                    dve.wait_ge(exped, chunk + 1)
                    nc.vector.reduce_sum(rs[:], pr[:], axis=AX.X).then_inc(summed, 1)
                    dve.wait_ge(summed, chunk + 1)
                    nc.vector.reciprocal(ri[:], rs[:]).then_inc(ri_ready, 1)
                    dve.wait_ge(ri_ready, chunk + 1)
                    nc.vector.tensor_tensor(go[:, c * CB:(c + 1) * CB, :], chosen[parity][:, c * CB:(c + 1) * CB, 1, :],
                                            ri[:].unsqueeze(2).broadcast_to([T, CB, E]), ALU.mult).then_inc(go_ready, 1)
                elif step == 2:
                    dve.wait_ge(ct_high, chunk + 1)
                    nc.vector.tensor_sub(ctl[:, c * CT:(c + 1) * CT], ps[:, TURNED, 0:CT],
                                         cth[:, c * CT:(c + 1) * CT].bitcast(F32)).then_inc(ct_low, 1)

            def head(h, parity, first, last):
                if not last:
                    steps = choose(h + 1, 1 - parity)
                for b in range(B):
                    if not first or b >= CB:
                        attend(*chunk_of(h, b), parity if b >= CB else 1 - parity)
                    if b == QK_AT and not last:
                        weights_turned(h + 1)
                    if not last and b in CHOOSE_AT:
                        if b == CHOOSE_AT[-1]:
                            wait(dve, v_act, h * B * 2)
                            wait(dve, go_ready, h * NC)
                        for _ in range(2):
                            next(steps, None)
                    if not first:
                        if b % CB == 0:
                            dve.wait_ge(go_ready, (h - 1) * NC + b // CB + 1)
                        outputs(h - 1, b, range(EH))
                    values_sum(h, b)
                    if b in V_AT and not last:
                        raw, high, low = v_pieces(1 - parity)[V_AT[b]]
                        dve.wait_ge(vw_high, h * DC + DC + V_AT[b] + 1)
                        nc.vector.tensor_sub(low, raw, high.bitcast(F32)).then_inc(vw_low, 1)
                    if b in O_AT:
                        raw, high, low = o_pieces(parity)[O_AT[b]]
                        dve.wait_ge(ow_high, h * 2 + O_AT[b] + 1)
                        nc.vector.tensor_sub(low, raw, high.bitcast(F32)).then_inc(ow_low, 1)

            def drain():
                for b in range(B):
                    if b < CB:
                        attend(*chunk_of(HS, b), 1)
                    if b % CB == 0:
                        dve.wait_ge(go_ready, (HS - 1) * NC + b // CB + 1)
                    outputs(HS - 1, b, range(EH))

            dve.sem_inc(out_step, 4)
            weights_turned(0)
            over_heads(dve, head, drain)


def stage_final_norm(nc, x, x_odd, out):
    with Stage(nc, "final") as s:
        half = s.sb("half", [T, B])
        st = s.sb("st", [T, B, 6])
        mv = s.sb("mv", [T, B, 2])
        var = s.sb("var", [T, B])
        rstd = s.sb("rstd", [T, B])
        half_ready, chain, var_ready, rstd_ready, y_ready, stored = (
            s.sem(n) for n in ("half_ready", "chain", "var_ready", "rstd_ready", "y_ready", "stored"))
        block = s.block()

        @block.gpsimd
        def _(pool):
            pool.memset(half[:], -0.5).then_inc(half_ready, 1)
            pool.wait_ge(half_ready, 1)
            for c in range(NC):
                part = slice(c * CB, (c + 1) * CB)
                pool.wait_ge(var_ready, c + 1)
                pool.tensor_tensor(rstd[:, part], var[:, part], half[:, part], ALU.pow).then_inc(rstd_ready, 1)

        @block.vector
        def _(dve):
            ch = Chain(dve, chain)
            for c in range(NC):
                part = slice(c * CB, (c + 1) * CB)
                ch.link(nc.vector.tensor_add(x[:, part, :], x[:, part, :], x_odd[:, part, :]))
                for b in range(c * CB, (c + 1) * CB):
                    last = nc.vector.bn_stats(st[:, b, :], x[:, b, :])
                ch.link(last)
                for b in range(c * CB, (c + 1) * CB):
                    last = nc.vector.bn_aggr(mv[:, b, :], st[:, b, :])
                ch.link(last)
                nc.vector.tensor_scalar_add(var[:, part], mv[:, part, 1], EPS).then_inc(var_ready, 1)
            for c in range(NC):
                dve.wait_ge(rstd_ready, c + 1)
                for b in range(c * CB, (c + 1) * CB):
                    last = nc.vector.tensor_scalar(x[:, b, :], x[:, b, :], mv[:, b, 0:1], rstd[:, b:b + 1],
                                                   ALU.subtract, ALU.mult)
                last.then_inc(y_ready, 1)

        @block.sync
        def _(sp):
            for c in range(NC):
                part = slice(c * CB, (c + 1) * CB)
                sp.wait_ge(y_ready, c + 1)
                sp.dma_start(out[part].rearrange("b t d -> t b d"), x[:, part, :]).then_inc(stored, 16)
            sp.wait_ge(stored, 16 * NC)


def stage_store(nc, x, out):
    with Stage(nc, "store") as s:
        stored = s.sem("stored")
        block = s.block()

        @block.sync
        def _(sp):
            sp.dma_start(out.rearrange("b t d -> t b d"), x[:]).then_inc(stored, 16)
            sp.wait_ge(stored, 16)


def build(nc, i, out, stages=(1, 2, 3, 4, 5, 6)):
    with Stage(nc, "all") as s:
        x = s.sb("x", [T, B, D])
        xt = s.sb("xt", [P, DC, TOK])
        ident = s.sb("ident", [P, P])
        if 1 in stages:
            with Stage(nc, "first") as f:
                w, wp = f.sb("w", [P, DC, 3 * D]), f.sb("wp", [P, DC, D])
                qk_bias, gamma = f.sb("qk_bias", [P, 4]), f.sb("gamma", [T, 1])
                v_bias, y_bias = f.sb("v_bias", [T, D]), f.sb("y_bias", [T, D])
                bqkv = i["L0_attn_bqkv"]
                pairs = [(gamma[:], rows(i["L0_attn_gamma"], T)),
                         (w[:], i["L0_attn_Wqkv"].rearrange("(c p) n -> p c n", p=P)),
                         (wp[:], i["L0_attn_Wproj"].rearrange("(c p) n -> p c n", p=P)),
                         (v_bias[:], rows(bqkv[2 * D:3 * D], T)), (y_bias[:], rows(i["L0_attn_bproj"], T))]
                pairs += [(qk_bias[:, m:m + 1], column(bqkv, m)) for m in range(2 * DC)]
                stage_load(nc, i["x"], x, xt, ident, pairs)
                stage_decay_attention(nc, x, xt, ident, w, wp, qk_bias, v_bias, y_bias, gamma)
        else:
            stage_load(nc, i["x"], x, xt, ident, [])
        if 2 in stages:
            stage_cross_attention(nc, "cross0", x, xt, ident, i["ctx_1024"],
                                  [i["L0_xattn_W_" + n] for n in "qkvo"], [True] * 4, None,
                                  i["mask_1x1xSxS2_if1"].rearrange("a b s t -> (a b s) t"), False)
        if 3 in stages:
            E, _, HID = i["L0_ffn_w1"].shape
            with Stage(nc, "experts") as f:
                comb_t = f.sb("comb_t", [E + 1, TOK])
                acc = f.sb("acc", [P, DC, TOK])
                xh, xl = (f.sb(n, [P, DC, TOK], F32R) for n in ("xh", "xl"))
                w1_raw, w2_raw = f.sb("w1_raw", [P, DC, HID]), f.sb("w2_raw", [P, HID // P, D])
                stage_moe_routes(nc, xt, xh, xl, ident, i["L0_ffn_gate_w"], i["L0_ffn_gate_b"], i["L0_ffn_b2"],
                                 i["L0_ffn_bs2"], i["L0_ffn_ws1"], i["L0_ffn_ws2"], w1_raw, w2_raw, comb_t, acc, E)
                stage_moe(nc, xh, xl, ident, i["L0_ffn_w1"], i["L0_ffn_b1"], i["L0_ffn_w2"], i["L0_ffn_bs1"],
                          w1_raw, w2_raw, comb_t, acc, E, HID)
                stage_moe_norm(nc, x, xt, ident, acc)
        if 4 in stages:
            stage_coupled_attention(nc, x, xt, ident, [i["L1_attn_W" + n] for n in "qkvo"],
                                    [i["L1_attn_b" + n] for n in "qkvo"], i["L1_attn_J_attn"],
                                    i["L1_attn_lambda_attn"])
        if 5 in stages:
            kv, kvb = i["L1_xattn_W_kv"], i["L1_xattn_b_kv"]
            stage_cross_attention(nc, "cross1", x, xt, ident, i["ctx_1024"],
                                  [i["L1_xattn_W_q"], kv[:, 0:D], kv[:, D:2 * D], i["L1_xattn_W_o"]], [False] * 4,
                                  [i["L1_xattn_b_q"], kvb[0:D], kvb[D:2 * D], i["L1_xattn_b_o"]],
                                  i["mask_BxS2_bf1"], True)
        if 6 in stages:
            HE, _, PW = i["L1_ffn_v_w"].shape
            HS = i["L1_ffn_q_w"].shape[0] // PW
            E = HE // HS
            with Stage(nc, "switchgates") as f:
                ex = f.sb("ex", [T, B, 2 * HE])
                xh, xl = (f.sb(n, [P, DC, TOK], F32R) for n in ("xh", "xl"))
                stage_switch_logits(nc, xt, xh, xl, ident, i["L1_ffn_sel_v_w"], i["L1_ffn_sel_o_w"], ex)
                x_odd = f.sb("x_odd", [T, B, D])
                stage_switch(nc, x, x_odd, xt, xh, xl, ident, i["L1_ffn_q_w"], i["L1_ffn_k_w"], i["L1_ffn_v_w"],
                             i["L1_ffn_o_w"], i["L1_ffn_route_scale"], ex, HS, E, PW)
                stage_final_norm(nc, x, x_odd, out)
        else:
            stage_store(nc, x, out)


_INS = [
    "x", "ctx_1024", "mask_1x1xSxS2_if1", "mask_BxS2_bf1", "L0_attn_Wqkv", "L0_attn_bqkv", "L0_attn_Wproj",
    "L0_attn_bproj", "L0_attn_gamma", "L0_xattn_W_q", "L0_xattn_W_k", "L0_xattn_W_v", "L0_xattn_W_o",
    "L0_ffn_gate_w", "L0_ffn_gate_b", "L0_ffn_w1", "L0_ffn_b1", "L0_ffn_w2", "L0_ffn_b2", "L0_ffn_ws1", "L0_ffn_bs1",
    "L0_ffn_ws2", "L0_ffn_bs2", "L1_attn_Wq", "L1_attn_bq", "L1_attn_Wk", "L1_attn_bk", "L1_attn_Wv", "L1_attn_bv",
    "L1_attn_Wo", "L1_attn_bo", "L1_attn_J_attn", "L1_attn_lambda_attn", "L1_xattn_W_q", "L1_xattn_b_q",
    "L1_xattn_W_kv", "L1_xattn_b_kv", "L1_xattn_W_o", "L1_xattn_b_o", "L1_ffn_q_w", "L1_ffn_k_w", "L1_ffn_v_w",
    "L1_ffn_o_w", "L1_ffn_sel_v_w", "L1_ffn_sel_o_w", "L1_ffn_route_scale",
]


def kernel(**inputs):
    import numpy as _np
    import concourse.bacc as _bacc
    from concourse import mybir as _mybir
    from concourse.bass_utils import run_bass_kernel_spmd as _run

    nc = _bacc.Bacc("TRN2", target_bir_lowering=False, num_devices=1)
    arrays, args = {}, {}
    for name in _INS:
        a = _np.ascontiguousarray(inputs[name])
        a = a.reshape(a.shape or (1,))
        arrays[f"in_{name}_dram"] = a
        args[name] = nc.dram_tensor(f"in_{name}_dram", a.shape, _mybir.dt.from_np(a.dtype), kind="ExternalInput").ap()
    out = nc.dram_tensor("out_0_dram", (B, T, D), F32, kind="ExternalOutput").ap()
    build(nc, args, out)
    r = _run(nc, [arrays], core_ids=[0])
    return r.results[0]["out_0_dram"]
```
